# Optimizing a Trainium2 kernel written in Bass

```python
import numpy as np
import jax
import jax.numpy as jnp

def _softmax(x, axis=-1):
    return jax.nn.softmax(x, axis=axis)

def _gelu(x):
    return jax.nn.gelu(x, approximate=True)

def _silu(x):
    return jax.nn.silu(x)

def _sigmoid(x):
    return jax.nn.sigmoid(x)

def _layernorm(x, axis=-1, eps=1e-05):
    m = jnp.mean(x, axis=axis, keepdims=True)
    v = jnp.var(x, axis=axis, keepdims=True)
    return (x - m) / jnp.sqrt(v + eps)

def _scatter_add(tgt, idx, src, axis=0):
    return tgt.at[idx].add(src)

def _segment_sum(src, seg, n):
    return jax.ops.segment_sum(src, seg, n)
kernel_name = 'mk_xattn_ffn_d1_seqx_r4_f2c84f'

def setup_inputs(seed: int=0):
    np.random.seed(seed)
    _w = jnp.asarray

    def _rec_inputs():
        import jax
        import jax.numpy as jnp
        _rk = jax.random.key(seed)
        x = 7.22e-05 + 1 * jax.random.normal(jax.random.fold_in(_rk, 1), (1, 2048, 256), jnp.float32)
        _lenS = 2048 - jax.random.randint(jax.random.fold_in(_rk, 7), (1,), 0, max(1, 2048 // 4) + 1, jnp.int32)
        _lenS2 = 1601 - jax.random.randint(jax.random.fold_in(_rk, 8), (1,), 0, max(1, 1601 // 4) + 1, jnp.int32)
        _ctx_768P = jax.random.normal(jax.random.fold_in(_rk, 11), (1, 16, 192), jnp.float32)
        _ctx_768c = jax.random.dirichlet(jax.random.fold_in(_rk, 511), 0.3 * jnp.ones((16,), jnp.float32), (1, 1601))
        _ctx_768t = jnp.einsum('bsk,bkd->bsd', _ctx_768c, _ctx_768P)
        _ctx_768t = _ctx_768t * jax.lax.rsqrt(jnp.mean(jnp.square(_ctx_768t)) + 1e-12) * 0.953939
        ctx_768 = 2.09791e-05 + 1.00001 * (_ctx_768t + 0.3 * jax.random.normal(jax.random.fold_in(_rk, 611), (1, 1601, 192), jnp.float32))
        return (x, ctx_768)
    x, ctx_768 = _rec_inputs()

    def _L0_xattn_setup():
        import jax, jax.numpy as jnp
        import numpy as np
        HEADS = 16
        DIM_HEAD = 64
        key = jax.random.key(seed)
        ks = jax.random.split(key, 7)
        B, Nq, Dq = (4, 512, 256)
        Nk, Dc = (256, 192)
        inner = HEADS * DIM_HEAD
        sq = 1.0 / np.sqrt(Dq)
        sc = 1.0 / np.sqrt(Dc)
        si = 1.0 / np.sqrt(inner)
        return {'x': jax.random.normal(ks[0], (B, Nq, Dq), dtype=jnp.float32), 'context': jax.random.normal(ks[1], (B, Nk, Dc), dtype=jnp.float32), 'Wq': jax.random.normal(ks[2], (Dq, inner), dtype=jnp.float32) * sq, 'Wk': jax.random.normal(ks[3], (Dc, inner), dtype=jnp.float32) * sc, 'Wv': jax.random.normal(ks[4], (Dc, inner), dtype=jnp.float32) * sc, 'Wo': jax.random.normal(ks[5], (inner, Dq), dtype=jnp.float32) * si, 'bo': jax.random.normal(ks[6], (Dq,), dtype=jnp.float32) * 0.01}
    _L0_xattn_all = _L0_xattn_setup()
    _L0_xattn_in = {k: v for k, v in _L0_xattn_all.items() if k in ('Wq', 'Wk', 'Wv', 'Wo', 'bo')}
    del _L0_xattn_all

    def _L0_ffn_setup():
        import jax, jax.numpy as jnp
        import numpy as np
        DIM = 256
        NUM_EXPERTS = 8
        HIDDEN = 1024
        CAP_FACTOR = 2.0
        B, S = (4, 512)
        key = jax.random.key(seed)
        ks = jax.random.split(key, 6)
        scale_r = 1.0 / np.sqrt(DIM)
        scale_1 = 1.0 / np.sqrt(DIM)
        scale_2 = 1.0 / np.sqrt(HIDDEN)
        return {'x': jax.random.normal(ks[0], (B, S, DIM), dtype=jnp.float32), 'router_w': jax.random.uniform(ks[1], (NUM_EXPERTS, DIM), jnp.float32, -scale_r, scale_r), 'w1': jax.random.uniform(ks[2], (NUM_EXPERTS, DIM, HIDDEN), jnp.float32, -scale_1, scale_1), 'b1': jax.random.uniform(ks[3], (NUM_EXPERTS, HIDDEN), jnp.float32, -scale_1, scale_1), 'w2': jax.random.uniform(ks[4], (NUM_EXPERTS, HIDDEN, DIM), jnp.float32, -scale_2, scale_2), 'b2': jax.random.uniform(ks[5], (NUM_EXPERTS, DIM), jnp.float32, -scale_2, scale_2)}
    _L0_ffn_all = _L0_ffn_setup()
    _L0_ffn_in = {k: v for k, v in _L0_ffn_all.items() if k in ('router_w', 'w1', 'b1', 'w2', 'b2')}
    del _L0_ffn_all
    return {'x': x, 'ctx_768': ctx_768, 'L0_xattn_Wq': _L0_xattn_in['Wq'], 'L0_xattn_Wk': _L0_xattn_in['Wk'], 'L0_xattn_Wv': _L0_xattn_in['Wv'], 'L0_xattn_Wo': _L0_xattn_in['Wo'], 'L0_xattn_bo': _L0_xattn_in['bo'], 'L0_ffn_router_w': _L0_ffn_in['router_w'], 'L0_ffn_w1': _L0_ffn_in['w1'], 'L0_ffn_b1': _L0_ffn_in['b1'], 'L0_ffn_w2': _L0_ffn_in['w2'], 'L0_ffn_b2': _L0_ffn_in['b2']}

def reference(x, ctx_768, L0_xattn_Wq, L0_xattn_Wk, L0_xattn_Wv, L0_xattn_Wo, L0_xattn_bo, L0_ffn_router_w, L0_ffn_w1, L0_ffn_b1, L0_ffn_w2, L0_ffn_b2):
    import jax
    import jax.numpy as jnp

    def _L0_xattn_ref(x, context, Wq, Wk, Wv, Wo, bo):
        import jax, jax.numpy as jnp
        import numpy as np
        HEADS = 16
        DIM_HEAD = 64
        B, Nq, _ = x.shape
        Nk = context.shape[1]
        h, dh = (HEADS, DIM_HEAD)
        q = (x @ Wq).reshape(B, Nq, h, dh)
        k = (context @ Wk).reshape(B, Nk, h, dh)
        v = (context @ Wv).reshape(B, Nk, h, dh)
        scale = 1.0 / jnp.sqrt(jnp.asarray(dh, dtype=x.dtype))
        scores = jnp.einsum('bqhd,bkhd->bhqk', q, k) * scale
        attn = jax.nn.softmax(scores, axis=-1)
        out = jnp.einsum('bhqk,bkhd->bqhd', attn, v).reshape(B, Nq, h * dh)
        return out @ Wo + bo

    def _L0_ffn_ref(x, router_w, w1, b1, w2, b2):
        import jax, jax.numpy as jnp
        import numpy as np
        DIM = 256
        NUM_EXPERTS = 8
        HIDDEN = 1024
        CAP_FACTOR = 2.0
        B, S = (4, 512)
        Bz, Sz, Dz = x.shape
        E = router_w.shape[0]
        capacity = max(1, int(Sz * CAP_FACTOR / E) + 1)
        scores = jax.nn.softmax(jnp.einsum('bsd,ed->bse', x, router_w), axis=-1)
        scores_t = jnp.swapaxes(scores, 1, 2)
        gate_vals, sel_idx = jax.lax.top_k(scores_t, capacity)
        b_idx = jnp.arange(Bz)[:, None, None]
        tokens = x[b_idx, sel_idx]
        h = jnp.einsum('becd,edh->bech', tokens, w1) + b1[None, :, None, :]
        h = jax.nn.gelu(h, approximate=False)
        y = jnp.einsum('bech,ehd->becd', h, w2) + b2[None, :, None, :]
        gated = y * gate_vals[..., None]
        out = jnp.zeros_like(x).at[b_idx, sel_idx].add(gated)
        return out
    x = x + _L0_xattn_ref(_layernorm(x, axis=-1), ctx_768, L0_xattn_Wq, L0_xattn_Wk, L0_xattn_Wv, L0_xattn_Wo, L0_xattn_bo)
    x = x + _L0_ffn_ref(_layernorm(x, axis=-1), L0_ffn_router_w, L0_ffn_w1, L0_ffn_b1, L0_ffn_w2, L0_ffn_b2)
    return x

_drawn_inputs = setup_inputs


def setup_inputs(seed=0):
    import zlib

    import numpy as np

    out = dict(_drawn_inputs(seed))
    spreads = {}
    factors = {'L0_xattn_bo': 6.099, 'L0_ffn_b1': 8.0, 'L0_ffn_b2': 8.0}
    for name, (base, spread) in spreads.items():
        noise = np.random.default_rng([zlib.crc32(name.encode()), seed]).standard_normal(out[name].shape)
        drawn = base * np.exp(spread * noise) if base else spread * noise
        out[name] = jnp.asarray(drawn.astype(out[name].dtype))
    for name, factor in factors.items():
        out[name] = (out[name] * factor).astype(out[name].dtype)
    return out
```

```python
from contextlib import ExitStack

import concourse.bass as bass
from concourse import mybir

ALU = mybir.AluOpType
ACT = mybir.ActivationFunctionType
AX = mybir.AxisListType
F32 = mybir.dt.float32
F32R = mybir.dt.float32r
BF16 = mybir.dt.bfloat16
I32 = mybir.dt.int32
U32 = mybir.dt.uint32

P = 128
EPS = 1e-5


def raw(ap):
    return ap.bitcast(F32)


class Shapes:

    def __init__(self, x, ctx, wq, router_w, w1):
        self.NT, self.D = x.shape[1], x.shape[2]
        self.NK, self.DC = ctx.shape[1], ctx.shape[2]
        self.DI = wq.shape[1]
        self.DH = 64
        self.H = self.DI // self.DH
        self.TT = self.NT // P
        self.KT = -(-self.NK // P)
        self.NKP = self.KT * P
        self.LAST = self.NK - (self.KT - 1) * P
        self.KD = self.D // P
        self.NP = self.H // 2
        self.QC = 512
        self.QB = self.NT // self.QC
        self.UQ = 2 * self.QC
        self.KC = self.NKP // 4
        self.MC = 402
        self.MS = [0, self.MC - 2, self.NK - 2 * self.MC + 2, self.NK - self.MC]
        assert self.MS[2] <= self.MS[1] + self.MC and self.DC == P + P // 2
        self.E, self.HID = router_w.shape[0], w1.shape[2]
        self.HT = self.HID // P
        self.CAP = int(self.NT * 2.0 / self.E) + 1


def refine_rstd(dve, var, rstd, tmp, done, count):
    dve.tensor_tensor(tmp, rstd, rstd, ALU.mult).then_inc(done, 1)
    dve.wait_ge(done, count + 1)
    dve.scalar_tensor_tensor(out=tmp, in0=var, scalar=EPS, in1=tmp, op0=ALU.add, op1=ALU.mult).then_inc(done, 1)
    dve.wait_ge(done, count + 2)
    dve.tensor_scalar(tmp, tmp, -0.5, 1.5, ALU.mult, ALU.add).then_inc(done, 1)
    dve.wait_ge(done, count + 3)
    dve.tensor_tensor(rstd, rstd, tmp, ALU.mult).then_inc(done, 1)
    dve.wait_ge(done, count + 4)


def phase_prologue(nc, S, A, G, sem):
    with ExitStack() as ctx:
        def sb(name, shape, dt=F32):
            return ctx.enter_context(nc.sbuf_tensor(name, shape, dt))

        TT, KT, KD, LAST = S.TT, S.KT, S.KD, S.LAST
        HP = P // 2
        x_in = sb("x_in", [P, TT, S.D])
        stats = sb("ln1_stats", [P, TT, 6])
        mv = sb("ln1_mv", [P, TT, 2])
        std = sb("ln1_std", [P, TT])
        rstd = sb("ln1_rstd", [P, TT])
        nt = sb("ln1_nt", [P, TT])
        eps = sb("ln1_eps", [P, 1])
        c_in = sb("c_in", [P, KT, 2 * P])
        w_in = [sb(f"w_in{n}", [P, 2, S.DI]) for n in range(3)]
        w_hi = [sb(f"w_hi{n}", [P, 2, S.DI], F32R) for n in range(3)]
        w_lo = [sb(f"w_lo{n}", [P, 2, S.DI], F32R) for n in range(3)]
        v_st = sb("v_st", [P, 2, S.DI])
        ps = [ctx.enter_context(nc.psum_tensor(f"pro_ps{i}", [P, 512], F32)) for i in range(8)]

        s_c, s_cz = sem("p_c_loaded"), sem("p_c_padded")
        s_x = [sem(f"p_x_loaded{i}") for i in range(4)]
        s_w = [sem(f"p_w_loaded{i}") for i in range(3)]
        s_eps, s_stats, s_mv, s_std, s_rstd, s_xn = (sem(f"p_{n}") for n in ("eps", "stats", "mv", "std", "rstd", "xn"))
        s_whi, s_wlo, s_wst = sem("p_whi"), sem("p_wlo"), sem("p_wstored")
        s_ps, s_hi, s_lo = sem("p_ps_ready"), sem("p_hi_done"), sem("p_lo_done")
        s_v = sem("p_v_ready")
        s_vev = [sem(f"p_v_copied{i}") for i in range(2)]
        s_vst = [sem(f"p_v_stored{i}") for i in range(2)]
        s_id, s_ones = sem("p_ident"), sem("p_ones")
        s_rows = sem("p_rows")
        ident = G.ident

        xt = [("x", range(4 * g, 4 * g + 4), k) for g in range(TT // 4) for k in range(KD)]
        ct = [("c", range(4 * g, min(4 * g + 4, KT)), k) for g in range(-(-KT // 4)) for k in range(2)]
        tjobs = ct + xt
        NTJ = len(tjobs)

        def targets(job):
            src, tiles, k = job
            a, b = tiles[0] * P, (tiles[-1] + 1) * P
            if src == "x":
                return G.xt_hi[:, k, a:b], G.xt_lo[:, k, a:b], 0, b - a
            if k == 0:
                return G.c1_hi[:, a:b], G.c1_lo[:, a:b], 0, b - a
            return G.c2[:, a:b], G.c2[HP:P, a:b], HP, b - a

        vjobs = [(kt, half) for kt in range(KT) for half in range(2)]

        with nc.Block() as block:

            @block.sync
            def _(sp):
                sp.dma_start(c_in[:, 0:KT - 1, 0:S.DC],
                             A["ctx"][0, 0:(KT - 1) * P, :].rearrange("(t p) d -> p t d", p=P)).then_inc(s_c, 16)
                sp.dma_start(c_in[:, 0:KT - 1, S.DC:2 * P],
                             A["ctx"][0, 0:(KT - 1) * P, P:S.DC].rearrange("(t p) d -> p t d", p=P)).then_inc(s_c, 16)
                sp.wait_ge(s_cz, 1)
                sp.dma_start(c_in[0:LAST, KT - 1, 0:S.DC], A["ctx"][0, (KT - 1) * P:S.NK, :]).then_inc(s_c, 16)
                sp.dma_start(c_in[0:LAST, KT - 1, S.DC:2 * P],
                             A["ctx"][0, (KT - 1) * P:S.NK, P:S.DC]).then_inc(s_c, 16)
                for n, w in enumerate(("wv", "wk")):
                    sp.dma_start(w_in[n][:, 0, :], A[w][0:P, :]).then_inc(s_w[n], 16)
                    sp.dma_start(w_in[n][0:HP, 1, :], A[w][P:S.DC, :]).then_inc(s_w[n], 16)
                    sp.dma_start(w_in[n][HP:P, 1, :], A[w][P:S.DC, :]).then_inc(s_w[n], 16)
                    if n == 0:
                        for g in range(4):
                            t = slice(g * TT // 4, (g + 1) * TT // 4)
                            sp.dma_start(x_in[:, t, :], A["x"][0].rearrange("(t p) d -> p t d", p=P)[:, t, :]).then_inc(s_x[g], 16)
                sp.dma_start(w_in[2][:], A["wq"].rearrange("(k p) n -> p k n", p=P)).then_inc(s_w[2], 16)
                for n, scr in ((1, G.wk_scr), (2, G.wq_scr)):
                    sp.wait_ge(s_whi, n + 1)
                    sp.wait_ge(s_wlo, n + 1)
                    for k in range(2):
                        for part, w in ((0, w_hi[n]), (1, w_lo[n])):
                            sp.dma_start(scr[:, :, part, k, :].rearrange("h p c -> p h c"),
                                         raw(w[:, k, :]).rearrange("p (h c) -> p h c", c=P)).then_inc(s_wst, 16)
                for kt in range(KT):
                    sp.wait_ge(s_vev[0], kt + 1)
                    sp.wait_ge(s_vev[1], kt + 1)
                    sp.dma_start(G.v_scr[:, :, kt, :].rearrange("h p d -> p h d"),
                                 v_st[:, kt % 2, :].rearrange("p (h d) -> p h d", d=S.DH)).then_inc(s_vst[kt % 2], 16)
                sp.wait_ge(s_wst, 128)
                sp.wait_ge(s_vst[0], 16 * ((KT + 1) // 2))
                sp.wait_ge(s_vst[1], 16 * (KT // 2))

            @block.gpsimd
            def _(pool):
                pool.memset(ident[:], 0.0).then_inc(s_id, 1)
                pool.wait_ge(s_id, 1)
                pool.affine_select(out=ident[:], in_=ident[:], compare_op=ALU.not_equal, fill=1.0, base=0,
                                   pattern=[[-1, P]], channel_multiplier=1).then_inc(s_id, 1)
                pool.memset(G.ones[:], 1.0).then_inc(s_ones, 1)
                pool.memset(G.pad_bias[:], 0.0).then_inc(s_ones, 1)
                pool.wait_ge(s_ones, 2)
                pool.affine_select(out=G.pad_bias[:], in_=G.pad_bias[:], compare_op=ALU.is_gt, fill=-10000.0,
                                   base=LAST, pattern=[[0, 1]], channel_multiplier=-1).then_inc(s_ones, 1)
                for n in range(3):
                    pool.wait_ge(s_w[n], 48 if n < 2 else 16)
                    pool.wait_ge(s_whi, n + 1)
                    pool.tensor_tensor(w_lo[n][:], w_in[n][:], raw(w_hi[n][:]), ALU.subtract).then_inc(s_wlo, 1)

            @block.vector
            def _(dve):
                dve.memset(c_in[HP:P, KT - 1, :], 0.0).then_inc(s_cz, 1)
                dve.memset(eps[:], EPS).then_inc(s_eps, 1)
                for b in range(2):
                    dve.memset(raw(G.k2[b][HP:P, :]), 0.0).then_inc(s_rows, 1)
                    dve.memset(raw(G.q2[b][HP:P, :]), 0.0).then_inc(s_rows, 1)
                dve.wait_ge(s_rows, 4)
                for b in range(2):
                    dve.memset(raw(G.k2[b][HP:HP + 1, 0:S.NK]), 1.0).then_inc(s_rows, 1)

                def weight_hi(n):
                    dve.wait_ge(s_w[n], 48 if n < 2 else 16)
                    dve.tensor_copy(w_hi[n][:], w_in[n][:]).then_inc(s_whi, 1)

                def lo(j):
                    hi_t, lo_t, r0, n = targets(tjobs[j])
                    dve.wait_ge(s_ps, j + 1)
                    dve.wait_ge(s_hi, j + 1)
                    src = hi_t if r0 == 0 else G.c2[HP:P, tjobs[j][1][0] * P:(tjobs[j][1][-1] + 1) * P]
                    dve.tensor_tensor(lo_t, ps[j % 4][r0:P, 0:n], raw(src), ALU.subtract).then_inc(s_lo, 1)

                weight_hi(0)
                for j in range(len(ct)):
                    lo(j)
                for t in range(TT):
                    if t % (TT // 4) == 0:
                        dve.wait_ge(s_x[t // (TT // 4)], 16)
                    dve.bn_stats(stats[:, t, :], x_in[:, t, :]).then_inc(s_stats, 1)
                for t in range(TT):
                    dve.wait_ge(s_stats, t + 1)
                    dve.bn_aggr(mv[:, t, :], stats[:, t, :]).then_inc(s_mv, 1)
                dve.wait_ge(s_std, 1)
                dve.reciprocal(rstd[:], std[:]).then_inc(s_rstd, 1)
                dve.wait_ge(s_rstd, 1)
                refine_rstd(dve, mv[:, :, 1], rstd[:], nt[:], s_rstd, 1)
                for t in range(TT):
                    dve.tensor_scalar(x_in[:, t, :], x_in[:, t, :], mv[:, t, 0:1], rstd[:, t:t + 1],
                                      ALU.subtract, ALU.mult).then_inc(s_xn, 1)
                for j in range(len(ct), NTJ):
                    lo(j)
                weight_hi(1)
                weight_hi(2)
                for kt in range(KT):
                    dve.wait_ge(s_v, 2 * kt + 2)
                    if kt >= 2:
                        dve.wait_ge(s_vst[kt % 2], 16 * (kt // 2))
                    dve.tensor_copy(v_st[:, kt % 2, 512:1024], ps[4 + (2 * kt + 1) % 4][:]).then_inc(s_vev[1], 1)

            @block.scalar
            def _(act):
                def hi(j):
                    hi_t, lo_t, r0, n = targets(tjobs[j])
                    act.wait_ge(s_ps, j + 1)
                    act.activation(hi_t, ps[j % 4][:, 0:n], ACT.Copy).then_inc(s_hi, 1)

                for j in range(len(ct)):
                    hi(j)
                act.wait_ge(s_mv, TT)
                act.wait_ge(s_eps, 1)
                act.activation(std[:], mv[:, :, 1], ACT.Sqrt, bias=eps[:, 0:1]).then_inc(s_std, 1)
                for j in range(len(ct), NTJ):
                    hi(j)
                for kt in range(KT):
                    act.wait_ge(s_v, 2 * kt + 1)
                    if kt >= 2:
                        act.wait_ge(s_vst[kt % 2], 16 * (kt // 2))
                    act.activation(v_st[:, kt % 2, 0:512], ps[4 + (2 * kt) % 4][:], ACT.Copy).then_inc(s_vev[0], 1)

            @block.tensor
            def _(pe):
                pe.wait_ge(s_id, 2)
                pe.wait_ge(s_c, 64)
                for j, (src, tiles, k) in enumerate(tjobs):
                    if j >= 4:
                        pe.wait_ge(s_lo, j - 3)
                    if src == "x":
                        pe.wait_ge(s_xn, tiles[-1] + 1)
                    buf = x_in if src == "x" else c_in
                    for i, t in enumerate(tiles):
                        last = pe.transpose(ps[j % 4][:, i * P:(i + 1) * P], buf[:, t, k * P:(k + 1) * P], ident[:])
                    last.then_inc(s_ps, 1)
                pe.wait_ge(s_lo, NTJ)
                pe.wait_ge(s_whi, 1)
                pe.wait_ge(s_wlo, 1)
                for j, (kt, half) in enumerate(vjobs):
                    if j >= 4:
                        pe.wait_ge(s_vev[half], kt - 1)
                    keys = slice(kt * P, (kt + 1) * P)
                    cols = slice(half * 512, half * 512 + 512)
                    v_hi, v_lo = w_hi[0], w_lo[0]
                    terms = [(G.c1_hi, v_hi, 0), (G.c1_lo, v_hi, 0), (G.c1_hi, v_lo, 0), (G.c2, v_hi, 1), (G.c2, v_lo, 1)]
                    for n, (c, w, k) in enumerate(terms):
                        last = pe.matmul(ps[4 + j % 4][:], c[:, keys], w[:, k, cols],
                                         start=(n == 0), stop=(n == len(terms) - 1))
                    last.then_inc(s_v, 1)


UNITS = 4
LAG = 2
RING = 4
DVE_TILES = (1, 3, 8, 12)
POOL_TILES = (0, 2, 4, 5, 6, 7, 9, 10, 11)
PROJ_SLOTS = (4, 6, 8, 10)
DEN_SLOT, MROW_SLOT = 2, 11
REC_SLOT, NORM_SLOT = 6, 11
MJOBS, MAHEAD = 16, 3
PROJ_JOBS = 2 * len(PROJ_SLOTS)


def wait_for(eng, s, count):
    if not (isinstance(count, int) and count <= 0):
        eng.wait_ge(s, count)


def tile_summed(t):
    tiles = DVE_TILES if t in DVE_TILES else POOL_TILES
    return t in DVE_TILES, max(tiles.index(t), 1)


def phase_attention(nc, S, A, G, sem):
    KT, DH, NP, UQ, QC, KC, MC = S.KT, S.DH, S.NP, S.UQ, S.QC, S.KC, S.MC
    HP = P // 2
    SLOTS = UNITS * KT
    SCALE = float(DH) ** -0.5
    NMU = UQ // P
    ND, NPL = len(DVE_TILES) - 1, len(POOL_TILES) - 1
    assert SLOTS % RING == 0
    with ExitStack() as ctx:
        def sb(name, shape, dt=F32):
            return ctx.enter_context(nc.sbuf_tensor(name, shape, dt))

        wq_s = sb("wq_s", [P, 4, P], F32R)
        wk_s = sb("wk_s", [P, 4, P], F32R)
        st_hi = sb("st_hi", [P, 2, QC], F32R)
        st_lo = sb("st_lo", [P, 2, QC], F32R)
        probs = sb("probs", [P, RING, UQ])
        acc_d = sb("acc_d", [P, UQ])
        acc_p = sb("acc_p", [P, UQ])
        den_sb = sb("den_sb", [P, QC])
        den_c = sb("den_c", [16, 2 * QC // 16])
        rec_c = sb("rec_c", [16, 2 * QC // 16])
        mx_half = sb("mx_half", [P, NMU, 2])
        mx = sb("mx", [P, NMU])
        m_row = sb("m_row", [NMU, P], F32R)
        o_sb = sb("o_sb", [P, QC])
        rec = sb("rec", [P, QC])
        o_n = sb("o_n", [P, 2, QC])
        vh = [sb(f"vh{b}", [P, KT, DH]) for b in range(2)]
        k1 = [sb(f"k1_{b}", [P, S.NKP], F32R) for b in range(2)]
        q1 = [sb(f"q1_{b}", [P, S.NT], F32R) for b in range(2)]
        k2, q2 = G.k2, G.q2
        ps_s = ctx.enter_context(nc.psum_tensor("ps_s", [P, 2, 2 * QC], F32))
        ps_m = ctx.enter_context(nc.psum_tensor("ps_m", [P, 2, QC], F32))
        ps_o = ctx.enter_context(nc.psum_tensor("ps_o", [P, QC], F32))
        ps_x = ctx.enter_context(nc.psum_tensor("ps_x", [P, QC], F32))

        w_loaded = sem("w_loaded")
        qk_loaded = [sem(f"qk_loaded{b}") for b in range(2)]
        v_loaded = [sem(f"v_loaded{b}") for b in range(2)]
        stage_stored = [sem(f"stage_stored{b}") for b in range(2)]
        mrow_placed = sem("mrow_placed")
        o_stored = [sem(f"o_stored{b}") for b in range(2)]
        den_moved, rec_stored, rec_placed = sem("den_moved"), sem("rec_stored"), sem("rec_placed")
        scores_ready, exp_done, pv_done = sem("scores_ready"), sem("exp_done"), sem("pv_done")
        rough_ready, rough_used, max_ready, maxt_ready, mrow_ready = (
            sem(n) for n in ("rough_ready", "rough_used", "max_ready", "maxt_ready", "mrow_ready"))
        proj_ready, stage_hi, stage_lo = sem("proj_ready"), sem("stage_hi"), sem("stage_lo")
        summed_dve, summed_pool = sem("summed_dve"), sem("summed_pool")
        den_ready, den_copied, rec_ready, o_copied, o_ready = sem("den_ready"), sem("den_copied"), sem("rec_ready"), sem("o_copied"), sem("o_ready")

        def rough_jobs(u, s, last):
            ahead = 1 if s < KT - MAHEAD else 2
            place = (s + MAHEAD) % KT
            if last and u + ahead >= UNITS:
                return []
            return [(j, ahead) for j in range(MJOBS) if j * KT // MJOBS == place]

        def x_wait(pe, p, u, s, last):
            unit = UNITS * p + u
            if s == DEN_SLOT:
                pe.wait_ge(mrow_ready, unit + 1)
            elif s in PROJ_SLOTS and s != PROJ_SLOTS[0]:
                pe.wait_ge(stage_lo, PROJ_JOBS * (p + 1) + u * len(PROJ_SLOTS) + PROJ_SLOTS.index(s))
            elif s == MROW_SLOT and u < 2 and not last:
                pe.wait_ge(stage_lo, PROJ_JOBS * (p + 1) + (u + 1) * len(PROJ_SLOTS))
            else:
                wait_for(pe, den_copied, unit)

        def pe_rough(pe, hd, half, j, count):
            wait_for(pe, rough_used, count)
            q0 = half * UQ + (j // 2) * P
            for i in range(2):
                k0 = S.MS[2 * (j % 2) + i]
                last = pe.matmul(ps_m[:, i, 0:MC], q1[hd][:, q0:q0 + P], k1[hd][:, k0:k0 + MC], start=True, stop=True)
            last.then_inc(rough_ready, 1)

        def dve_rough(dve, j, unit, count):
            if j == 0:
                wait_for(dve, max_ready, unit)
            dve.wait_ge(rough_ready, count + 1)
            dve.tensor_reduce(mx_half[:, j // 2, j % 2:j % 2 + 1], ps_m[:, :, 0:MC], AX.XY, ALU.max).then_inc(rough_used, 1)

        def dve_max(dve, unit):
            dve.wait_ge(rough_used, (unit + 1) * MJOBS)
            wait_for(dve, maxt_ready, unit)
            dve.tensor_reduce(mx[:], mx_half[:], AX.X, ALU.max).then_inc(max_ready, 1)

        def pe_maxt(pe, unit):
            pe.wait_ge(max_ready, unit + 1)
            pe.transpose(ps_x[0:NMU, 0:P], mx[:], G.ident[:]).then_inc(maxt_ready, 1)

        def act_mrow(act, unit):
            act.wait_ge(maxt_ready, unit + 1)
            wait_for(act, mrow_placed, 16 * unit)
            act.activation(m_row[:], ps_x[0:NMU, 0:P], ACT.Copy, scale=-1.0).then_inc(mrow_ready, 1)

        def sp_mrow(sp, unit, hd, half):
            sp.wait_ge(mrow_ready, unit + 1)
            sp.dma_start(raw(q2[hd][HP:HP + 1, half * UQ:(half + 1) * UQ]), raw(m_row[:])).then_inc(mrow_placed, 16)

        def block_of(n):
            return n % 2 == 0, n // 2

        def pe_proj(pe, n, pair):
            is_q, c = block_of(n)
            if n == 0:
                pe.wait_ge(w_loaded, 32 * (pair + 1))
            if is_q:
                cols = slice(c * QC, (c + 1) * QC)
                terms = [(wq_s[:, 2 * part + k, :], xt[:, k, cols])
                         for part, xt in ((0, G.xt_hi), (0, G.xt_lo), (1, G.xt_hi)) for k in range(S.KD)]
            else:
                cols = slice(c * KC, (c + 1) * KC)
                terms = [(wk_s[:, 0, :], G.c1_hi[:, cols]), (wk_s[:, 0, :], G.c1_lo[:, cols]),
                         (wk_s[:, 2, :], G.c1_hi[:, cols]), (wk_s[:, 1, :], G.c2[:, cols]), (wk_s[:, 3, :], G.c2[:, cols])]
            for i, (w, m) in enumerate(terms):
                last = pe.matmul(ps_x[:, 0:QC if is_q else KC], w, m, start=(i == 0), stop=(i == len(terms) - 1))
            last.then_inc(proj_ready, 1)

        def act_proj(act, n, count):
            w = QC if block_of(n)[0] else KC
            act.wait_ge(proj_ready, count + 1)
            wait_for(act, stage_stored[n % 2], 16 * (count - n % 2))
            act.activation(st_hi[:, n % 2, 0:w], ps_x[:, 0:w], ACT.Copy).then_inc(stage_hi, 1)

        def dve_proj(dve, n, count):
            w = QC if block_of(n)[0] else KC
            dve.wait_ge(stage_hi, count + 1)
            dve.tensor_tensor(st_lo[:, n % 2, 0:w], ps_x[:, 0:w], raw(st_hi[:, n % 2, 0:w]), ALU.subtract).then_inc(stage_lo, 1)

        def sp_proj(sp, n, pair, count):
            is_q, c = block_of(n)
            sp.wait_ge(stage_lo, count + 1)
            scr, w = (G.q_scr, QC) if is_q else (G.k_scr, KC)
            for part, st in ((0, st_hi), (1, st_lo)):
                sp.dma_start(scr[pair, part, :, c * w:(c + 1) * w], raw(st[:, n % 2, 0:w])).then_inc(stage_stored[n % 2], 16)

        def sp_load_w(sp, pair):
            sp.dma_start(raw(wq_s[:]), G.wq_scr[pair].rearrange("p a k c -> p (a k) c")).then_inc(w_loaded, 16)
            sp.dma_start(raw(wk_s[:]), G.wk_scr[pair].rearrange("p a k c -> p (a k) c")).then_inc(w_loaded, 16)

        def sp_load_head(sp, pair, hd):
            if hd == 0:
                for b in range(2):
                    sp.wait_ge(stage_stored[b], 16 * PROJ_JOBS * (pair + 1))
            rows = slice(hd * HP, (hd + 1) * HP)
            for dst, scr, part in ((q1[hd][0:HP, :], G.q_scr, 0), (q1[hd][HP:P, :], G.q_scr, 0), (q2[hd][0:HP, :], G.q_scr, 1),
                                   (k1[hd][0:HP, :], G.k_scr, 0), (k1[hd][HP:P, :], G.k_scr, 1), (k2[hd][0:HP, :], G.k_scr, 0)):
                sp.dma_start(raw(dst), scr[pair, part, rows, :]).then_inc(qk_loaded[hd], 16)
            sp.dma_start(vh[hd][:], G.v_scr[2 * pair + hd].rearrange("p t d -> p t d")).then_inc(v_loaded[hd], 16)

        def pe_pv(pe, g, slot, unit, pair):
            hd, s = g // (2 * KT), g % KT
            pe.wait_ge(exp_done, slot + 1)
            if s == 0:
                if g % (2 * KT) == 0:
                    pe.wait_ge(v_loaded[hd], 16 * (pair + 1))
                wait_for(pe, o_copied, unit)
            for b in range(2):
                last = pe.matmul(ps_o[b * HP:b * HP + DH, :], vh[hd][:, s, :], probs[:, g % RING, b * QC:(b + 1) * QC],
                                 start=(s == 0), stop=(s == KT - 1))
            last.then_inc(pv_done, 1)

        def pe_den(pe, unit):
            pe.wait_ge(summed_dve, (unit + 1) * ND)
            pe.wait_ge(summed_pool, (unit + 1) * NPL)
            for i, acc in enumerate((acc_d, acc_p)):
                for b in range(2):
                    last = pe.matmul(ps_x[b * HP:(b + 1) * HP, :], G.ones[:, 0:HP], acc[:, b * QC:(b + 1) * QC],
                                     start=(i == 0), stop=(i == 1))
            last.then_inc(den_ready, 1)

        def act_o(act, unit):
            act.wait_ge(pv_done, (unit + 1) * KT)
            wait_for(act, o_ready, unit)
            act.activation(o_sb[:], ps_o[:], ACT.Copy).then_inc(o_copied, 1)

        def act_den(act, unit):
            act.wait_ge(den_ready, unit + 1)
            wait_for(act, den_moved, 32 * unit)
            act.activation(den_sb[:], ps_x[:], ACT.Copy).then_inc(den_copied, 1)

        def sp_den(sp, unit):
            sp.wait_ge(den_copied, unit + 1)
            for b in range(2):
                sp.dma_start(den_c[8 * b:8 * b + 8, :], den_sb[b * HP:b * HP + 1, :]).then_inc(den_moved, 16)

        def dve_rec(dve, unit):
            dve.wait_ge(den_moved, 32 * (unit + 1))
            dve.reciprocal(rec_c[:], den_c[:]).then_inc(rec_ready, 1)

        def sp_rec(sp, unit):
            sp.wait_ge(rec_ready, unit + 1)
            sp.dma_start(G.rec_scr.rearrange("b (r c) -> (b r) c", r=8), rec_c[:]).then_inc(rec_stored, 16)
            sp.wait_ge(rec_stored, 16 * (unit + 1))
            for b in range(2):
                sp.dma_start(rec[b * HP:(b + 1) * HP, :], G.rec_scr[b:b + 1, :].to_broadcast([HP, QC])).then_inc(rec_placed, 16)

        def dve_norm(dve, unit, u):
            dve.wait_ge(rec_placed, 32 * (unit + 1))
            dve.wait_ge(o_copied, unit + 1)
            wait_for(dve, o_stored[u % 2], 16 * (unit - u % 2))
            dve.tensor_tensor(o_n[:, u % 2, :], o_sb[:], rec[:], ALU.mult).then_inc(o_ready, 1)

        def sp_store_o(sp, unit, pair, u):
            hd, q0 = u // 2, (u % 2) * UQ
            sp.wait_ge(o_ready, unit + 1)
            for b in range(2):
                sp.dma_start(G.o_scr[pair, hd * HP:(hd + 1) * HP, q0 + b * QC:q0 + (b + 1) * QC],
                             o_n[b * HP:(b + 1) * HP, u % 2, :]).then_inc(o_stored[u % 2], 16)

        def add_tile(eng, tiles, acc, done, k, u, unit, slot):
            t = tiles[k + 1]
            eng.wait_ge(exp_done, slot + t + 1)
            if k == 0:
                wait_for(eng, den_ready, unit)
                other = probs[:, (u * KT + tiles[0]) % RING, :]
            else:
                eng.wait_ge(done, unit * (len(tiles) - 1) + k)
                other = acc[:]
            eng.tensor_tensor(acc[:], other, probs[:, (u * KT + t) % RING, :], ALU.add).then_inc(done, 1)

        def pe_pair(pe, p, first=False, last=False):
            for g in range(SLOTS):
                u, s = divmod(g, KT)
                hd, half = divmod(u, 2)
                unit, slot = p * UNITS + u, p * SLOTS + g
                jobs = rough_jobs(u, s, last)

                def rough(jobs):
                    for j, ahead in jobs:
                        nu = (u + ahead) % UNITS
                        if j == 0 and nu % 2 == 0:
                            pe.wait_ge(qk_loaded[nu // 2], 96 * (p + 1 + (u + ahead) // UNITS))
                        pe_rough(pe, *divmod(nu, 2), j, (unit + ahead) * MJOBS + j)

                rough(jobs[:1])
                if s == 0:
                    pe.wait_ge(mrow_placed, 16 * (unit + 1))
                if not (first and g < 2):
                    pe.wait_ge(exp_done, slot - 1)
                keys = slice(s * P, (s + 1) * P)
                for b in range(2):
                    qs = slice(half * UQ + b * QC, half * UQ + (b + 1) * QC)
                    out = ps_s[:, g % 2, b * QC:(b + 1) * QC]
                    pe.matmul(out, k1[hd][:, keys], q1[hd][:, qs], start=True, stop=False)
                    mm = pe.matmul(out, k2[hd][:, keys], q2[hd][:, qs], start=False, stop=True)
                mm.then_inc(scores_ready, 1)
                if not (first and g < LAG):
                    pe_pv(pe, (g - LAG) % SLOTS, slot - LAG, p * UNITS + (g - LAG) // KT, p if g >= LAG else p - 1)
                rough(jobs[1:])
                if s == DEN_SLOT and not (first and u == 0):
                    x_wait(pe, p, u, s, last)
                    pe_den(pe, unit - 1)
                if s in PROJ_SLOTS and u < 2 and not last:
                    x_wait(pe, p, u, s, last)
                    pe_proj(pe, u * len(PROJ_SLOTS) + PROJ_SLOTS.index(s), p + 1)
                if s == MROW_SLOT and not (last and u == UNITS - 1):
                    x_wait(pe, p, u, s, last)
                    pe_maxt(pe, unit + 1)

        def act_pair(act, p, first=False, last=False):
            for g in range(SLOTS):
                u, s = divmod(g, KT)
                unit, slot = p * UNITS + u, p * SLOTS + g
                if not (first and g < RING):
                    act.wait_ge(pv_done, slot - RING + 1)
                    by_dve, n = tile_summed((g - RING) % KT)
                    then = p * UNITS + (g - RING) // KT
                    if by_dve:
                        act.wait_ge(summed_dve, then * ND + n)
                    else:
                        act.wait_ge(summed_pool, then * NPL + n)
                act.wait_ge(scores_ready, slot + 1)
                act.activation(probs[:, g % RING, :], ps_s[:, g % 2, :], ACT.Exp,
                               bias=G.pad_bias[:, 0:1] if s == KT - 1 else 0.0, scale=SCALE).then_inc(exp_done, 1)
                if s == LAG - 1 and not (first and u == 0):
                    act_o(act, unit - 1)
                if s == DEN_SLOT and not (first and u == 0):
                    act_den(act, unit - 1)
                if s in PROJ_SLOTS and u < 2 and not last:
                    n = u * len(PROJ_SLOTS) + PROJ_SLOTS.index(s)
                    act_proj(act, n, PROJ_JOBS * (p + 1) + n)
                if s == MROW_SLOT and not (last and u == UNITS - 1):
                    act_mrow(act, unit + 1)

        def dve_pair(dve, p, first=False, last=False):
            for g in range(SLOTS):
                u, s = divmod(g, KT)
                unit, slot = p * UNITS + u, p * SLOTS + g
                jobs = rough_jobs(u, s, last)
                if s == KT - MAHEAD and not (last and u == UNITS - 1):
                    dve_max(dve, unit + 1)
                for j, ahead in jobs[:1]:
                    dve_rough(dve, j, unit + ahead, (unit + ahead) * MJOBS + j)
                if s == 0 and not (first and u == 0):
                    add_tile(dve, DVE_TILES, acc_d, summed_dve, ND - 1, (u - 1) % UNITS, unit - 1, slot - KT)
                if s - 1 in DVE_TILES[1:]:
                    add_tile(dve, DVE_TILES, acc_d, summed_dve, DVE_TILES.index(s - 1) - 1, u, unit, slot - s)
                if s - 1 in PROJ_SLOTS and u < 2 and not last:
                    n = u * len(PROJ_SLOTS) + PROJ_SLOTS.index(s - 1)
                    dve_proj(dve, n, PROJ_JOBS * (p + 1) + n)
                for j, ahead in jobs[1:]:
                    dve_rough(dve, j, unit + ahead, (unit + ahead) * MJOBS + j)
                if s == REC_SLOT and not (first and u == 0):
                    dve_rec(dve, unit - 1)
                if s == NORM_SLOT and not (first and u == 0):
                    dve_norm(dve, unit - 1, (u - 1) % UNITS)

        def pool_pair(pool, p):
            for u in range(UNITS):
                for k in range(NPL):
                    add_tile(pool, POOL_TILES, acc_p, summed_pool, k, u, p * UNITS + u, p * SLOTS + u * KT)

        def sp_pair(sp, p, first=False, last=False):
            if not first:
                sp.wait_ge(scores_ready, p * SLOTS)
                sp.wait_ge(pv_done, p * SLOTS)
                sp_load_head(sp, p, 1)
            if not last:
                sp.wait_ge(proj_ready, PROJ_JOBS * (p + 1))
                sp_load_w(sp, p + 1)
            for u in range(UNITS):
                unit = p * UNITS + u
                if u == 2 and not last:
                    sp.wait_ge(scores_ready, p * SLOTS + 2 * KT)
                    sp.wait_ge(pv_done, p * SLOTS + 2 * KT)
                    sp_load_head(sp, p + 1, 0)
                blocks = range(u * len(PROJ_SLOTS), (u + 1) * len(PROJ_SLOTS)) if u < 2 and not last else []
                if not (first and u == 0):
                    sp_den(sp, unit - 1)
                for n in blocks[:1]:
                    sp_proj(sp, n, p + 1, PROJ_JOBS * (p + 1) + n)
                if not (first and u == 0):
                    sp_rec(sp, unit - 1)
                for n in blocks[1:]:
                    sp_proj(sp, n, p + 1, PROJ_JOBS * (p + 1) + n)
                if not (last and u == UNITS - 1):
                    sp_mrow(sp, unit + 1, *divmod((u + 1) % UNITS, 2))
                if not (first and u == 0):
                    sp_store_o(sp, unit - 1, p if u else p - 1, (u - 1) % UNITS)

        with nc.Block() as block:

            @block.sync
            def _(sp):
                sp_load_w(sp, 0)
                for n in range(PROJ_JOBS):
                    sp_proj(sp, n, 0, n)
                sp_load_head(sp, 0, 0)
                sp_load_head(sp, 0, 1)
                sp_mrow(sp, 0, 0, 0)
                sp_pair(sp, 0, first=True)
                with sp.Fori(1, NP - 1) as p:
                    sp_pair(sp, p)
                sp_pair(sp, NP - 1, last=True)
                sp_den(sp, NP * UNITS - 1)
                sp_rec(sp, NP * UNITS - 1)
                sp_store_o(sp, NP * UNITS - 1, NP - 1, UNITS - 1)
                for b in range(2):
                    sp.wait_ge(o_stored[b], 16 * NP * UNITS)

            @block.tensor
            def _(pe):
                for n in range(PROJ_JOBS):
                    if n:
                        pe.wait_ge(stage_lo, n)
                    pe_proj(pe, n, 0)
                pe.wait_ge(qk_loaded[0], 96)
                for j in range(MJOBS):
                    pe_rough(pe, 0, 0, j, j)
                pe.wait_ge(stage_lo, PROJ_JOBS)
                pe_maxt(pe, 0)
                for j, ahead in [(j, 1) for s in range(MAHEAD) for j in range(MJOBS) if j * KT // MJOBS == s]:
                    pe_rough(pe, 0, 1, j, MJOBS + j)
                pe_pair(pe, 0, first=True)
                with pe.Fori(1, NP - 1) as p:
                    pe_pair(pe, p)
                pe_pair(pe, NP - 1, last=True)
                for g in range(SLOTS - LAG, SLOTS):
                    pe_pv(pe, g, (NP - 1) * SLOTS + g, NP * UNITS - 1, NP - 1)
                pe.wait_ge(den_copied, NP * UNITS - 1)
                pe_den(pe, NP * UNITS - 1)

            @block.scalar
            def _(act):
                for n in range(PROJ_JOBS):
                    act_proj(act, n, n)
                act_mrow(act, 0)
                act_pair(act, 0, first=True)
                with act.Fori(1, NP - 1) as p:
                    act_pair(act, p)
                act_pair(act, NP - 1, last=True)
                act_o(act, NP * UNITS - 1)
                act_den(act, NP * UNITS - 1)

            @block.vector
            def _(dve):
                for n in range(PROJ_JOBS):
                    dve_proj(dve, n, n)
                for j in range(MJOBS):
                    dve_rough(dve, j, 0, j)
                dve_max(dve, 0)
                for j, ahead in [(j, 1) for s in range(MAHEAD) for j in range(MJOBS) if j * KT // MJOBS == s]:
                    dve_rough(dve, j, 1, MJOBS + j)
                dve_pair(dve, 0, first=True)
                with dve.Fori(1, NP - 1) as p:
                    dve_pair(dve, p)
                dve_pair(dve, NP - 1, last=True)
                add_tile(dve, DVE_TILES, acc_d, summed_dve, ND - 1, UNITS - 1, NP * UNITS - 1, NP * SLOTS - KT)
                dve_rec(dve, NP * UNITS - 1)
                dve_norm(dve, NP * UNITS - 1, UNITS - 1)

            @block.gpsimd
            def _(pool):
                pool_pair(pool, 0)
                with pool.Fori(1, NP) as p:
                    pool_pair(pool, p)


def phase_output(nc, S, A, G, sem, out):
    TT, D, E, NP, QC = S.TT, S.D, S.E, S.NP, S.QC
    BT = QC // P
    NB = TT // BT
    HN = NP // 2
    with ExitStack() as ctx:
        def sb(name, shape, dt=F32):
            return ctx.enter_context(nc.sbuf_tensor(name, shape, dt))

        wo_in = sb("wo_in", [P, NP, D])
        wo_hi, wo_lo = sb("wo_hi", [P, NP, D], F32R), sb("wo_lo", [P, NP, D], F32R)
        bo_sb = sb("bo_sb", [P, D])
        ot = [sb(f"ot{b}", [P, NP, QC]) for b in range(2)]
        ot_hi = [sb(f"ot_hi{b}", [P, NP, QC], F32R) for b in range(2)]
        ot_lo = sb("ot_lo", [P, NP, QC], F32R)
        x1 = sb("x1", [P, TT, D])
        xn = sb("xn2", [P, TT, D + E])
        xn_t = sb("xn_t", [P, S.KD, QC])
        rw_in = sb("rw_in", [E, D])
        rw_t = sb("rw_t", [P, S.KD, E])
        b1_in = sb("b1_in", [E * S.HT, P])
        stats, mv = sb("ln2_stats", [P, TT, 6]), sb("ln2_mv", [P, TT, 2])
        std, rstd, nt, eps = sb("ln2_std", [P, TT]), sb("ln2_rstd", [P, TT]), sb("ln2_nt", [P, TT]), sb("ln2_eps", [P, 1])
        lg = sb("lg", [P, TT, E])
        lmax, lsum, lrec = sb("lmax", [P, TT]), sb("lsum", [P, TT]), sb("lrec", [P, TT])
        ps_y = ctx.enter_context(nc.psum_tensor("ps_out", [P, 2, QC], F32))
        ps_t = ctx.enter_context(nc.psum_tensor("ps_out_t", [P, 2, QC], F32))
        ps_l = ctx.enter_context(nc.psum_tensor("ps_logits", [P, TT, E], F32))
        ps_r = ctx.enter_context(nc.psum_tensor("ps_small", [P, QC], F32))

        wo_loaded, bo_loaded, small_loaded = sem("wo_loaded"), sem("bo_loaded"), sem("small_loaded")
        x_loaded = [sem(f"x_loaded{b}") for b in range(NB)]
        ot_loaded = [sem(f"ot_loaded{b}") for b in range(2)]
        wo_hi_done, wo_lo_done = sem("wo_hi_done"), sem("wo_lo_done")
        ot_hi_done, ot_lo_dve, ot_lo_pool = sem("ot_hi_done"), sem("ot_lo_dve"), sem("ot_lo_pool")
        biased, eps_set = sem("biased"), sem("eps_set")
        y_ready, x1_done = sem("y_ready"), sem("x1_done")
        stats_done, mv_done, std_done, rstd_done, xn_done = (sem(f"ln2_{n}_done") for n in ("stats", "mv", "std", "rstd", "xn"))
        small_t, small_copied = sem("small_t"), sem("small_copied")
        t_ready, t_copied, logits_ready = sem("xn_t_ready"), sem("xn_t_copied"), sem("logits_ready")
        softmax, exp_l = sem("softmax_steps"), sem("logits_exp")
        x1_stored, table_stored = sem("x1_stored"), sem("table_stored")

        xv = A["x"][0].rearrange("(t p) d -> p t d", p=P)
        ov = out[0].rearrange("(t p) d -> p t d", p=P)

        with nc.Block() as block:

            @block.sync
            def _(sp):
                def load_ot(b):
                    sp.dma_start(ot[b % 2][:], G.o_scr[:, :, b * QC:(b + 1) * QC].rearrange("h p q -> p h q")).then_inc(ot_loaded[b % 2], 16)

                sp.dma_start(wo_in[:], A["wo"].rearrange("(h p) n -> p h n", p=P)).then_inc(wo_loaded, 16)
                load_ot(0)
                load_ot(1)
                sp.dma_start(rw_in[:], A["router_w"]).then_inc(small_loaded, 16)
                sp.dma_start(b1_in[:], A["b1"].rearrange("e (h p) -> (e h) p", p=P)).then_inc(small_loaded, 16)
                sp.dma_start(bo_sb[:], A["bo"].rearrange("(o n) -> o n", o=1).to_broadcast([P, D])).then_inc(bo_loaded, 16)
                for b in range(NB):
                    sp.dma_start(x1[:, b * BT:(b + 1) * BT, :], xv[:, b * BT:(b + 1) * BT, :]).then_inc(x_loaded[b], 16)
                for b in range(2, NB):
                    sp.wait_ge(ot_hi_done, b - 1)
                    sp.wait_ge(ot_lo_dve, b - 1)
                    sp.wait_ge(ot_lo_pool, b - 1)
                    load_ot(b)
                for b in range(NB):
                    sp.wait_ge(x1_done, (b + 1) * BT)
                    sp.dma_start(ov[:, b * BT:(b + 1) * BT, :], x1[:, b * BT:(b + 1) * BT, :]).then_inc(x1_stored, 16)
                sp.wait_ge(xn_done, TT)
                sp.wait_ge(softmax, 5)
                sp.dma_start(G.table.rearrange("(t p) d -> p t d", p=P), xn[:]).then_inc(table_stored, 16)
                sp.wait_ge(x1_stored, 16 * NB)
                sp.wait_ge(table_stored, 16)

            @block.gpsimd
            def _(pool):
                def bias(b):
                    pool.wait_ge(x_loaded[b], 16)
                    pool.tensor_tensor(x1[:, b * BT:(b + 1) * BT, :], x1[:, b * BT:(b + 1) * BT, :],
                                       bo_sb[:, None, :].to_broadcast([P, BT, D]), ALU.add).then_inc(biased, 1)

                def lo(b):
                    pool.wait_ge(ot_hi_done, b + 1)
                    if b >= 1:
                        pool.wait_ge(y_ready, b * BT)
                    pool.tensor_tensor(ot_lo[:, HN:NP, :], ot[b % 2][:, HN:NP, :], raw(ot_hi[b % 2][:, HN:NP, :]),
                                       ALU.subtract).then_inc(ot_lo_pool, 1)

                lo(0)
                pool.wait_ge(bo_loaded, 16)
                bias(0)
                for b in range(1, NB):
                    lo(b)
                    bias(b)

            @block.scalar
            def _(act):
                def hi(b):
                    act.wait_ge(ot_loaded[b % 2], 16 * (b // 2 + 1))
                    if b >= 2:
                        act.wait_ge(y_ready, (b - 1) * BT)
                    act.activation(ot_hi[b % 2][:], ot[b % 2][:], ACT.Copy).then_inc(ot_hi_done, 1)

                act.wait_ge(wo_loaded, 16)
                act.activation(wo_hi[:], wo_in[:], ACT.Copy).then_inc(wo_hi_done, 1)
                hi(0)
                hi(1)
                act.wait_ge(small_t, 1)
                act.activation(rw_t[:].rearrange("p k e -> p (k e)"), ps_r[:, 0:S.KD * E], ACT.Copy).then_inc(small_copied, 1)
                act.activation(G.b1_t[:], ps_r[:, S.KD * E:S.KD * E + E * S.HT], ACT.Copy).then_inc(small_copied, 1)
                act.wait_ge(eps_set, 1)
                for b in range(NB):
                    if b + 2 < NB:
                        hi(b + 2)
                    act.wait_ge(mv_done, (b + 1) * BT)
                    act.activation(std[:, b * BT:(b + 1) * BT], mv[:, b * BT:(b + 1) * BT, 1], ACT.Sqrt,
                                   bias=eps[:, 0:1]).then_inc(std_done, 1)
                    act.wait_ge(t_ready, b + 1)
                    if b >= 1:
                        act.wait_ge(logits_ready, b)
                    act.activation(xn_t[:], ps_t[:], ACT.Copy).then_inc(t_copied, 1)
                act.wait_ge(softmax, 2)
                act.activation(lg[:], lg[:], ACT.Exp).then_inc(exp_l, 1)

            @block.vector
            def _(dve):
                def lo(b):
                    dve.wait_ge(ot_hi_done, b + 1)
                    if b >= 1:
                        dve.wait_ge(y_ready, b * BT)
                    dve.tensor_tensor(ot_lo[:, 0:HN, :], ot[b % 2][:, 0:HN, :], raw(ot_hi[b % 2][:, 0:HN, :]),
                                      ALU.subtract).then_inc(ot_lo_dve, 1)

                dve.memset(eps[:], EPS).then_inc(eps_set, 1)
                dve.wait_ge(wo_loaded, 16)
                dve.wait_ge(wo_hi_done, 1)
                dve.tensor_tensor(wo_lo[:], wo_in[:], raw(wo_hi[:]), ALU.subtract).then_inc(wo_lo_done, 1)
                lo(0)
                for b in range(NB):
                    dve.wait_ge(biased, b + 1)
                    for t in range(b * BT, (b + 1) * BT):
                        dve.wait_ge(y_ready, t + 1)
                        dve.tensor_tensor(x1[:, t, :], ps_y[:, t % 2, 0:D], x1[:, t, :], ALU.add).then_inc(x1_done, 1)
                        if t == (b + 1) * BT - 1 and b + 1 < NB:
                            lo(b + 1)
                        dve.wait_ge(x1_done, t + 1)
                        dve.bn_stats(stats[:, t, :], x1[:, t, :]).then_inc(stats_done, 1)
                        dve.wait_ge(stats_done, t + 1)
                        dve.bn_aggr(mv[:, t, :], stats[:, t, :]).then_inc(mv_done, 1)
                    g = slice(b * BT, (b + 1) * BT)
                    dve.wait_ge(std_done, b + 1)
                    dve.reciprocal(rstd[:, g], std[:, g]).then_inc(rstd_done, 1)
                    dve.wait_ge(rstd_done, 5 * b + 1)
                    refine_rstd(dve, mv[:, g, 1], rstd[:, g], nt[:, g], rstd_done, 5 * b + 1)
                    for t in range(b * BT, (b + 1) * BT):
                        dve.tensor_scalar(xn[:, t, 0:D], x1[:, t, :], mv[:, t, 0:1], rstd[:, t:t + 1],
                                          ALU.subtract, ALU.mult).then_inc(xn_done, 1)
                dve.wait_ge(logits_ready, NB)
                dve.tensor_reduce(lmax[:], ps_l[:], AX.X, ALU.max).then_inc(softmax, 1)
                dve.wait_ge(softmax, 1)
                dve.tensor_tensor(lg[:], ps_l[:], lmax[:, :, None].to_broadcast([P, TT, E]), ALU.subtract).then_inc(softmax, 1)
                dve.wait_ge(exp_l, 1)
                dve.tensor_reduce(lsum[:], lg[:], AX.X, ALU.add).then_inc(softmax, 1)
                dve.wait_ge(softmax, 3)
                dve.reciprocal(lrec[:], lsum[:]).then_inc(softmax, 1)
                dve.wait_ge(softmax, 4)
                dve.tensor_tensor(xn[:, :, D:D + E], lg[:], lrec[:, :, None].to_broadcast([P, TT, E]), ALU.mult).then_inc(softmax, 1)
                dve.tensor_tensor(G.scores[:], lg[:].rearrange("p t e -> p e t"), lrec[:, None, :].to_broadcast([P, E, TT]),
                                  ALU.mult).then_inc(softmax, 1)

            @block.tensor
            def _(pe):
                def transposes(b):
                    pe.wait_ge(xn_done, (b + 1) * BT)
                    if b >= 1:
                        pe.wait_ge(t_copied, b)
                    for k in range(S.KD):
                        for i in range(BT):
                            last = pe.transpose(ps_t[:, k, i * P:(i + 1) * P], xn[:, b * BT + i, k * P:(k + 1) * P], G.ident[:])
                    last.then_inc(t_ready, 1)

                def logits(b):
                    pe.wait_ge(t_copied, b + 1)
                    for i in range(BT):
                        for k in range(S.KD):
                            last = pe.matmul(ps_l[:, b * BT + i, :], xn_t[:, k, i * P:(i + 1) * P], rw_t[:, k, :],
                                             start=(k == 0), stop=(k == S.KD - 1))
                    last.then_inc(logits_ready, 1)

                pe.wait_ge(small_loaded, 32)
                for k in range(S.KD):
                    pe.transpose(ps_r[:, k * E:(k + 1) * E], rw_in[:, k * P:(k + 1) * P], G.ident[0:E, 0:E])
                pe.transpose(ps_r[:, S.KD * E:S.KD * E + E * S.HT], b1_in[:], G.ident[0:E * S.HT, 0:E * S.HT]).then_inc(small_t, 1)
                pe.wait_ge(small_copied, 2)
                pe.wait_ge(wo_lo_done, 1)
                for b in range(NB):
                    pe.wait_ge(ot_hi_done, b + 1)
                    pe.wait_ge(ot_lo_dve, b + 1)
                    pe.wait_ge(ot_lo_pool, b + 1)
                    for i in range(BT):
                        t = b * BT + i
                        if t >= 2:
                            pe.wait_ge(x1_done, t - 1)
                        cols = slice(i * P, (i + 1) * P)
                        n = 0
                        for h in range(NP):
                            for o, w in ((ot_hi[b % 2], wo_hi), (ot_hi[b % 2], wo_lo), (ot_lo, wo_hi)):
                                last = pe.matmul(ps_y[:, t % 2, 0:D], o[:, h, cols], w[:, h, :], start=(n == 0), stop=(n == 3 * NP - 1))
                                n += 1
                        last.then_inc(y_ready, 1)
                        if i == 1 and b >= 1:
                            transposes(b - 1)
                        if i == 2 and b >= 1:
                            logits(b - 1)
                transposes(NB - 1)
                logits(NB - 1)


RT = 104
SEARCH_BITS = 30


def phase_experts(nc, S, A, G, sem, out):
    TT, D, E, HT, KD, CAP = S.TT, S.D, S.E, S.HT, S.KD, S.CAP
    ST = -(-CAP // RT)
    TAIL = CAP - (ST - 1) * RT
    NS = CAP + 3 - (CAP + 3) % 4
    HS = NS // 2
    ROUNDS = SEARCH_BITS // 2
    TJ = 3
    assert E * TT == P and TAIL % 2 == 1 and NS <= ST * RT and HS % 2 == 0
    rows = [RT] * (ST - 1) + [TAIL]
    with ExitStack() as ctx:
        def sb(name, shape, dt=F32):
            return ctx.enter_context(nc.sbuf_tensor(name, shape, dt))

        def ps(name, shape):
            return ctx.enter_context(nc.psum_tensor(name, shape, F32))

        cand = [sb(f"cand{i}", [P, E, 4], I32) for i in range(2)]
        step = sb("step", [P, 3], I32)
        above = sb("above", [P, E, 3, TT], BF16)
        part = sb("part", [P, E, 3], BF16)
        ones_b = sb("ones_b", [P, P], BF16)
        before = sb("before", [P, P], BF16)
        mask = sb("mask", [P, 2, E, TT], BF16)
        cnt = sb("cnt", [P, E], BF16)
        need = sb("need", [P, E])
        tie, sel, pos = sb("tie", [P, E, TT]), sb("sel", [P, E, TT]), sb("pos", [P, E, TT])
        tile_no, slot = sb("tile_no", [P, E, TT]), sb("slot", [P, E, TT])
        iota_i = sb("iota_i", [P, P], I32)
        iota_r = sb("iota_r", [P, RT])
        iota_p = sb("iota_p", [P, 1])
        tile_hot = sb("tile_hot", [P, E, TT, ST])
        ids = sb("ids", [P, E, TT, 2, ST], BF16)
        row_hot = [sb(f"row_hot{b}", [P, TT, RT], BF16) for b in range(2)]
        idx_g = [sb(f"idx_g{b}", [RT, ST], I32) for b in range(2)]
        idx_s = [sb(f"idx_s{b}", [RT, ST], I32) for b in range(2)]
        w1_in = [sb(f"w1_in{b}", [P, KD, S.HID]) for b in range(2)]
        w2_in = [sb(f"w2_in{b}", [P, HT, D]) for b in range(2)]
        w1_hi = [sb(f"w1_hi{b}", [P, KD, S.HID], F32R) for b in range(2)]
        w1_lo = [sb(f"w1_lo{b}", [P, KD, S.HID], F32R) for b in range(2)]
        w2_hi = [sb(f"w2_hi{b}", [P, HT, D], F32R) for b in range(2)]
        w2_lo = [sb(f"w2_lo{b}", [P, HT, D], F32R) for b in range(2)]
        b2_sb = sb("b2_sb", [RT, E, D])
        xg = [sb(f"xg{b}", [RT, ST, D + E]) for b in range(2)]
        xt_hi, xt_lo = sb("xgt_hi", [P, KD, ST * RT], F32R), sb("xgt_lo", [P, KD, ST * RT], F32R)
        h_f = sb("h_f", [P, 2, NS])
        h_hi, h_lo = sb("h_hi", [P, HT, NS], F32R), sb("h_lo", [P, HT, NS], F32R)
        y_sb = [sb(f"y_sb{b}", [RT, ST, D]) for b in range(2)]
        ps_h = ps("ps_h", [P, 2, 2, 512])
        ps_y = ps("ps_y2", [P, 2, 512])
        ps_t = ps("ps_xgt", [P, 2, 512])
        ps_c, ps_pre, ps_i = ps_y, ps_t[:, 0, 0:2 * P], ps_t[:, 1, 0:2 * ST]

        consts, masks_set = sem("consts"), sem("masks_set")
        srch, counted, cand_done = sem("srch"), sem("counted"), sem("parts_ready")
        counts_ready, ranks = sem("counts_ready"), sem("ranks_ready")
        hot_ready, list_ready, idx_ready, idx_kept = sem("hot_ready"), sem("list_ready"), sem("idx_ready"), sem("idx_kept")
        w1_loaded = [sem(f"w1_loaded{b}") for b in range(2)]
        w2_loaded = [sem(f"w2_loaded{b}") for b in range(2)]
        b2_loaded = sem("b2_loaded")
        w1_hi_done, w1_lo_done, w2_hi_done, w2_lo_done = (sem(n) for n in ("w1_hi_done", "w1_lo_done", "w2_hi_done", "w2_lo_done"))
        gathered = [sem(f"gathered{b}") for b in range(2)]
        scattered = [sem(f"scattered{b}") for b in range(2)]
        xgt_ready, xgt_hi_done, xgt_lo_done, padded = sem("xgt_ready"), sem("xgt_hi_done"), sem("xgt_lo_done"), sem("xgt_padded")
        h_ready, gelu_done, h_hi_done, h_lo_done = sem("h_ready"), sem("gelu_done"), sem("h_hi_done"), sem("h_lo_done")
        y_ready, y_read, y_done = sem("y2_ready"), sem("y2_read"), sem("y2_done")

        def sp_weights(sp, e, i, b):
            wait_for(sp, w1_lo_done, e - 1)
            sp.dma_start(w1_in[b][:], w1v(e)).then_inc(w1_loaded[b], 16)
            wait_for(sp, w2_lo_done, e - 1)
            sp.dma_start(w2_in[b][:], w2v(e)).then_inc(w2_loaded[b], 16)

        def w1v(e):
            return (A["w1"][e:e + 1] if isinstance(e, int) else A["w1"][bass.ds(e, 1)]).rearrange("o (k p) n -> p (o k) n", p=P)

        def w2v(e):
            return (A["w2"][e:e + 1] if isinstance(e, int) else A["w2"][bass.ds(e, 1)]).rearrange("o (h p) n -> p (o h) n", p=P)

        def at(e):
            return slice(e, e + 1) if isinstance(e, int) else bass.ds(e, 1)

        def dve_w1_hi(dve, e, i, b):
            dve.wait_ge(w1_loaded[b], 16 * (i + 1))
            wait_for(dve, h_ready, HT * (e - 1))
            dve.tensor_copy(w1_hi[b][:], w1_in[b][:]).then_inc(w1_hi_done, 1)

        def act_w2_hi(act, e, i, b):
            act.wait_ge(w2_loaded[b], 16 * (i + 1))
            wait_for(act, y_ready, ST * (e - 1))
            act.activation(w2_hi[b][:], w2_in[b][:], ACT.Copy).then_inc(w2_hi_done, 1)

        def pool_lo(pool, e, b):
            pool.wait_ge(w1_hi_done, e + 1)
            pool.tensor_tensor(w1_lo[b][:], w1_in[b][:], raw(w1_hi[b][:]), ALU.subtract).then_inc(w1_lo_done, 1)
            pool.wait_ge(w2_hi_done, e + 1)
            pool.tensor_tensor(w2_lo[b][:], w2_in[b][:], raw(w2_hi[b][:]), ALU.subtract).then_inc(w2_lo_done, 1)

        def dve_hot(dve, e, b):
            wait_for(dve, list_ready, e - 1)
            dve.tensor_tensor(row_hot[b][:], slot[:, at(e), :].rearrange("p o t -> p (o t)")[:, :, None].to_broadcast([P, TT, RT]),
                              iota_r[:, None, :].to_broadcast([P, TT, RT]), ALU.is_equal).then_inc(hot_ready, 1)

        def pe_list(pe, e, b):
            pe.wait_ge(hot_ready, e + 1)
            wait_for(pe, xgt_lo_done, TJ * e - 1)
            for t in range(TT):
                last = pe.matmul(ps_i[0:RT, :], row_hot[b][:, t, :], ids[:, at(e), t, :, :].rearrange("p o a j -> p (o a j)"),
                                 start=(t == 0), stop=(t == TT - 1))
            last.then_inc(list_ready, 1)

        def dve_index(dve, e, i, b):
            dve.wait_ge(list_ready, e + 1)
            wait_for(dve, gathered[b], 16 * ST * i)
            wait_for(dve, idx_kept, e - 1)
            dve.tensor_scalar(idx_f[:], ps_i[0:RT, 0:ST], float(P), None, ALU.mult).then_inc(idx_mul, 1)
            dve.wait_ge(idx_mul, e + 1)
            dve.tensor_tensor(idx_g[b][:], ps_i[0:RT, ST:2 * ST], idx_f[:], ALU.add).then_inc(idx_ready, 1)

        idx_f, idx_mul = sb("idx_f", [RT, ST]), sem("idx_mul")

        def pool_gather(pool, e, i, b):
            pool.wait_ge(idx_ready, e + 1)
            wait_for(pool, xgt_ready, TJ * (e - 1))
            wait_for(pool, y_done, ST * (e - 1))
            for j, n in enumerate(rows):
                pool.indirect_dma_start(xg[b][0:n, j, :], None, G.table,
                                        bass.IndirectOffsetOnAxis(ap=idx_g[b][0:n, j:j + 1], axis=0)).then_inc(gathered[b], 16)

        groups = [(0, [(j, 0) for j in range(ST - 1)]), (1, [(j, 1) for j in range(ST - 1)]), (0, [(ST - 1, 0), (ST - 1, 1)])]
        FULL = (ST - 1) * RT

        def xgt_views(n):
            if n < 2:
                return ps_t[:, n, 0:FULL], xt_hi[:, n, 0:FULL], xt_lo[:, n, 0:FULL]
            return (ps_t[:, 0, 0:2 * RT].rearrange("p (k c) -> p k c", k=2)[:, :, 0:TAIL],
                    xt_hi[:, :, FULL:FULL + TAIL], xt_lo[:, :, FULL:FULL + TAIL])

        def pe_xgt(pe, e, i, b, n):
            if n == 0:
                pe.wait_ge(gathered[b], 16 * ST * (i + 1))
                wait_for(pe, xgt_lo_done, TJ * e)
            elif n == 1:
                pe.wait_ge(idx_ready, e + 1)
            else:
                pe.wait_ge(xgt_lo_done, TJ * e + 1)
            bank, tiles = groups[n]
            for c, (j, k) in enumerate(tiles):
                r = rows[j]
                last = pe.transpose(ps_t[:, bank, c * RT:c * RT + r], xg[b][0:r, j, k * P:(k + 1) * P], G.ident[0:r, 0:r])
            last.then_inc(xgt_ready, 1)

        def act_xgt(act, e, n):
            act.wait_ge(xgt_ready, TJ * e + n + 1)
            src, hi, _ = xgt_views(n)
            act.activation(hi, src, ACT.Copy).then_inc(xgt_hi_done, 1)

        def dve_xgt(dve, e, n):
            dve.wait_ge(xgt_hi_done, TJ * e + n + 1)
            src, hi, lo = xgt_views(n)
            dve.tensor_tensor(lo, src, raw(hi), ALU.subtract).then_inc(xgt_lo_done, 1)

        def pe_h(pe, e, b, h):
            if h == 0:
                pe.wait_ge(w1_lo_done, e + 1)
                pe.wait_ge(xgt_lo_done, TJ * (e + 1))
            wait_for(pe, gelu_done, HT * e + h - 1)
            cols = slice(h * P, (h + 1) * P)
            terms = [(w, x, k) for k in range(KD) for w, x in ((w1_hi[b], xt_hi), (w1_hi[b], xt_lo), (w1_lo[b], xt_hi))]
            for c in range(2):
                for n, (w, x, k) in enumerate(terms):
                    last = pe.matmul(ps_h[:, h % 2, c, 0:HS], w[:, k, cols], x[:, k, c * HS:(c + 1) * HS],
                                     start=(n == 0), stop=(n == len(terms) - 1))
            last.then_inc(h_ready, 1)

        def act_h(act, e, h):
            act.wait_ge(h_ready, HT * e + h + 1)
            wait_for(act, h_lo_done, HT * e + h - 1)
            act.activation(h_f[:, h % 2, :].rearrange("p (c n) -> p c n", c=2), ps_h[:, h % 2, :, 0:HS], ACT.Gelu,
                           bias=G.b1_t[:, b1_col(e, h)]).then_inc(gelu_done, 1)
            act.wait_ge(gelu_done, HT * e + h + 1)
            act.activation(h_hi[:, h, :], h_f[:, h % 2, :], ACT.Copy).then_inc(h_hi_done, 1)

        def b1_col(e, h):
            return at(e * HT + h)

        def dve_h(dve, e, h):
            dve.wait_ge(h_hi_done, HT * e + h + 1)
            dve.tensor_tensor(h_lo[:, h, :], h_f[:, h % 2, :], raw(h_hi[:, h, :]), ALU.subtract).then_inc(h_lo_done, 1)

        def pe_y(pe, e, b, j):
            if j == 0:
                pe.wait_ge(w2_lo_done, e + 1)
            wait_for(pe, y_read, ST * e + j - 1)
            m = rows[j] + rows[j] % 2
            bank = (ST * b + j) % 2
            for h in range(HT):
                if j == 0:
                    pe.wait_ge(h_lo_done, HT * e + h + 1)
                for n, (x, w) in enumerate(((h_hi, w2_hi[b]), (h_hi, w2_lo[b]), (h_lo, w2_hi[b]))):
                    last = pe.matmul(ps_y[0:m, bank, 0:D], x[:, h, j * RT:j * RT + m], w[:, h, :],
                                     start=(h == 0 and n == 0), stop=(h == HT - 1 and n == 2))
            last.then_inc(y_ready, 1)

        def dve_y(dve, e, i, b, j):
            n = rows[j]
            dve.wait_ge(y_ready, ST * e + j + 1)
            if j == 0:
                wait_for(dve, scattered[b], 16 * ST * i)
                dve.tensor_copy(idx_s[b][:], idx_g[b][:]).then_inc(idx_kept, 1)
            dve.tensor_tensor(y_sb[b][0:n, j, :], ps_y[0:n, (ST * b + j) % 2, 0:D],
                              b2_sb[0:n, at(e), :].rearrange("p o d -> p (o d)"), ALU.add).then_inc(y_read, 1)
            dve.wait_ge(y_read, ST * e + j + 1)
            dve.tensor_scalar(y_sb[b][0:n, j, :], y_sb[b][0:n, j, :], xg[b][0:n, j, at(D + e)], None, ALU.mult).then_inc(y_done, 1)

        def pool_scatter(pool, e, i, b):
            pool.wait_ge(idx_kept, e + 1)
            pool.wait_ge(y_done, ST * (e + 1))
            wait_for(pool, scattered[1 - b], 16 * ST * (i + b))
            for j, n in enumerate(rows):
                pool.indirect_dma_start(out[0], bass.IndirectOffsetOnAxis(ap=idx_s[b][0:n, j:j + 1], axis=0),
                                        y_sb[b][0:n, j, :], None, compute_op=ALU.add).then_inc(scattered[b], 16)

        def nxt(i, b):
            return i + b, 1 - b

        def pe_expert(pe, e, i, b, last):
            for h in range(HT):
                pe_h(pe, e, b, h)
                if h == 1 and not last:
                    pe_list(pe, e + 1, 1 - b)
            for j in range(ST):
                pe_y(pe, e, b, j)
                if not last:
                    for n in {0: (0, 1), 1: (2,)}.get(j, ()):
                        pe_xgt(pe, e + 1, *nxt(i, b), n)

        def act_expert(act, e, i, b, last):
            for h in range(HT):
                act_h(act, e, h)
            if not last:
                for n in range(TJ):
                    act_xgt(act, e + 1, n)
                act_w2_hi(act, e + 1, *nxt(i, b))

        def dve_expert(dve, e, i, b, last):
            if not last:
                dve_hot(dve, e + 1, 1 - b)
            for h in range(HT):
                dve_h(dve, e, h)
                if h == 1 and not last:
                    dve_index(dve, e + 1, *nxt(i, b))
                if h == 2 and not last:
                    dve_w1_hi(dve, e + 1, *nxt(i, b))
            for j in range(ST):
                dve_y(dve, e, i, b, j)
                if not last:
                    for n in {0: (0, 1), 1: (2,)}.get(j, ()):
                        dve_xgt(dve, e + 1, n)

        def pool_expert(pool, e, i, b, last):
            if not (isinstance(e, int) and e == 0):
                pool_scatter(pool, e - 1, i - 1 + b, 1 - b)
            if not last:
                pool_gather(pool, e + 1, *nxt(i, b))
                pool_lo(pool, e + 1, 1 - b)

        def all_experts(eng, expert):
            for b in range(2):
                expert(eng, b, 0, b, False)
            with eng.Fori(1, E // 2 - 1) as i:
                for b in range(2):
                    expert(eng, 2 * i + b, i, b, False)
            for b in range(2):
                expert(eng, E - 2 + b, E // 2 - 1, b, b == 1)

        STEPS = 5

        with nc.Block() as block:

            @block.sync
            def _(sp):
                sp_weights(sp, 0, 0, 0)
                sp_weights(sp, 1, 0, 1)
                sp.dma_start(b2_sb[:], A["b2"].rearrange("(o e) n -> o (e n)", o=1).to_broadcast([RT, E * D])
                             .rearrange("p (e n) -> p e n", e=E)).then_inc(b2_loaded, 16)
                with sp.Fori(1, E // 2) as i:
                    for b in range(2):
                        sp_weights(sp, 2 * i + b, i, b)

            @block.gpsimd
            def _(pool):
                pool.memset(step[:, 0:1], 1 << (SEARCH_BITS - 2)).then_inc(consts, 1)
                pool.memset(step[:, 1:2], 2 << (SEARCH_BITS - 2)).then_inc(consts, 1)
                pool.memset(step[:, 2:3], 3 << (SEARCH_BITS - 2)).then_inc(consts, 1)
                pool.memset(cand[0][:], 0).then_inc(consts, 1)
                pool.memset(ones_b[:], 1.0).then_inc(consts, 1)
                pool.memset(before[:], 1.0).then_inc(masks_set, 1)
                pool.wait_ge(masks_set, 1)
                pool.affine_select(out=before[:], in_=before[:], compare_op=ALU.is_gt, fill=0.0, base=0,
                                   pattern=[[1, P]], channel_multiplier=-1).then_inc(masks_set, 1)
                pool.iota(iota_i[:], pattern=[[1, P]], base=0, channel_multiplier=0).then_inc(masks_set, 1)
                pool.wait_ge(masks_set, 3)
                pool.tensor_copy(iota_r[:], iota_i[:, 0:RT]).then_inc(masks_set, 1)
                pool.wait_ge(masks_set, 4)
                pool.iota(iota_i[:, 0:1], pattern=[[0, 1]], base=0, channel_multiplier=1).then_inc(masks_set, 1)
                pool.wait_ge(masks_set, 5)
                pool.tensor_copy(iota_p[:], iota_i[:, 0:1]).then_inc(masks_set, 1)
                pool.memset(raw(xt_hi[:, :, CAP:NS]), 0.0).then_inc(padded, 1)
                pool.memset(raw(xt_lo[:, :, CAP:NS]), 0.0).then_inc(padded, 1)
                pool_lo(pool, 0, 0)
                pool_gather(pool, 0, 0, 0)
                for e in range(E):
                    pool_expert(pool, e, e // 2, e % 2, e == E - 1)
                pool_scatter(pool, E - 1, E // 2 - 1, 1)
                for b in range(2):
                    pool.wait_ge(scattered[b], 16 * ST * (E // 2))

            @block.scalar
            def _(act):
                act_w2_hi(act, 0, 0, 0)
                for n in range(TJ):
                    act_xgt(act, 0, n)
                all_experts(act, act_expert)

            @block.tensor
            def _(pe):
                pe.wait_ge(consts, 5)
                with pe.Fori(0, ROUNDS) as r:
                    pe.wait_ge(cand_done, r + 1)
                    pe.matmul(ps_c[:, 0, 0:3 * E], ones_b[:], part[:].rearrange("p e j -> p (e j)"), start=True, stop=True).then_inc(counts_ready, 1)
                pe.wait_ge(masks_set, 2)
                pe.wait_ge(ranks, 3)
                pe.matmul(ps_c[:, 1, 0:E], ones_b[:], cnt[:], start=True, stop=True).then_inc(counts_ready, 1)
                flat = mask[:].rearrange("p a e t -> p (a e) t")
                pre = ps_pre.rearrange("p (a t) -> p a t", t=TT)
                pe.matmul(pre, before[:], flat, start=True, stop=False)
                for t in range(TT - 1):
                    last = pe.matmul(pre[:, :, t + 1:TT], ones_b[:], flat[:, :, t:t + 1].to_broadcast([P, 2 * E, TT - 1 - t]),
                                     start=False, stop=(t == TT - 2))
                last.then_inc(counts_ready, 1)
                pe.wait_ge(ranks, RANKS)
                pe_list(pe, 0, 0)
                pe.wait_ge(padded, 2)
                for n in range(TJ):
                    pe_xgt(pe, 0, 0, 0, n)
                all_experts(pe, pe_expert)

            @block.vector
            def _(dve):
                dve_w1_hi(dve, 0, 0, 0)
                dve.wait_ge(consts, 5)
                with dve.Fori(0, ROUNDS) as r:
                    a, c = cand
                    base = r * STEPS
                    dve.tensor_tensor(a[:, :, 1:4], a[:, :, 0:1].to_broadcast([P, E, 3]),
                                      step[:, None, :].to_broadcast([P, E, 3]), ALU.bitwise_or).then_inc(srch, 1)
                    dve.wait_ge(srch, base + 1)
                    dve.tensor_scalar(step[:], step[:], 2, None, ALU.logical_shift_right).then_inc(srch, 1)
                    dve.tensor_tensor(above[:], G.scores[:, :, None, :].to_broadcast([P, E, 3, TT]),
                                      a[:, :, 1:4, None].bitcast(F32).to_broadcast([P, E, 3, TT]), ALU.is_ge).then_inc(srch, 1)
                    dve.wait_ge(srch, base + 3)
                    with nc.allow_low_precision("counts of at most 16"):
                        dve.tensor_reduce(part[:], above[:], AX.X, ALU.add).then_inc(cand_done, 1)
                    dve.wait_ge(counts_ready, r + 1)
                    dve.scalar_tensor_tensor(out=a[:, :, 1:4].bitcast(F32), in0=ps_c[:, 0, 0:3 * E].rearrange("p (e j) -> p e j", j=3),
                                             scalar=float(CAP), in1=a[:, :, 1:4].bitcast(F32), op0=ALU.is_ge,
                                             op1=ALU.mult).then_inc(srch, 1)
                    dve.wait_ge(srch, base + 4)
                    dve.tensor_reduce(c[:, :, 0].bitcast(F32), a[:].bitcast(F32), AX.X, ALU.max).then_inc(srch, 1)
                    dve.wait_ge(srch, base + 5)
                    dve.tensor_copy(a[:, :, 0], c[:, :, 0]).then_inc(counted, 1)
                    dve.wait_ge(counted, r + 1)
                n = 0

                def step_done(ins):
                    nonlocal n
                    n += 1
                    ins.then_inc(ranks, 1)

                thr = cand[0][:, :, 0:1].bitcast(F32).to_broadcast([P, E, TT])
                step_done(dve.tensor_tensor(mask[:, 0], G.scores[:], thr, ALU.is_gt))
                step_done(dve.tensor_tensor(mask[:, 1], G.scores[:], thr, ALU.is_equal))
                dve.wait_ge(ranks, 2)
                with nc.allow_low_precision("counts of at most 16"):
                    step_done(dve.tensor_reduce(cnt[:], mask[:, 0], AX.X, ALU.add))
                dve.wait_ge(counts_ready, ROUNDS + 1)
                step_done(dve.tensor_scalar(need[:], ps_c[:, 1, 0:E], -1.0, float(CAP), ALU.mult, ALU.add))
                dve.wait_ge(ranks, n)
                dve.wait_ge(counts_ready, ROUNDS + 2)
                above_before, equal_before = (ps_pre[:, k * P:(k + 1) * P].rearrange("p (e t) -> p e t", e=E) for k in range(2))
                need_b = need[:, :, None].to_broadcast([P, E, TT])
                step_done(dve.tensor_tensor(tie[:], equal_before, need_b, ALU.is_lt))
                step_done(dve.tensor_tensor(pos[:], equal_before, need_b, ALU.min))
                dve.wait_ge(ranks, n)
                step_done(dve.tensor_tensor(sel[:], tie[:], mask[:, 1], ALU.mult))
                step_done(dve.tensor_tensor(pos[:], pos[:], above_before, ALU.add))
                dve.wait_ge(ranks, n)
                step_done(dve.tensor_tensor(sel[:], sel[:], mask[:, 0], ALU.add))
                dve.wait_ge(ranks, n)
                step_done(dve.scalar_tensor_tensor(out=pos[:], in0=pos[:], scalar=-float(FAR), in1=sel[:], op0=ALU.add, op1=ALU.mult))
                dve.wait_ge(ranks, n)
                step_done(dve.tensor_scalar(pos[:], pos[:], float(FAR), None, ALU.add))
                dve.wait_ge(ranks, n)
                step_done(dve.tensor_scalar(tile_no[:], pos[:], float(RT), None, ALU.is_ge))
                for j in range(2, ST):
                    dve.wait_ge(ranks, n)
                    step_done(dve.scalar_tensor_tensor(out=tile_no[:], in0=pos[:], scalar=float(j * RT), in1=tile_no[:],
                                                       op0=ALU.is_ge, op1=ALU.add))
                dve.wait_ge(ranks, n)
                dve.wait_ge(masks_set, 6)
                step_done(dve.scalar_tensor_tensor(out=slot[:], in0=tile_no[:], scalar=-float(RT), in1=pos[:], op0=ALU.mult, op1=ALU.add))
                step_done(dve.tensor_tensor(tile_hot[:], tile_no[:, :, :, None].to_broadcast([P, E, TT, ST]),
                                            iota_r[:, None, None, 0:ST].to_broadcast([P, E, TT, ST]), ALU.is_equal))
                dve.wait_ge(ranks, n)
                step_done(dve.tensor_tensor(ids[:, :, :, 0, :], tile_hot[:],
                                            iota_r[:, None, 0:TT, None].to_broadcast([P, E, TT, ST]), ALU.mult))
                step_done(dve.tensor_scalar(ids[:, :, :, 1, :], tile_hot[:], iota_p[:, 0:1], None, ALU.mult))
                assert n == RANKS
                dve_hot(dve, 0, 0)
                dve_index(dve, 0, 0, 0)
                dve.wait_ge(b2_loaded, 16)
                for k in range(TJ):
                    dve_xgt(dve, 0, k)
                all_experts(dve, dve_expert)


FAR = 4096
RANKS = 19


class Shared:
    pass


def build(nc, A, out, debug=None):
    S = Shapes(A["x"], A["ctx"], A["wq"], A["router_w"], A["w1"])
    G = Shared()
    with ExitStack() as top:
        def sem(name):
            return top.enter_context(nc.semaphore(name))

        G.wq_scr = nc.dram_tensor("wq_scr", [S.NP, P, 2, 2, P], F32).ap()
        G.wk_scr = nc.dram_tensor("wk_scr", [S.NP, P, 2, 2, P], F32).ap()
        G.q_scr = nc.dram_tensor("q_scr", [S.NP, 2, P, S.NT], F32).ap()
        G.k_scr = nc.dram_tensor("k_scr", [S.NP, 2, P, S.NKP], F32).ap()
        G.v_scr = nc.dram_tensor("v_scr", [S.H, P, S.KT, S.DH], F32).ap()
        G.rec_scr = nc.dram_tensor("rec_scr", [2, S.QC], F32).ap()
        G.o_scr = nc.dram_tensor("o_scr", [S.NP, P, S.NT], F32).ap()
        G.table = nc.dram_tensor("table", [S.NT, S.D + S.E], F32).ap()
        G.ident = top.enter_context(nc.sbuf_tensor("ident", [P, P], F32))
        G.ones = top.enter_context(nc.sbuf_tensor("ones", [P, P], F32))
        G.pad_bias = top.enter_context(nc.sbuf_tensor("pad_bias", [P, 1], F32))
        with ExitStack() as att:
            def sb(name, shape, dt=F32R):
                return att.enter_context(nc.sbuf_tensor(name, shape, dt))
            G.xt_hi, G.xt_lo = sb("xt_hi", [P, S.KD, S.NT]), sb("xt_lo", [P, S.KD, S.NT])
            G.c1_hi, G.c1_lo, G.c2 = sb("c1_hi", [P, S.NKP]), sb("c1_lo", [P, S.NKP]), sb("c2", [P, S.NKP])
            G.k2 = [sb(f"k2_{b}", [P, S.NKP]) for b in range(2)]
            G.q2 = [sb(f"q2_{b}", [P, S.NT]) for b in range(2)]
            phase_prologue(nc, S, A, G, sem)
            if debug != "prologue":
                phase_attention(nc, S, A, G, sem)
        if debug is None:
            G.scores = top.enter_context(nc.sbuf_tensor("scores", [P, S.E, S.TT], F32))
            G.b1_t = top.enter_context(nc.sbuf_tensor("b1_t", [P, S.E * S.HT], F32))
            phase_output(nc, S, A, G, sem, out)
            phase_experts(nc, S, A, G, sem, out)


_INS = {"x": "x", "ctx_768": "ctx", "L0_xattn_Wq": "wq", "L0_xattn_Wk": "wk", "L0_xattn_Wv": "wv", "L0_xattn_Wo": "wo",
        "L0_xattn_bo": "bo", "L0_ffn_router_w": "router_w", "L0_ffn_w1": "w1", "L0_ffn_b1": "b1", "L0_ffn_w2": "w2",
        "L0_ffn_b2": "b2"}


def kernel(**inputs):
    import numpy as _np
    import concourse.bacc as _bacc
    from concourse.bass_utils import run_bass_kernel_spmd as _run

    nc = _bacc.Bacc("TRN2", target_bir_lowering=False, num_devices=1)
    arrays, A = {}, {}
    for name, short in _INS.items():
        a = _np.ascontiguousarray(inputs[name])
        arrays[f"in_{short}"] = a
        A[short] = nc.dram_tensor(f"in_{short}", a.shape, mybir.dt.from_np(a.dtype), kind="ExternalInput").ap()
    out = nc.dram_tensor("out_0", inputs["x"].shape, F32, kind="ExternalOutput").ap()
    build(nc, A, out)
    r = _run(nc, [arrays], core_ids=[0])
    return r.results[0]["out_0"]
```

```python
from contextlib import ExitStack

import concourse.bass as bass
from concourse import mybir

ALU = mybir.AluOpType
ACT = mybir.ActivationFunctionType
AX = mybir.AxisListType
F32 = mybir.dt.float32
F32R = mybir.dt.float32r
BF16 = mybir.dt.bfloat16
I32 = mybir.dt.int32
U32 = mybir.dt.uint32

P = 128
EPS = 1e-5


def raw(ap):
    return ap.bitcast(F32)


class Shapes:

    def __init__(self, x, ctx, wq, router_w, w1):
        self.NT, self.D = x.shape[1], x.shape[2]
        self.NK, self.DC = ctx.shape[1], ctx.shape[2]
        self.DI = wq.shape[1]
        self.DH = 64
        self.H = self.DI // self.DH
        self.TT = self.NT // P
        self.KT = -(-self.NK // P)
        self.NKP = self.KT * P
        self.LAST = self.NK - (self.KT - 1) * P
        self.KD = self.D // P
        self.NP = self.H // 2
        self.QC = 512
        self.QB = self.NT // self.QC
        self.UQ = 2 * self.QC
        self.KC = self.NKP // 4
        self.MC = 402
        self.MS = [0, self.MC - 2, self.NK - 2 * self.MC + 2, self.NK - self.MC]
        assert self.MS[2] <= self.MS[1] + self.MC and self.DC == P + P // 2
        self.E, self.HID = router_w.shape[0], w1.shape[2]
        self.HT = self.HID // P
        self.CAP = int(self.NT * 2.0 / self.E) + 1


def refine_rstd(dve, var, rstd, tmp, done, count):
    dve.tensor_tensor(tmp, rstd, rstd, ALU.mult).then_inc(done, 1)
    dve.wait_ge(done, count + 1)
    dve.scalar_tensor_tensor(out=tmp, in0=var, scalar=EPS, in1=tmp, op0=ALU.add, op1=ALU.mult).then_inc(done, 1)
    dve.wait_ge(done, count + 2)
    dve.tensor_scalar(tmp, tmp, -0.5, 1.5, ALU.mult, ALU.add).then_inc(done, 1)
    dve.wait_ge(done, count + 3)
    dve.tensor_tensor(rstd, rstd, tmp, ALU.mult).then_inc(done, 1)
    dve.wait_ge(done, count + 4)


def head_parts(S, G, hd):
    HP = P // 2
    q1, q2, k1, k2 = G.q1[hd], G.q2[hd], G.k1[hd], G.k2[hd]
    return ((q1[0:HP, :], G.q_scr, 0), (q1[HP:P, :], G.q_scr, 0), (q2[0:HP, :], G.q_scr, 1),
            (k1[0:HP, :], G.k_scr, 0), (k1[HP:P, :], G.k_scr, 1), (k2[0:HP, :], G.k_scr, 0))


MJOBS = 32


def rough_scores(S, G, pe, bank, hd, half, j):
    q0, k0 = half * S.UQ + (j // 4) * P, S.MS[j % 4]
    pe.matmul(bank[:, 0:S.MC], G.q1[hd][:, q0:q0 + P], G.k1[hd][:, k0:k0 + S.MC], start=True, stop=True).then_inc(G.rough_ready, 1)


def rough_max(S, G, dve, bank, j):
    dve.tensor_reduce(G.mx_part[:, j // 4, j % 4:j % 4 + 1], bank[:, 0:S.MC], AX.X, ALU.max).then_inc(G.rough_used, 1)


def phase_prologue(nc, S, A, G, sem):
    with ExitStack() as ctx:
        def sb(name, shape, dt=F32):
            return ctx.enter_context(nc.sbuf_tensor(name, shape, dt))

        TT, KT, KD, LAST = S.TT, S.KT, S.KD, S.LAST
        HP = P // 2
        x_in = sb("x_in", [P, TT, S.D])
        stats = sb("ln1_stats", [P, TT, 6])
        mv = sb("ln1_mv", [P, TT, 2])
        std = sb("ln1_std", [P, TT])
        rstd = sb("ln1_rstd", [P, TT])
        nt = sb("ln1_nt", [P, TT])
        eps = sb("ln1_eps", [P, 1])
        c_in = sb("c_in", [P, KT, 2 * P])
        w_in = [sb(f"w_in{n}", [P, 2, S.DI]) for n in range(2)]
        w_in.append(w_in[0])
        w_hi = [sb(f"w_hi{n}", [P, 2, S.DI], F32R)[:] for n in range(2)] + [G.wo_hi[:].rearrange("p (k a) n -> p k (a n)", k=2)]
        w_lo = [sb(f"w_lo{n}", [P, 2, S.DI], F32R)[:] for n in range(2)] + [G.wo_lo[:].rearrange("p (k a) n -> p k (a n)", k=2)]
        v_st = sb("v_st", [P, 2, S.DI])
        ps = [ctx.enter_context(nc.psum_tensor(f"pro_ps{i}", [P, 512], F32)) for i in range(8)]

        s_c, s_cz = sem("p_c_loaded"), sem("p_c_padded")
        s_x = [sem(f"p_x_loaded{i}") for i in range(4)]
        s_w = [sem(f"p_w_loaded{i}") for i in range(3)]
        s_eps, s_stats, s_mv, s_std, s_rstd, s_xn = (sem(f"p_{n}") for n in ("eps", "stats", "mv", "std", "rstd", "xn"))
        s_whi, s_wlo, s_wst = sem("p_whi"), sem("p_wlo"), sem("p_wstored")
        s_ps, s_hi, s_lo = sem("p_ps_ready"), sem("p_hi_done"), sem("p_lo_done")
        s_v = sem("p_v_ready")
        s_vev = [sem(f"p_v_copied{i}") for i in range(2)]
        s_vst = [sem(f"p_v_stored{i}") for i in range(2)]
        s_id, s_ones = sem("p_ident"), sem("p_ones")
        s_rows = sem("p_rows")
        s_proj, s_sthi, s_stlo, s_head = sem("p_proj_ready"), sem("p_stage_hi"), sem("p_stage_lo"), sem("p_head_loaded")
        s_sst = [sem(f"p_stage_stored{i}") for i in range(2)]
        ident = G.ident

        xt = [("x", range(4 * g, 4 * g + 4), k) for g in range(TT // 4) for k in range(KD)]
        ct = [("c", range(4 * g, min(4 * g + 4, KT)), k) for g in range(-(-KT // 4)) for k in range(2)]
        tjobs = ct + xt
        NTJ = len(tjobs)

        def targets(job):
            src, tiles, k = job
            a, b = tiles[0] * P, (tiles[-1] + 1) * P
            if src == "x":
                return G.xt_hi[:, k, a:b], G.xt_lo[:, k, a:b], 0, b - a
            if k == 0:
                return G.c1_hi[:, a:b], G.c1_lo[:, a:b], 0, b - a
            return G.c2[:, a:b], G.c2[HP:P, a:b], HP, b - a

        vjobs = [(kt, half) for kt in range(KT) for half in range(2)]
        LOADS = (48, 16, 48)
        NPJ = 4

        def width(n):
            return S.KC if n < NPJ else S.QC

        def proj_before(j):
            return {len(ct): (0, 1), len(ct) + 4: (2, 3)}.get(j, ())

        def rough_after(j):
            first = len(vjobs) - MJOBS // 2
            return [2 * (j - first) + i for i in range(2)] if j >= first else []

        def stage(n, part):
            return v_st[:, part, (n % 2) * S.QC:(n % 2) * S.QC + width(n)].bitcast(F32R)

        with nc.Block() as block:

            @block.sync
            def _(sp):
                sp.dma_start(c_in[:, 0:KT - 1, 0:S.DC],
                             A["ctx"][0, 0:(KT - 1) * P, :].rearrange("(t p) d -> p t d", p=P)).then_inc(s_c, 16)
                sp.dma_start(c_in[:, 0:KT - 1, S.DC:2 * P],
                             A["ctx"][0, 0:(KT - 1) * P, P:S.DC].rearrange("(t p) d -> p t d", p=P)).then_inc(s_c, 16)
                sp.wait_ge(s_cz, 1)
                sp.dma_start(c_in[0:LAST, KT - 1, 0:S.DC], A["ctx"][0, (KT - 1) * P:S.NK, :]).then_inc(s_c, 16)
                sp.dma_start(c_in[0:LAST, KT - 1, S.DC:2 * P],
                             A["ctx"][0, (KT - 1) * P:S.NK, P:S.DC]).then_inc(s_c, 16)

                def load_split(n, w):
                    sp.dma_start(w_in[n][:, 0, :], A[w][0:P, :]).then_inc(s_w[n], 16)
                    sp.dma_start(w_in[n][0:HP, 1, :], A[w][P:S.DC, :]).then_inc(s_w[n], 16)
                    sp.dma_start(w_in[n][HP:P, 1, :], A[w][P:S.DC, :]).then_inc(s_w[n], 16)

                load_split(0, "wk")
                for g in range(4):
                    t = slice(g * TT // 4, (g + 1) * TT // 4)
                    sp.dma_start(x_in[:, t, :], A["x"][0].rearrange("(t p) d -> p t d", p=P)[:, t, :]).then_inc(s_x[g], 16)
                sp.dma_start(w_in[1][:], A["wq"].rearrange("(k p) n -> p k n", p=P)).then_inc(s_w[1], 16)
                sp.wait_ge(s_wlo, 1)
                load_split(2, "wv")

                def store_weight(n, scr):
                    sp.wait_ge(s_whi, n + 1)
                    sp.wait_ge(s_wlo, n + 1)
                    for k in range(2):
                        for part, w in ((0, w_hi[n]), (1, w_lo[n])):
                            sp.dma_start(scr[:, :, part, k, :].rearrange("h p c -> p h c"),
                                         raw(w[:, k, :]).rearrange("p (h c) -> p h c", c=P)).then_inc(s_wst, 16)

                def store_blocks(blocks, scr, w):
                    for c, n in enumerate(blocks):
                        sp.wait_ge(s_stlo, n + 1)
                        for part in range(2):
                            sp.dma_start(scr[0, part, :, c * w:(c + 1) * w], raw(stage(n, part))).then_inc(s_sst[n % 2], 16)

                def store_v(kt):
                    sp.wait_ge(s_vev[0], kt + 1)
                    sp.wait_ge(s_vev[1], kt + 1)
                    sp.dma_start(G.v_scr[:, :, kt, :].rearrange("h p d -> p h d"),
                                 v_st[:, kt % 2, :].rearrange("p (h d) -> p h d", d=S.DH)).then_inc(s_vst[kt % 2], 16)

                store_weight(0, G.wk_scr)
                store_blocks(range(NPJ), G.k_scr, S.KC)
                store_weight(1, G.wq_scr)
                store_blocks(range(NPJ, 2 * NPJ), G.q_scr, S.QC)
                for b in range(2):
                    sp.wait_ge(s_sst[b], 32 * NPJ)
                for dst, scr, part in head_parts(S, G, 0):
                    sp.dma_start(raw(dst), scr[0, part, 0:HP, :]).then_inc(s_head, 16)
                for kt in range(KT):
                    store_v(kt)
                sp.wait_ge(s_head, 96)
                sp.wait_ge(s_wst, 128)
                sp.wait_ge(s_vst[0], 16 * ((KT + 1) // 2))
                sp.wait_ge(s_vst[1], 16 * (KT // 2))

            @block.gpsimd
            def _(pool):
                pool.memset(ident[:], 0.0).then_inc(s_id, 1)
                pool.wait_ge(s_id, 1)
                pool.affine_select(out=ident[:], in_=ident[:], compare_op=ALU.not_equal, fill=1.0, base=0,
                                   pattern=[[-1, P]], channel_multiplier=1).then_inc(s_id, 1)
                pool.memset(G.ones[:], 1.0).then_inc(s_ones, 1)
                pool.memset(G.pad_bias[:], 0.0).then_inc(s_ones, 1)
                pool.wait_ge(s_ones, 2)
                pool.affine_select(out=G.pad_bias[:], in_=G.pad_bias[:], compare_op=ALU.is_gt, fill=-10000.0,
                                   base=LAST, pattern=[[0, 1]], channel_multiplier=-1).then_inc(s_ones, 1)
                for n in range(3):
                    pool.wait_ge(s_w[n], LOADS[n])
                    pool.wait_ge(s_whi, n + 1)
                    pool.tensor_tensor(w_lo[n], w_in[n][:], raw(w_hi[n]), ALU.subtract).then_inc(s_wlo, 1)

            @block.vector
            def _(dve):
                dve.memset(c_in[HP:P, KT - 1, :], 0.0).then_inc(s_cz, 1)
                dve.memset(eps[:], EPS).then_inc(s_eps, 1)
                for b in range(2):
                    dve.memset(raw(G.k2[b][HP:P, :]), 0.0).then_inc(s_rows, 1)
                    dve.memset(raw(G.q2[b][HP:P, :]), 0.0).then_inc(s_rows, 1)
                dve.wait_ge(s_rows, 4)
                for b in range(2):
                    dve.memset(raw(G.k2[b][HP:HP + 1, 0:S.NK]), 1.0).then_inc(s_rows, 1)

                def weight_hi(n):
                    dve.wait_ge(s_w[n], LOADS[n])
                    dve.tensor_copy(w_hi[n], w_in[n][:]).then_inc(s_whi, 1)

                def lo(j):
                    hi_t, lo_t, r0, n = targets(tjobs[j])
                    dve.wait_ge(s_ps, j + 1)
                    dve.wait_ge(s_hi, j + 1)
                    src = hi_t if r0 == 0 else G.c2[HP:P, tjobs[j][1][0] * P:(tjobs[j][1][-1] + 1) * P]
                    dve.tensor_tensor(lo_t, ps[j % 4][r0:P, 0:n], raw(src), ALU.subtract).then_inc(s_lo, 1)

                def proj_lo(n):
                    dve.wait_ge(s_sthi, n + 1)
                    dve.tensor_tensor(stage(n, 1), ps[4 + n % 4][:, 0:width(n)], raw(stage(n, 0)), ALU.subtract).then_inc(s_stlo, 1)

                for j in range(len(ct)):
                    lo(j)
                    if j == 2:
                        weight_hi(0)
                for t in range(TT):
                    if t % (TT // 4) == 0:
                        dve.wait_ge(s_x[t // (TT // 4)], 16)
                    dve.bn_stats(stats[:, t, :], x_in[:, t, :]).then_inc(s_stats, 1)
                for t in range(TT):
                    dve.wait_ge(s_stats, t + 1)
                    dve.bn_aggr(mv[:, t, :], stats[:, t, :]).then_inc(s_mv, 1)
                weight_hi(1)
                dve.wait_ge(s_std, 1)
                dve.reciprocal(rstd[:], std[:]).then_inc(s_rstd, 1)
                dve.wait_ge(s_rstd, 1)
                refine_rstd(dve, mv[:, :, 1], rstd[:], nt[:], s_rstd, 1)
                for t in range(TT):
                    dve.tensor_scalar(x_in[:, t, :], x_in[:, t, :], mv[:, t, 0:1], rstd[:, t:t + 1],
                                      ALU.subtract, ALU.mult).then_inc(s_xn, 1)
                for j in range(len(ct), NTJ):
                    for n in proj_before(j):
                        proj_lo(n)
                    lo(j)
                weight_hi(2)
                for n in range(NPJ, 2 * NPJ):
                    proj_lo(n)

                def rough(job):
                    for j in rough_after(job):
                        dve.wait_ge(G.rough_ready, j + 1)
                        rough_max(S, G, dve, ps[j % 2], j)

                for kt in range(KT):
                    rough(2 * kt)
                    dve.wait_ge(s_v, 2 * kt + 2)
                    if kt >= 2:
                        dve.wait_ge(s_vst[kt % 2], 16 * (kt // 2))
                    elif kt == 0:
                        for b in range(2):
                            dve.wait_ge(s_sst[b], 32 * NPJ)
                    dve.tensor_copy(v_st[:, kt % 2, 512:1024], ps[4 + (2 * kt + 1) % 4][:]).then_inc(s_vev[1], 1)
                    rough(2 * kt + 1)

            @block.scalar
            def _(act):
                def hi(j):
                    hi_t, lo_t, r0, n = targets(tjobs[j])
                    act.wait_ge(s_ps, j + 1)
                    act.activation(hi_t, ps[j % 4][:, 0:n], ACT.Copy).then_inc(s_hi, 1)

                def proj_hi(n):
                    act.wait_ge(s_proj, n + 1)
                    if n >= 2:
                        act.wait_ge(s_sst[n % 2], 32 * (n // 2))
                    act.activation(stage(n, 0), ps[4 + n % 4][:, 0:width(n)], ACT.Copy).then_inc(s_sthi, 1)

                for j in range(len(ct)):
                    hi(j)
                act.wait_ge(s_mv, TT)
                act.wait_ge(s_eps, 1)
                act.activation(std[:], mv[:, :, 1], ACT.Sqrt, bias=eps[:, 0:1]).then_inc(s_std, 1)
                for j in range(len(ct), NTJ):
                    for n in proj_before(j):
                        proj_hi(n)
                    hi(j)
                for n in range(NPJ, 2 * NPJ):
                    proj_hi(n)
                for kt in range(KT):
                    act.wait_ge(s_v, 2 * kt + 1)
                    if kt >= 2:
                        act.wait_ge(s_vst[kt % 2], 16 * (kt // 2))
                    elif kt == 0:
                        for b in range(2):
                            act.wait_ge(s_sst[b], 32 * NPJ)
                    act.activation(v_st[:, kt % 2, 0:512], ps[4 + (2 * kt) % 4][:], ACT.Copy).then_inc(s_vev[0], 1)

            @block.tensor
            def _(pe):
                def product(bank, terms):
                    for i, (a, b) in enumerate(terms):
                        last = pe.matmul(bank, a, b, start=(i == 0), stop=(i == len(terms) - 1))
                    return last

                def proj(n):
                    if n >= NPJ:
                        pe.wait_ge(s_stlo, n - NPJ + 1)
                    if n < NPJ:
                        hi, lo, cols = w_hi[0], w_lo[0], slice(n * S.KC, (n + 1) * S.KC)
                        terms = [(hi[:, 0, 0:P], G.c1_hi[:, cols]), (hi[:, 0, 0:P], G.c1_lo[:, cols]), (lo[:, 0, 0:P], G.c1_hi[:, cols]),
                                 (hi[:, 1, 0:P], G.c2[:, cols]), (lo[:, 1, 0:P], G.c2[:, cols])]
                    else:
                        hi, lo, cols = w_hi[1], w_lo[1], slice((n - NPJ) * S.QC, (n - NPJ + 1) * S.QC)
                        terms = [(w[:, k, 0:P], xt[:, k, cols]) for w, xt in ((hi, G.xt_hi), (hi, G.xt_lo), (lo, G.xt_hi))
                                 for k in range(KD)]
                    product(ps[4 + n % 4][:, 0:width(n)], terms).then_inc(s_proj, 1)

                pe.wait_ge(s_id, 2)
                pe.wait_ge(s_c, 64)
                for j, (src, tiles, k) in enumerate(tjobs):
                    if j == len(ct):
                        pe.wait_ge(s_lo, len(ct))
                        pe.wait_ge(s_whi, 1)
                        pe.wait_ge(s_wlo, 1)
                        for n in range(NPJ):
                            proj(n)
                    if j >= 4:
                        pe.wait_ge(s_lo, j - 3)
                    if src == "x":
                        pe.wait_ge(s_xn, tiles[-1] + 1)
                    buf = x_in if src == "x" else c_in
                    for i, t in enumerate(tiles):
                        last = pe.transpose(ps[j % 4][:, i * P:(i + 1) * P], buf[:, t, k * P:(k + 1) * P], ident[:])
                    last.then_inc(s_ps, 1)
                pe.wait_ge(s_lo, NTJ)
                pe.wait_ge(s_whi, 2)
                pe.wait_ge(s_wlo, 2)
                for n in range(NPJ, 2 * NPJ):
                    proj(n)
                pe.wait_ge(s_whi, 3)
                pe.wait_ge(s_wlo, 3)
                for j, (kt, half) in enumerate(vjobs):
                    if j < 4:
                        pe.wait_ge(s_stlo, NPJ + j + 1)
                    else:
                        pe.wait_ge(s_vev[half], kt - 1)
                    keys = slice(kt * P, (kt + 1) * P)
                    cols = slice(half * 512, half * 512 + 512)
                    product(ps[4 + j % 4][:], [(c[:, keys], w[:, k, cols]) for c, w, k in (
                        (G.c1_hi, w_hi[2], 0), (G.c1_lo, w_hi[2], 0), (G.c1_hi, w_lo[2], 0), (G.c2, w_hi[2], 1),
                        (G.c2, w_lo[2], 1))]).then_inc(s_v, 1)
                    for r in rough_after(j):
                        if r == 0:
                            pe.wait_ge(s_head, 96)
                        if r >= 2:
                            pe.wait_ge(G.rough_used, r - 1)
                        rough_scores(S, G, pe, ps[r % 2], 0, 0, r)


UNITS = 4
LAG = 2
RING = 4
DVE_TILES = (1, 3, 8, 12)
POOL_TILES = (0, 2, 4, 5, 6, 7, 9, 10, 11)
PROJ_SLOTS = (4, 6, 8, 10)
DEN_SLOT, MROW_SLOT = 3, 11
REC_SLOT, NORM_SLOT = 7, 12
MAHEAD = 3
PLACES = 3
PROJ_JOBS = 2 * len(PROJ_SLOTS)


def wait_for(eng, s, count):
    if not (isinstance(count, int) and count <= 0):
        eng.wait_ge(s, count)


def tile_summed(t):
    tiles = DVE_TILES if t in DVE_TILES else POOL_TILES
    return t in DVE_TILES, max(tiles.index(t), 1)


def phase_attention(nc, S, A, G, sem):
    KT, DH, NP, UQ, QC, KC, MC = S.KT, S.DH, S.NP, S.UQ, S.QC, S.KC, S.MC
    HP = P // 2
    SLOTS = UNITS * KT
    SCALE = float(DH) ** -0.5
    NMU = UQ // P
    ND, NPL = len(DVE_TILES) - 1, len(POOL_TILES) - 1
    assert SLOTS % RING == 0
    with ExitStack() as ctx:
        def sb(name, shape, dt=F32):
            return ctx.enter_context(nc.sbuf_tensor(name, shape, dt))

        wq_s = sb("wq_s", [P, 4, P], F32R)
        wk_s = sb("wk_s", [P, 4, P], F32R)
        st_hi = sb("st_hi", [P, 2, QC], F32R)
        st_lo = sb("st_lo", [P, 2, QC], F32R)
        probs = sb("probs", [P, RING, UQ])
        acc_d = sb("acc_d", [P, UQ])
        acc_p = sb("acc_p", [P, 2, UQ])
        den_sb = sb("den_sb", [P, QC])
        den_c = sb("den_c", [16, 2 * QC // 16])
        rec_c = sb("rec_c", [16, 2 * QC // 16])
        mx = sb("mx", [P, NMU])
        m_row = sb("m_row", [NMU, P], F32R)
        o_sb = sb("o_sb", [P, QC])
        rec = sb("rec", [P, QC])
        o_n = sb("o_n", [P, 2, QC])
        vh = [sb(f"vh{b}", [P, KT, DH]) for b in range(2)]
        G.k1.append(sb("k1_1", [P, S.NKP], F32R))
        G.q1.append(sb("q1_1", [P, S.NT], F32R))
        k1, q1 = G.k1, G.q1
        k2, q2 = G.k2, G.q2
        ps_s = ctx.enter_context(nc.psum_tensor("ps_s", [P, 2, 2 * QC], F32))
        ps_m = ctx.enter_context(nc.psum_tensor("ps_m", [P, 2, QC], F32))
        ps_o = ctx.enter_context(nc.psum_tensor("ps_o", [P, QC], F32))
        ps_x = ctx.enter_context(nc.psum_tensor("ps_x", [P, QC], F32))

        w_loaded = sem("w_loaded")
        qk_loaded = [sem(f"qk_loaded{b}") for b in range(2)]
        v_loaded = [sem(f"v_loaded{b}") for b in range(2)]
        stage_stored = [sem(f"stage_stored{b}") for b in range(2)]
        mrow_placed = sem("mrow_placed")
        o_stored = [sem(f"o_stored{b}") for b in range(2)]
        den_moved, rec_stored, rec_placed = sem("den_moved"), sem("rec_stored"), sem("rec_placed")
        scores_ready, exp_done, pv_done = sem("scores_ready"), sem("exp_done"), sem("pv_done")
        rough_ready, rough_used = G.rough_ready, G.rough_used
        max_ready, maxt_ready, mrow_ready = (sem(n) for n in ("max_ready", "maxt_ready", "mrow_ready"))
        proj_ready, stage_hi, stage_lo = sem("proj_ready"), sem("stage_hi"), sem("stage_lo")
        summed_dve, summed_pool = sem("summed_dve"), sem("summed_pool")
        joined = sem("joined")
        den_ready, den_copied, rec_ready, o_copied, o_ready = sem("den_ready"), sem("den_copied"), sem("rec_ready"), sem("o_copied"), sem("o_ready")

        def rough_places():
            return [(j, j * KT * PLACES // MJOBS) for j in range(MJOBS)]

        def rough_jobs(u, s, last):
            ahead = 1 if s < KT - MAHEAD else 2
            place = (s + MAHEAD) % KT
            if last and u + ahead >= UNITS:
                return []
            return [(j, ahead, at % PLACES) for j, at in rough_places() if at // PLACES == place]

        def x_wait(pe, p, u, s, last):
            unit = UNITS * p + u
            if s == DEN_SLOT:
                pe.wait_ge(mrow_ready, unit + 1)
            elif s in PROJ_SLOTS and s != PROJ_SLOTS[0]:
                pe.wait_ge(stage_lo, PROJ_JOBS * p + u * len(PROJ_SLOTS) + PROJ_SLOTS.index(s))
            elif s == MROW_SLOT and u < 2 and not last:
                pe.wait_ge(stage_lo, PROJ_JOBS * p + (u + 1) * len(PROJ_SLOTS))
            else:
                wait_for(pe, den_copied, unit)

        def pe_rough(pe, hd, half, j, count):
            wait_for(pe, rough_used, count - 1)
            rough_scores(S, G, pe, ps_m[:, j % 2, :], hd, half, j)

        def dve_rough(dve, j, unit, count):
            if j == 0:
                wait_for(dve, max_ready, unit)
            dve.wait_ge(rough_ready, count + 1)
            rough_max(S, G, dve, ps_m[:, j % 2, :], j)

        def dve_max(dve, unit):
            dve.wait_ge(rough_used, (unit + 1) * MJOBS)
            wait_for(dve, maxt_ready, unit)
            dve.tensor_reduce(mx[:], G.mx_part[:], AX.X, ALU.max).then_inc(max_ready, 1)

        def pe_maxt(pe, unit):
            pe.wait_ge(max_ready, unit + 1)
            pe.transpose(ps_x[0:NMU, 0:P], mx[:], G.ident[:]).then_inc(maxt_ready, 1)

        def act_mrow(act, unit):
            act.wait_ge(maxt_ready, unit + 1)
            wait_for(act, mrow_placed, 16 * unit)
            act.activation(m_row[:], ps_x[0:NMU, 0:P], ACT.Copy, scale=-1.0).then_inc(mrow_ready, 1)

        def sp_mrow(sp, unit, hd, half):
            sp.wait_ge(mrow_ready, unit + 1)
            sp.dma_start(raw(q2[hd][HP:HP + 1, half * UQ:(half + 1) * UQ]), raw(m_row[:])).then_inc(mrow_placed, 16)

        def block_of(n):
            return n % 2 == 0, n // 2

        def pe_proj(pe, n, pair):
            is_q, c = block_of(n)
            if n == 0:
                pe.wait_ge(w_loaded, 32 * pair)
            if is_q:
                cols = slice(c * QC, (c + 1) * QC)
                terms = [(wq_s[:, 2 * part + k, :], xt[:, k, cols])
                         for part, xt in ((0, G.xt_hi), (0, G.xt_lo), (1, G.xt_hi)) for k in range(S.KD)]
            else:
                cols = slice(c * KC, (c + 1) * KC)
                terms = [(wk_s[:, 0, :], G.c1_hi[:, cols]), (wk_s[:, 0, :], G.c1_lo[:, cols]),
                         (wk_s[:, 2, :], G.c1_hi[:, cols]), (wk_s[:, 1, :], G.c2[:, cols]), (wk_s[:, 3, :], G.c2[:, cols])]
            for i, (w, m) in enumerate(terms):
                last = pe.matmul(ps_x[:, 0:QC if is_q else KC], w, m, start=(i == 0), stop=(i == len(terms) - 1))
            last.then_inc(proj_ready, 1)

        def act_proj(act, n, count):
            w = QC if block_of(n)[0] else KC
            act.wait_ge(proj_ready, count + 1)
            wait_for(act, stage_stored[n % 2], 16 * (count - n % 2))
            act.activation(st_hi[:, n % 2, 0:w], ps_x[:, 0:w], ACT.Copy).then_inc(stage_hi, 1)

        def dve_proj(dve, n, count):
            w = QC if block_of(n)[0] else KC
            dve.wait_ge(stage_hi, count + 1)
            dve.tensor_tensor(st_lo[:, n % 2, 0:w], ps_x[:, 0:w], raw(st_hi[:, n % 2, 0:w]), ALU.subtract).then_inc(stage_lo, 1)

        def sp_proj(sp, n, pair, count):
            is_q, c = block_of(n)
            sp.wait_ge(stage_lo, count + 1)
            scr, w = (G.q_scr, QC) if is_q else (G.k_scr, KC)
            for part, st in ((0, st_hi), (1, st_lo)):
                sp.dma_start(scr[pair, part, :, c * w:(c + 1) * w], raw(st[:, n % 2, 0:w])).then_inc(stage_stored[n % 2], 16)

        def sp_load_w(sp, pair):
            sp.dma_start(raw(wq_s[:]), G.wq_scr[pair].rearrange("p a k c -> p (a k) c")).then_inc(w_loaded, 16)
            sp.dma_start(raw(wk_s[:]), G.wk_scr[pair].rearrange("p a k c -> p (a k) c")).then_inc(w_loaded, 16)

        def sp_load_head(sp, pair, hd):
            sp.dma_start(vh[hd][:], G.v_scr[2 * pair + hd]).then_inc(v_loaded[hd], 16)
            rows = slice(hd * HP, (hd + 1) * HP)
            if not (isinstance(pair, int) and pair == 0 and hd == 0):
                for n, (dst, scr, part) in enumerate(head_parts(S, G, hd)):
                    if hd == 0 and n % 3 == 0:
                        sp.wait_ge(stage_stored[n // 3], 16 * PROJ_JOBS * pair)
                    sp.dma_start(raw(dst), scr[pair, part, rows, :]).then_inc(qk_loaded[hd], 16)

        def pe_pv(pe, g, slot, unit, pair):
            hd, s = g // (2 * KT), g % KT
            pe.wait_ge(exp_done, slot + 1)
            if s == 0:
                if g % (2 * KT) == 0:
                    pe.wait_ge(v_loaded[hd], 16 * (pair + 1))
                wait_for(pe, o_copied, unit)
            for b in range(2):
                last = pe.matmul(ps_o[b * HP:b * HP + DH, :], vh[hd][:, s, :], probs[:, g % RING, b * QC:(b + 1) * QC],
                                 start=(s == 0), stop=(s == KT - 1))
            last.then_inc(pv_done, 1)

        def pool_join(pool, u, unit):
            pool.wait_ge(summed_dve, (unit + 1) * ND)
            pool.wait_ge(summed_pool, (unit + 1) * NPL)
            pool.tensor_tensor(acc_p[:, u % 2, :], acc_p[:, u % 2, :], acc_d[:], ALU.add).then_inc(joined, 1)

        def pe_den(pe, u, unit):
            pe.wait_ge(joined, unit + 1)
            for b in range(2):
                last = pe.matmul(ps_x[b * HP:(b + 1) * HP, :], G.ones[:, 0:HP], acc_p[:, u % 2, b * QC:(b + 1) * QC],
                                 start=True, stop=True)
            last.then_inc(den_ready, 1)

        def act_o(act, unit):
            act.wait_ge(pv_done, (unit + 1) * KT)
            wait_for(act, o_ready, unit)
            act.activation(o_sb[:], ps_o[:], ACT.Copy).then_inc(o_copied, 1)

        def act_den(act, unit):
            act.wait_ge(den_ready, unit + 1)
            wait_for(act, den_moved, 32 * unit)
            act.activation(den_sb[:], ps_x[:], ACT.Copy).then_inc(den_copied, 1)

        def sp_den(sp, unit):
            sp.wait_ge(den_copied, unit + 1)
            for b in range(2):
                sp.dma_start(den_c[8 * b:8 * b + 8, :], den_sb[b * HP:b * HP + 1, :]).then_inc(den_moved, 16)

        def dve_rec(dve, unit):
            dve.wait_ge(den_moved, 32 * (unit + 1))
            dve.reciprocal(rec_c[:], den_c[:]).then_inc(rec_ready, 1)

        def sp_rec(sp, unit):
            sp.wait_ge(rec_ready, unit + 1)
            sp.dma_start(G.rec_scr.rearrange("b (r c) -> (b r) c", r=8), rec_c[:]).then_inc(rec_stored, 16)
            sp.wait_ge(rec_stored, 16 * (unit + 1))
            for b in range(2):
                sp.dma_start(rec[b * HP:(b + 1) * HP, :], G.rec_scr[b:b + 1, :].to_broadcast([HP, QC])).then_inc(rec_placed, 16)

        def dve_norm(dve, unit, u):
            dve.wait_ge(rec_placed, 32 * (unit + 1))
            dve.wait_ge(o_copied, unit + 1)
            wait_for(dve, o_stored[u % 2], 16 * (unit - u % 2))
            dve.tensor_tensor(o_n[:, u % 2, :], o_sb[:], rec[:], ALU.mult).then_inc(o_ready, 1)

        def sp_store_o(sp, unit, pair, u):
            hd, q0 = u // 2, (u % 2) * UQ
            sp.wait_ge(o_ready, unit + 1)
            for b in range(2):
                sp.dma_start(G.o_scr[pair, hd * HP:(hd + 1) * HP, q0 + b * QC:q0 + (b + 1) * QC],
                             o_n[b * HP:(b + 1) * HP, u % 2, :]).then_inc(o_stored[u % 2], 16)

        def add_tile(eng, k, u, unit, slot, dve=False):
            tiles, done = (DVE_TILES, summed_dve) if dve else (POOL_TILES, summed_pool)
            acc = acc_d[:] if dve else acc_p[:, u % 2, :]
            t = tiles[k + 1]
            eng.wait_ge(exp_done, slot + t + 1)
            if k == 0:
                if dve:
                    wait_for(eng, joined, unit)
                else:
                    wait_for(eng, den_ready, unit - 1)
                other = probs[:, (u * KT + tiles[0]) % RING, :]
            else:
                eng.wait_ge(done, unit * (len(tiles) - 1) + k)
                other = acc
            eng.tensor_tensor(acc, other, probs[:, (u * KT + t) % RING, :], ALU.add).then_inc(done, 1)

        def pe_pair(pe, p, first=False, last=False):
            for g in range(SLOTS):
                u, s = divmod(g, KT)
                hd, half = divmod(u, 2)
                unit, slot = p * UNITS + u, p * SLOTS + g
                jobs = rough_jobs(u, s, last)

                def rough(place):
                    for j, ahead, at in jobs:
                        if at != place:
                            continue
                        nu = (u + ahead) % UNITS
                        if j == 0 and nu % 2 == 0:
                            pe.wait_ge(qk_loaded[nu // 2], 96 * (p + (u + ahead) // UNITS + (nu // 2)))
                        pe_rough(pe, *divmod(nu, 2), j, (unit + ahead) * MJOBS + j)

                rough(0)
                if s == 0:
                    pe.wait_ge(mrow_placed, 16 * (unit + 1))
                if not (first and g < 2):
                    pe.wait_ge(exp_done, slot - 1)
                keys = slice(s * P, (s + 1) * P)
                for b in range(2):
                    qs = slice(half * UQ + b * QC, half * UQ + (b + 1) * QC)
                    out = ps_s[:, g % 2, b * QC:(b + 1) * QC]
                    pe.matmul(out, k1[hd][:, keys], q1[hd][:, qs], start=True, stop=False)
                    mm = pe.matmul(out, k2[hd][:, keys], q2[hd][:, qs], start=False, stop=True)
                    if b:
                        mm.then_inc(scores_ready, 1)
                    rough(b + 1)
                if not (first and g < LAG):
                    pe_pv(pe, (g - LAG) % SLOTS, slot - LAG, p * UNITS + (g - LAG) // KT, p if g >= LAG else p - 1)
                if s == DEN_SLOT and not (first and u == 0):
                    x_wait(pe, p, u, s, last)
                    pe_den(pe, (u - 1) % UNITS, unit - 1)
                if s in PROJ_SLOTS and u < 2 and not last:
                    x_wait(pe, p, u, s, last)
                    pe_proj(pe, u * len(PROJ_SLOTS) + PROJ_SLOTS.index(s), p + 1)
                if s == MROW_SLOT and not (last and u == UNITS - 1):
                    x_wait(pe, p, u, s, last)
                    pe_maxt(pe, unit + 1)

        def act_pair(act, p, first=False, last=False):
            for g in range(SLOTS):
                u, s = divmod(g, KT)
                unit, slot = p * UNITS + u, p * SLOTS + g
                if not (first and g < RING):
                    act.wait_ge(pv_done, slot - RING + 1)
                    by_dve, n = tile_summed((g - RING) % KT)
                    then = p * UNITS + (g - RING) // KT
                    if by_dve:
                        act.wait_ge(summed_dve, then * ND + n)
                    else:
                        act.wait_ge(summed_pool, then * NPL + n)
                act.wait_ge(scores_ready, slot + 1)
                act.activation(probs[:, g % RING, :], ps_s[:, g % 2, :], ACT.Exp,
                               bias=G.pad_bias[:, 0:1] if s == KT - 1 else 0.0, scale=SCALE).then_inc(exp_done, 1)
                if s == LAG - 1 and not (first and u == 0):
                    act_o(act, unit - 1)
                if s == DEN_SLOT and not (first and u == 0):
                    act_den(act, unit - 1)
                if s in PROJ_SLOTS and u < 2 and not last:
                    n = u * len(PROJ_SLOTS) + PROJ_SLOTS.index(s)
                    act_proj(act, n, PROJ_JOBS * p + n)
                if s == MROW_SLOT and not (last and u == UNITS - 1):
                    act_mrow(act, unit + 1)

        def dve_pair(dve, p, first=False, last=False):
            for g in range(SLOTS):
                u, s = divmod(g, KT)
                unit, slot = p * UNITS + u, p * SLOTS + g
                jobs = rough_jobs(u, s, last)
                if s == KT - MAHEAD and not (last and u == UNITS - 1):
                    dve_max(dve, unit + 1)

                def rough(*places):
                    for j, ahead, at in jobs:
                        if at in places:
                            dve_rough(dve, j, unit + ahead, (unit + ahead) * MJOBS + j)

                rough(0)
                if s == 0 and not (first and u == 0):
                    add_tile(dve, ND - 1, (u - 1) % UNITS, unit - 1, slot - KT, dve=True)
                if s - 1 in DVE_TILES[1:]:
                    add_tile(dve, DVE_TILES.index(s - 1) - 1, u, unit, slot - s, dve=True)
                if s - 1 in PROJ_SLOTS and u < 2 and not last:
                    n = u * len(PROJ_SLOTS) + PROJ_SLOTS.index(s - 1)
                    dve_proj(dve, n, PROJ_JOBS * p + n)
                rough(1, 2)
                if s == REC_SLOT and not (first and u == 0):
                    dve_rec(dve, unit - 1)
                if s == NORM_SLOT and not (first and u == 0):
                    dve_norm(dve, unit - 1, (u - 1) % UNITS)

        def pool_pair(pool, p, first=False):
            for u in range(UNITS):
                if not (first and u == 0):
                    pool_join(pool, (u - 1) % UNITS, p * UNITS + u - 1)
                for k in range(NPL):
                    add_tile(pool, k, u, p * UNITS + u, p * SLOTS + u * KT)

        def sp_pair(sp, p, first=False, last=False):
            if not last:
                wait_for(sp, proj_ready, PROJ_JOBS * p)
                sp_load_w(sp, p + 1)
            if not first:
                sp.wait_ge(pv_done, p * SLOTS)
                sp_load_head(sp, p, 1)
            for u in range(UNITS):
                unit = p * UNITS + u
                if u == 2 and not last:
                    sp.wait_ge(pv_done, p * SLOTS + 2 * KT)
                    sp_load_head(sp, p + 1, 0)
                blocks = range(u * len(PROJ_SLOTS), (u + 1) * len(PROJ_SLOTS)) if u < 2 and not last else []
                if not (first and u == 0):
                    sp_den(sp, unit - 1)
                for n in blocks[:1]:
                    sp_proj(sp, n, p + 1, PROJ_JOBS * p + n)
                if not (first and u == 0):
                    sp_rec(sp, unit - 1)
                for n in blocks[1:]:
                    sp_proj(sp, n, p + 1, PROJ_JOBS * p + n)
                if not (last and u == UNITS - 1):
                    sp_mrow(sp, unit + 1, *divmod((u + 1) % UNITS, 2))
                if not (first and u == 0):
                    sp_store_o(sp, unit - 1, p if u else p - 1, (u - 1) % UNITS)

        with nc.Block() as block:

            @block.sync
            def _(sp):
                sp_load_head(sp, 0, 0)
                sp_load_head(sp, 0, 1)
                sp_mrow(sp, 0, 0, 0)
                sp_pair(sp, 0, first=True)
                with sp.Fori(1, NP - 1) as p:
                    sp_pair(sp, p)
                sp_pair(sp, NP - 1, last=True)
                sp_den(sp, NP * UNITS - 1)
                sp_rec(sp, NP * UNITS - 1)
                sp_store_o(sp, NP * UNITS - 1, NP - 1, UNITS - 1)
                for b in range(2):
                    sp.wait_ge(o_stored[b], 16 * NP * UNITS)

            @block.tensor
            def _(pe):
                pe_maxt(pe, 0)
                for j, ahead in [(j, 1) for j, at in rough_places() if at // PLACES < MAHEAD]:
                    pe_rough(pe, 0, 1, j, MJOBS + j)
                pe_pair(pe, 0, first=True)
                with pe.Fori(1, NP - 1) as p:
                    pe_pair(pe, p)
                pe_pair(pe, NP - 1, last=True)
                for g in range(SLOTS - LAG, SLOTS):
                    pe_pv(pe, g, (NP - 1) * SLOTS + g, NP * UNITS - 1, NP - 1)
                pe.wait_ge(den_copied, NP * UNITS - 1)
                pe_den(pe, UNITS - 1, NP * UNITS - 1)

            @block.scalar
            def _(act):
                act_mrow(act, 0)
                act_pair(act, 0, first=True)
                with act.Fori(1, NP - 1) as p:
                    act_pair(act, p)
                act_pair(act, NP - 1, last=True)
                act_o(act, NP * UNITS - 1)
                act_den(act, NP * UNITS - 1)

            @block.vector
            def _(dve):
                dve_max(dve, 0)
                for j, ahead in [(j, 1) for j, at in rough_places() if at // PLACES < MAHEAD]:
                    dve_rough(dve, j, 1, MJOBS + j)
                dve_pair(dve, 0, first=True)
                with dve.Fori(1, NP - 1) as p:
                    dve_pair(dve, p)
                dve_pair(dve, NP - 1, last=True)
                add_tile(dve, ND - 1, UNITS - 1, NP * UNITS - 1, NP * SLOTS - KT, dve=True)
                dve_rec(dve, NP * UNITS - 1)
                dve_norm(dve, NP * UNITS - 1, UNITS - 1)

            @block.gpsimd
            def _(pool):
                pool_pair(pool, 0, first=True)
                with pool.Fori(1, NP) as p:
                    pool_pair(pool, p)
                pool_join(pool, UNITS - 1, NP * UNITS - 1)


def phase_output(nc, S, A, G, sem, out):
    TT, D, E, NP, QC = S.TT, S.D, S.E, S.NP, S.QC
    BT = QC // P
    NB = TT // BT
    HN = NP // 2
    with ExitStack() as ctx:
        def sb(name, shape, dt=F32):
            return ctx.enter_context(nc.sbuf_tensor(name, shape, dt))

        wo_in = sb("wo_in", [P, NP, D])
        wo_hi, wo_lo = sb("wo_hi_", [P, NP, D], F32R), sb("wo_lo_", [P, NP, D], F32R)
        bo_sb = sb("bo_sb", [P, D])
        ot = [sb(f"ot{b}", [P, NP, QC]) for b in range(2)]
        ot_hi = [sb(f"ot_hi{b}", [P, NP, QC], F32R) for b in range(2)]
        ot_lo = sb("ot_lo", [P, NP, QC], F32R)
        x1 = sb("x1", [P, TT, D])
        xn = sb("xn2", [P, TT, D + E])
        xn_t = sb("xn_t", [P, S.KD, QC])
        rw_in = sb("rw_in", [E, D])
        rw_t = sb("rw_t", [P, S.KD, E])
        b1_in = sb("b1_in", [E * S.HT, P])
        stats, mv = sb("ln2_stats", [P, TT, 6]), sb("ln2_mv", [P, TT, 2])
        std, rstd, nt, eps = sb("ln2_std", [P, TT]), sb("ln2_rstd", [P, TT]), sb("ln2_nt", [P, TT]), sb("ln2_eps", [P, 1])
        lg = sb("lg", [P, TT, E])
        lmax, lsum, lrec = sb("lmax", [P, TT]), sb("lsum", [P, TT]), sb("lrec", [P, TT])
        ps_y = ctx.enter_context(nc.psum_tensor("ps_out", [P, 2, QC], F32))
        ps_t = ctx.enter_context(nc.psum_tensor("ps_out_t", [P, 2, QC], F32))
        ps_l = ctx.enter_context(nc.psum_tensor("ps_logits", [P, TT, E], F32))
        ps_r = ctx.enter_context(nc.psum_tensor("ps_small", [P, QC], F32))

        wo_loaded, bo_loaded, small_loaded = sem("wo_loaded"), sem("bo_loaded"), sem("small_loaded")
        x_loaded = [sem(f"x_loaded{b}") for b in range(NB)]
        ot_loaded = [sem(f"ot_loaded{b}") for b in range(2)]
        wo_hi_done, wo_lo_done = sem("wo_hi_done"), sem("wo_lo_done")
        ot_hi_done, ot_lo_dve, ot_lo_pool = sem("ot_hi_done"), sem("ot_lo_dve"), sem("ot_lo_pool")
        biased, eps_set = sem("biased"), sem("eps_set")
        y_ready, x1_done = sem("y_ready"), sem("x1_done")
        stats_done, mv_done, std_done, rstd_done, xn_done = (sem(f"ln2_{n}_done") for n in ("stats", "mv", "std", "rstd", "xn"))
        small_t, small_copied = sem("small_t"), sem("small_copied")
        t_ready, t_copied, logits_ready = sem("xn_t_ready"), sem("xn_t_copied"), sem("logits_ready")
        softmax, exp_l = sem("softmax_steps"), sem("logits_exp")
        x1_stored, table_stored = sem("x1_stored"), sem("table_stored")

        xv = A["x"][0].rearrange("(t p) d -> p t d", p=P)
        ov = out[0].rearrange("(t p) d -> p t d", p=P)

        with nc.Block() as block:

            @block.sync
            def _(sp):
                def load_ot(b):
                    sp.dma_start(ot[b % 2][:], G.o_scr[:, :, b * QC:(b + 1) * QC].rearrange("h p q -> p h q")).then_inc(ot_loaded[b % 2], 16)

                sp.dma_start(wo_in[:], A["wo"].rearrange("(h p) n -> p h n", p=P)).then_inc(wo_loaded, 16)
                load_ot(0)
                load_ot(1)
                sp.dma_start(rw_in[:], A["router_w"]).then_inc(small_loaded, 16)
                sp.dma_start(b1_in[:], A["b1"].rearrange("e (h p) -> (e h) p", p=P)).then_inc(small_loaded, 16)
                sp.dma_start(bo_sb[:], A["bo"].rearrange("(o n) -> o n", o=1).to_broadcast([P, D])).then_inc(bo_loaded, 16)
                for b in range(NB):
                    sp.dma_start(x1[:, b * BT:(b + 1) * BT, :], xv[:, b * BT:(b + 1) * BT, :]).then_inc(x_loaded[b], 16)
                for b in range(2, NB):
                    sp.wait_ge(ot_hi_done, b - 1)
                    sp.wait_ge(ot_lo_dve, b - 1)
                    sp.wait_ge(ot_lo_pool, b - 1)
                    load_ot(b)
                for b in range(NB):
                    sp.wait_ge(x1_done, (b + 1) * BT)
                    sp.dma_start(ov[:, b * BT:(b + 1) * BT, :], x1[:, b * BT:(b + 1) * BT, :]).then_inc(x1_stored, 16)
                sp.wait_ge(xn_done, TT)
                sp.wait_ge(softmax, 5)
                sp.dma_start(G.table.rearrange("(t p) d -> p t d", p=P), xn[:]).then_inc(table_stored, 16)
                sp.wait_ge(x1_stored, 16 * NB)
                sp.wait_ge(table_stored, 16)

            @block.gpsimd
            def _(pool):
                def bias(b):
                    pool.wait_ge(x_loaded[b], 16)
                    pool.tensor_tensor(x1[:, b * BT:(b + 1) * BT, :], x1[:, b * BT:(b + 1) * BT, :],
                                       bo_sb[:, None, :].to_broadcast([P, BT, D]), ALU.add).then_inc(biased, 1)

                def lo(b):
                    pool.wait_ge(ot_hi_done, b + 1)
                    if b >= 1:
                        pool.wait_ge(y_ready, b * BT)
                    pool.tensor_tensor(ot_lo[:, HN:NP, :], ot[b % 2][:, HN:NP, :], raw(ot_hi[b % 2][:, HN:NP, :]),
                                       ALU.subtract).then_inc(ot_lo_pool, 1)

                lo(0)
                pool.wait_ge(bo_loaded, 16)
                bias(0)
                for b in range(1, NB):
                    lo(b)
                    bias(b)

            @block.scalar
            def _(act):
                def hi(b):
                    act.wait_ge(ot_loaded[b % 2], 16 * (b // 2 + 1))
                    if b >= 2:
                        act.wait_ge(y_ready, (b - 1) * BT)
                    act.activation(ot_hi[b % 2][:], ot[b % 2][:], ACT.Copy).then_inc(ot_hi_done, 1)

                act.wait_ge(wo_loaded, 16)
                act.activation(wo_hi[:], wo_in[:], ACT.Copy).then_inc(wo_hi_done, 1)
                hi(0)
                hi(1)
                act.wait_ge(small_t, 1)
                act.activation(rw_t[:].rearrange("p k e -> p (k e)"), ps_r[:, 0:S.KD * E], ACT.Copy).then_inc(small_copied, 1)
                act.activation(G.b1_t[:], ps_r[:, S.KD * E:S.KD * E + E * S.HT], ACT.Copy).then_inc(small_copied, 1)
                act.wait_ge(eps_set, 1)
                for b in range(NB):
                    if b + 2 < NB:
                        hi(b + 2)
                    act.wait_ge(mv_done, (b + 1) * BT)
                    act.activation(std[:, b * BT:(b + 1) * BT], mv[:, b * BT:(b + 1) * BT, 1], ACT.Sqrt,
                                   bias=eps[:, 0:1]).then_inc(std_done, 1)
                    act.wait_ge(t_ready, b + 1)
                    if b >= 1:
                        act.wait_ge(logits_ready, b)
                    act.activation(xn_t[:], ps_t[:], ACT.Copy).then_inc(t_copied, 1)
                act.wait_ge(softmax, 2)
                act.activation(lg[:], lg[:], ACT.Exp).then_inc(exp_l, 1)

            @block.vector
            def _(dve):
                def lo(b):
                    dve.wait_ge(ot_hi_done, b + 1)
                    if b >= 1:
                        dve.wait_ge(y_ready, b * BT)
                    dve.tensor_tensor(ot_lo[:, 0:HN, :], ot[b % 2][:, 0:HN, :], raw(ot_hi[b % 2][:, 0:HN, :]),
                                      ALU.subtract).then_inc(ot_lo_dve, 1)

                dve.memset(eps[:], EPS).then_inc(eps_set, 1)
                dve.wait_ge(wo_loaded, 16)
                dve.wait_ge(wo_hi_done, 1)
                dve.tensor_tensor(wo_lo[:], wo_in[:], raw(wo_hi[:]), ALU.subtract).then_inc(wo_lo_done, 1)
                lo(0)
                for b in range(NB):
                    dve.wait_ge(biased, b + 1)
                    for t in range(b * BT, (b + 1) * BT):
                        dve.wait_ge(y_ready, t + 1)
                        dve.tensor_tensor(x1[:, t, :], ps_y[:, t % 2, 0:D], x1[:, t, :], ALU.add).then_inc(x1_done, 1)
                        if t == (b + 1) * BT - 1 and b + 1 < NB:
                            lo(b + 1)
                        dve.wait_ge(x1_done, t + 1)
                        dve.bn_stats(stats[:, t, :], x1[:, t, :]).then_inc(stats_done, 1)
                        dve.wait_ge(stats_done, t + 1)
                        dve.bn_aggr(mv[:, t, :], stats[:, t, :]).then_inc(mv_done, 1)
                    g = slice(b * BT, (b + 1) * BT)
                    dve.wait_ge(std_done, b + 1)
                    dve.reciprocal(rstd[:, g], std[:, g]).then_inc(rstd_done, 1)
                    dve.wait_ge(rstd_done, 5 * b + 1)
                    refine_rstd(dve, mv[:, g, 1], rstd[:, g], nt[:, g], rstd_done, 5 * b + 1)
                    for t in range(b * BT, (b + 1) * BT):
                        dve.tensor_scalar(xn[:, t, 0:D], x1[:, t, :], mv[:, t, 0:1], rstd[:, t:t + 1],
                                          ALU.subtract, ALU.mult).then_inc(xn_done, 1)
                dve.wait_ge(logits_ready, NB)
                dve.tensor_reduce(lmax[:], ps_l[:], AX.X, ALU.max).then_inc(softmax, 1)
                dve.wait_ge(softmax, 1)
                dve.tensor_tensor(lg[:], ps_l[:], lmax[:, :, None].to_broadcast([P, TT, E]), ALU.subtract).then_inc(softmax, 1)
                dve.wait_ge(exp_l, 1)
                dve.tensor_reduce(lsum[:], lg[:], AX.X, ALU.add).then_inc(softmax, 1)
                dve.wait_ge(softmax, 3)
                dve.reciprocal(lrec[:], lsum[:]).then_inc(softmax, 1)
                dve.wait_ge(softmax, 4)
                dve.tensor_tensor(xn[:, :, D:D + E], lg[:], lrec[:, :, None].to_broadcast([P, TT, E]), ALU.mult).then_inc(softmax, 1)
                dve.tensor_tensor(G.scores[:], lg[:].rearrange("p t e -> p e t"), lrec[:, None, :].to_broadcast([P, E, TT]),
                                  ALU.mult).then_inc(softmax, 1)

            @block.tensor
            def _(pe):
                def transposes(b):
                    pe.wait_ge(xn_done, (b + 1) * BT)
                    if b >= 1:
                        pe.wait_ge(t_copied, b)
                    for k in range(S.KD):
                        for i in range(BT):
                            last = pe.transpose(ps_t[:, k, i * P:(i + 1) * P], xn[:, b * BT + i, k * P:(k + 1) * P], G.ident[:])
                    last.then_inc(t_ready, 1)

                def logits(b):
                    pe.wait_ge(t_copied, b + 1)
                    for i in range(BT):
                        for k in range(S.KD):
                            last = pe.matmul(ps_l[:, b * BT + i, :], xn_t[:, k, i * P:(i + 1) * P], rw_t[:, k, :],
                                             start=(k == 0), stop=(k == S.KD - 1))
                    last.then_inc(logits_ready, 1)

                pe.wait_ge(small_loaded, 32)
                for k in range(S.KD):
                    pe.transpose(ps_r[:, k * E:(k + 1) * E], rw_in[:, k * P:(k + 1) * P], G.ident[0:E, 0:E])
                pe.transpose(ps_r[:, S.KD * E:S.KD * E + E * S.HT], b1_in[:], G.ident[0:E * S.HT, 0:E * S.HT]).then_inc(small_t, 1)
                pe.wait_ge(small_copied, 2)
                pe.wait_ge(wo_lo_done, 1)
                for b in range(NB):
                    pe.wait_ge(ot_hi_done, b + 1)
                    pe.wait_ge(ot_lo_dve, b + 1)
                    pe.wait_ge(ot_lo_pool, b + 1)
                    for i in range(BT):
                        t = b * BT + i
                        if t >= 2:
                            pe.wait_ge(x1_done, t - 1)
                        cols = slice(i * P, (i + 1) * P)
                        n = 0
                        for h in range(NP):
                            for o, w in ((ot_hi[b % 2], wo_hi), (ot_hi[b % 2], wo_lo), (ot_lo, wo_hi)):
                                last = pe.matmul(ps_y[:, t % 2, 0:D], o[:, h, cols], w[:, h, :], start=(n == 0), stop=(n == 3 * NP - 1))
                                n += 1
                        last.then_inc(y_ready, 1)
                        if i == 1 and b >= 1:
                            transposes(b - 1)
                        if i == 2 and b >= 1:
                            logits(b - 1)
                transposes(NB - 1)
                logits(NB - 1)


RT = 104
SEARCH_BITS = 30


def phase_experts(nc, S, A, G, sem, out):
    TT, D, E, HT, KD, CAP = S.TT, S.D, S.E, S.HT, S.KD, S.CAP
    ST = -(-CAP // RT)
    TAIL = CAP - (ST - 1) * RT
    NS = CAP + 3 - (CAP + 3) % 4
    HS = NS // 2
    ROUNDS = SEARCH_BITS // 2
    TJ = 3
    assert E * TT == P and TAIL % 2 == 1 and NS <= ST * RT and HS % 2 == 0
    rows = [RT] * (ST - 1) + [TAIL]
    with ExitStack() as ctx:
        def sb(name, shape, dt=F32):
            return ctx.enter_context(nc.sbuf_tensor(name, shape, dt))

        def ps(name, shape):
            return ctx.enter_context(nc.psum_tensor(name, shape, F32))

        cand = [sb(f"cand{i}", [P, E, 4], I32) for i in range(2)]
        step = sb("step", [P, 3], I32)
        above = sb("above", [P, E, 3, TT], BF16)
        part = sb("part", [P, E, 3], BF16)
        ones_b = sb("ones_b", [P, P], BF16)
        before = sb("before", [P, P], BF16)
        mask = sb("mask", [P, 2, E, TT], BF16)
        cnt = sb("cnt", [P, E], BF16)
        need = sb("need", [P, E])
        tie, sel, pos = sb("tie", [P, E, TT]), sb("sel", [P, E, TT]), sb("pos", [P, E, TT])
        tile_no, slot = sb("tile_no", [P, E, TT]), sb("slot", [P, E, TT])
        iota_i = sb("iota_i", [P, P], I32)
        iota_r = sb("iota_r", [P, RT])
        iota_p = sb("iota_p", [P, 1])
        tile_hot = sb("tile_hot", [P, E, TT, ST])
        ids = sb("ids", [P, E, TT, 2, ST], BF16)
        row_hot = [sb(f"row_hot{b}", [P, TT, RT], BF16) for b in range(2)]
        idx_g = [sb(f"idx_g{b}", [RT, ST], I32) for b in range(2)]
        idx_s = [sb(f"idx_s{b}", [RT, ST], I32) for b in range(2)]
        w1_in = [sb(f"w1_in{b}", [P, KD, S.HID]) for b in range(2)]
        w2_in = [sb(f"w2_in{b}", [P, HT, D]) for b in range(2)]
        w1_hi = [sb(f"w1_hi{b}", [P, KD, S.HID], F32R) for b in range(2)]
        w1_lo = [sb(f"w1_lo{b}", [P, KD, S.HID], F32R) for b in range(2)]
        w2_hi = [sb(f"w2_hi{b}", [P, HT, D], F32R) for b in range(2)]
        w2_lo = [sb(f"w2_lo{b}", [P, HT, D], F32R) for b in range(2)]
        b2_sb = sb("b2_sb", [RT, E, D])
        xg = [sb(f"xg{b}", [RT, ST, D + E]) for b in range(2)]
        xt_hi, xt_lo = sb("xgt_hi", [P, KD, ST * RT], F32R), sb("xgt_lo", [P, KD, ST * RT], F32R)
        h_f = sb("h_f", [P, 2, NS])
        h_hi, h_lo = sb("h_hi", [P, HT, NS], F32R), sb("h_lo", [P, HT, NS], F32R)
        y_sb = [sb(f"y_sb{b}", [RT, ST, D]) for b in range(2)]
        ps_h = ps("ps_h", [P, 2, 2, 512])
        ps_y = ps("ps_y2", [P, 2, 512])
        ps_t = ps("ps_xgt", [P, 2, 512])
        ps_c, ps_pre, ps_i = ps_y, ps_t[:, 0, 0:2 * P], ps_t[:, 1, 0:2 * ST]

        consts, masks_set = sem("consts"), sem("masks_set")
        srch, counted, cand_done = sem("srch"), sem("counted"), sem("parts_ready")
        counts_ready, ranks = sem("counts_ready"), sem("ranks_ready")
        hot_ready, list_ready, idx_ready, idx_kept = sem("hot_ready"), sem("list_ready"), sem("idx_ready"), sem("idx_kept")
        w1_loaded = [sem(f"w1_loaded{b}") for b in range(2)]
        w2_loaded = [sem(f"w2_loaded{b}") for b in range(2)]
        b2_loaded = sem("b2_loaded")
        w1_hi_done, w1_lo_done, w2_hi_done, w2_lo_done = (sem(n) for n in ("w1_hi_done", "w1_lo_done", "w2_hi_done", "w2_lo_done"))
        gathered = [sem(f"gathered{b}") for b in range(2)]
        scattered = [sem(f"scattered{b}") for b in range(2)]
        xgt_ready, xgt_hi_done, xgt_lo_done, padded = sem("xgt_ready"), sem("xgt_hi_done"), sem("xgt_lo_done"), sem("xgt_padded")
        h_ready, gelu_done, h_hi_done, h_lo_done = sem("h_ready"), sem("gelu_done"), sem("h_hi_done"), sem("h_lo_done")
        y_ready, y_read, y_done = sem("y2_ready"), sem("y2_read"), sem("y2_done")

        def sp_weights(sp, e, i, b):
            wait_for(sp, w1_lo_done, e - 1)
            sp.dma_start(w1_in[b][:], w1v(e)).then_inc(w1_loaded[b], 16)
            wait_for(sp, w2_lo_done, e - 1)
            sp.dma_start(w2_in[b][:], w2v(e)).then_inc(w2_loaded[b], 16)

        def w1v(e):
            return (A["w1"][e:e + 1] if isinstance(e, int) else A["w1"][bass.ds(e, 1)]).rearrange("o (k p) n -> p (o k) n", p=P)

        def w2v(e):
            return (A["w2"][e:e + 1] if isinstance(e, int) else A["w2"][bass.ds(e, 1)]).rearrange("o (h p) n -> p (o h) n", p=P)

        def at(e):
            return slice(e, e + 1) if isinstance(e, int) else bass.ds(e, 1)

        def dve_w1_hi(dve, e, i, b):
            dve.wait_ge(w1_loaded[b], 16 * (i + 1))
            wait_for(dve, h_ready, HT * (e - 1))
            dve.tensor_copy(w1_hi[b][:], w1_in[b][:]).then_inc(w1_hi_done, 1)

        def act_w2_hi(act, e, i, b):
            act.wait_ge(w2_loaded[b], 16 * (i + 1))
            wait_for(act, y_ready, ST * (e - 1))
            act.activation(w2_hi[b][:], w2_in[b][:], ACT.Copy).then_inc(w2_hi_done, 1)

        def pool_lo(pool, e, b):
            pool.wait_ge(w1_hi_done, e + 1)
            pool.tensor_tensor(w1_lo[b][:], w1_in[b][:], raw(w1_hi[b][:]), ALU.subtract).then_inc(w1_lo_done, 1)
            pool.wait_ge(w2_hi_done, e + 1)
            pool.tensor_tensor(w2_lo[b][:], w2_in[b][:], raw(w2_hi[b][:]), ALU.subtract).then_inc(w2_lo_done, 1)

        def dve_hot(dve, e, b):
            wait_for(dve, list_ready, e - 1)
            dve.tensor_tensor(row_hot[b][:], slot[:, at(e), :].rearrange("p o t -> p (o t)")[:, :, None].to_broadcast([P, TT, RT]),
                              iota_r[:, None, :].to_broadcast([P, TT, RT]), ALU.is_equal).then_inc(hot_ready, 1)

        def pe_list(pe, e, b):
            pe.wait_ge(hot_ready, e + 1)
            wait_for(pe, xgt_lo_done, TJ * e - 1)
            for t in range(TT):
                last = pe.matmul(ps_i[0:RT, :], row_hot[b][:, t, :], ids[:, at(e), t, :, :].rearrange("p o a j -> p (o a j)"),
                                 start=(t == 0), stop=(t == TT - 1))
            last.then_inc(list_ready, 1)

        def dve_index(dve, e, i, b):
            dve.wait_ge(list_ready, e + 1)
            wait_for(dve, gathered[b], 16 * ST * i)
            wait_for(dve, idx_kept, e - 1)
            dve.tensor_scalar(idx_f[:], ps_i[0:RT, 0:ST], float(P), None, ALU.mult).then_inc(idx_mul, 1)
            dve.wait_ge(idx_mul, e + 1)
            dve.tensor_tensor(idx_g[b][:], ps_i[0:RT, ST:2 * ST], idx_f[:], ALU.add).then_inc(idx_ready, 1)

        idx_f, idx_mul = sb("idx_f", [RT, ST]), sem("idx_mul")

        def pool_gather(pool, e, i, b):
            pool.wait_ge(idx_ready, e + 1)
            wait_for(pool, xgt_ready, TJ * (e - 1))
            wait_for(pool, y_done, ST * (e - 1))
            for j, n in enumerate(rows):
                pool.indirect_dma_start(xg[b][0:n, j, :], None, G.table,
                                        bass.IndirectOffsetOnAxis(ap=idx_g[b][0:n, j:j + 1], axis=0)).then_inc(gathered[b], 16)

        groups = [(0, [(j, 0) for j in range(ST - 1)]), (1, [(j, 1) for j in range(ST - 1)]), (0, [(ST - 1, 0), (ST - 1, 1)])]
        FULL = (ST - 1) * RT

        def xgt_views(n):
            if n < 2:
                return ps_t[:, n, 0:FULL], xt_hi[:, n, 0:FULL], xt_lo[:, n, 0:FULL]
            return (ps_t[:, 0, 0:2 * RT].rearrange("p (k c) -> p k c", k=2)[:, :, 0:TAIL],
                    xt_hi[:, :, FULL:FULL + TAIL], xt_lo[:, :, FULL:FULL + TAIL])

        def pe_xgt(pe, e, i, b, n):
            if n == 0:
                pe.wait_ge(gathered[b], 16 * ST * (i + 1))
                wait_for(pe, xgt_lo_done, TJ * e)
            elif n == 1:
                pe.wait_ge(idx_ready, e + 1)
            else:
                pe.wait_ge(xgt_lo_done, TJ * e + 1)
            bank, tiles = groups[n]
            for c, (j, k) in enumerate(tiles):
                r = rows[j]
                last = pe.transpose(ps_t[:, bank, c * RT:c * RT + r], xg[b][0:r, j, k * P:(k + 1) * P], G.ident[0:r, 0:r])
            last.then_inc(xgt_ready, 1)

        def act_xgt(act, e, n):
            act.wait_ge(xgt_ready, TJ * e + n + 1)
            src, hi, _ = xgt_views(n)
            act.activation(hi, src, ACT.Copy).then_inc(xgt_hi_done, 1)

        def dve_xgt(dve, e, n):
            dve.wait_ge(xgt_hi_done, TJ * e + n + 1)
            src, hi, lo = xgt_views(n)
            dve.tensor_tensor(lo, src, raw(hi), ALU.subtract).then_inc(xgt_lo_done, 1)

        def pe_h(pe, e, b, h):
            if h == 0:
                pe.wait_ge(w1_lo_done, e + 1)
                pe.wait_ge(xgt_lo_done, TJ * (e + 1))
            wait_for(pe, gelu_done, HT * e + h - 1)
            cols = slice(h * P, (h + 1) * P)
            terms = [(w, x, k) for k in range(KD) for w, x in ((w1_hi[b], xt_hi), (w1_hi[b], xt_lo), (w1_lo[b], xt_hi))]
            for c in range(2):
                for n, (w, x, k) in enumerate(terms):
                    last = pe.matmul(ps_h[:, h % 2, c, 0:HS], w[:, k, cols], x[:, k, c * HS:(c + 1) * HS],
                                     start=(n == 0), stop=(n == len(terms) - 1))
            last.then_inc(h_ready, 1)

        def act_h(act, e, h):
            act.wait_ge(h_ready, HT * e + h + 1)
            wait_for(act, h_lo_done, HT * e + h - 1)
            act.activation(h_f[:, h % 2, :].rearrange("p (c n) -> p c n", c=2), ps_h[:, h % 2, :, 0:HS], ACT.Gelu,
                           bias=G.b1_t[:, b1_col(e, h)]).then_inc(gelu_done, 1)
            act.wait_ge(gelu_done, HT * e + h + 1)
            act.activation(h_hi[:, h, :], h_f[:, h % 2, :], ACT.Copy).then_inc(h_hi_done, 1)

        def b1_col(e, h):
            return at(e * HT + h)

        def dve_h(dve, e, h):
            dve.wait_ge(h_hi_done, HT * e + h + 1)
            dve.tensor_tensor(h_lo[:, h, :], h_f[:, h % 2, :], raw(h_hi[:, h, :]), ALU.subtract).then_inc(h_lo_done, 1)

        def pe_y(pe, e, b, j):
            if j == 0:
                pe.wait_ge(w2_lo_done, e + 1)
            wait_for(pe, y_read, ST * e + j - 1)
            m = rows[j] + rows[j] % 2
            bank = (ST * b + j) % 2
            for h in range(HT):
                if j == 0:
                    pe.wait_ge(h_lo_done, HT * e + h + 1)
                for n, (x, w) in enumerate(((h_hi, w2_hi[b]), (h_hi, w2_lo[b]), (h_lo, w2_hi[b]))):
                    last = pe.matmul(ps_y[0:m, bank, 0:D], x[:, h, j * RT:j * RT + m], w[:, h, :],
                                     start=(h == 0 and n == 0), stop=(h == HT - 1 and n == 2))
            last.then_inc(y_ready, 1)

        def dve_y(dve, e, i, b, j):
            n = rows[j]
            dve.wait_ge(y_ready, ST * e + j + 1)
            if j == 0:
                wait_for(dve, scattered[b], 16 * ST * i)
                dve.tensor_copy(idx_s[b][:], idx_g[b][:]).then_inc(idx_kept, 1)
            dve.tensor_tensor(y_sb[b][0:n, j, :], ps_y[0:n, (ST * b + j) % 2, 0:D],
                              b2_sb[0:n, at(e), :].rearrange("p o d -> p (o d)"), ALU.add).then_inc(y_read, 1)
            dve.wait_ge(y_read, ST * e + j + 1)
            dve.tensor_scalar(y_sb[b][0:n, j, :], y_sb[b][0:n, j, :], xg[b][0:n, j, at(D + e)], None, ALU.mult).then_inc(y_done, 1)

        def pool_scatter(pool, e, i, b):
            pool.wait_ge(idx_kept, e + 1)
            pool.wait_ge(y_done, ST * (e + 1))
            wait_for(pool, scattered[1 - b], 16 * ST * (i + b))
            for j, n in enumerate(rows):
                pool.indirect_dma_start(out[0], bass.IndirectOffsetOnAxis(ap=idx_s[b][0:n, j:j + 1], axis=0),
                                        y_sb[b][0:n, j, :], None, compute_op=ALU.add).then_inc(scattered[b], 16)

        def nxt(i, b):
            return i + b, 1 - b

        def pe_expert(pe, e, i, b, last):
            for h in range(HT):
                pe_h(pe, e, b, h)
                if h == 1 and not last:
                    pe_list(pe, e + 1, 1 - b)
            for j in range(ST):
                pe_y(pe, e, b, j)
                if not last:
                    for n in {0: (0, 1), 1: (2,)}.get(j, ()):
                        pe_xgt(pe, e + 1, *nxt(i, b), n)

        def act_expert(act, e, i, b, last):
            for h in range(HT):
                act_h(act, e, h)
            if not last:
                for n in range(TJ):
                    act_xgt(act, e + 1, n)
                act_w2_hi(act, e + 1, *nxt(i, b))

        def dve_expert(dve, e, i, b, last):
            if not last:
                dve_hot(dve, e + 1, 1 - b)
            for h in range(HT):
                dve_h(dve, e, h)
                if h == 1 and not last:
                    dve_index(dve, e + 1, *nxt(i, b))
                if h == 2 and not last:
                    dve_w1_hi(dve, e + 1, *nxt(i, b))
            for j in range(ST):
                dve_y(dve, e, i, b, j)
                if not last:
                    for n in {0: (0, 1), 1: (2,)}.get(j, ()):
                        dve_xgt(dve, e + 1, n)

        def pool_expert(pool, e, i, b, last):
            if not (isinstance(e, int) and e == 0):
                pool_scatter(pool, e - 1, i - 1 + b, 1 - b)
            if not last:
                pool_gather(pool, e + 1, *nxt(i, b))
                pool_lo(pool, e + 1, 1 - b)

        def all_experts(eng, expert):
            for b in range(2):
                expert(eng, b, 0, b, False)
            with eng.Fori(1, E // 2 - 1) as i:
                for b in range(2):
                    expert(eng, 2 * i + b, i, b, False)
            for b in range(2):
                expert(eng, E - 2 + b, E // 2 - 1, b, b == 1)

        STEPS = 5

        with nc.Block() as block:

            @block.sync
            def _(sp):
                sp_weights(sp, 0, 0, 0)
                sp_weights(sp, 1, 0, 1)
                sp.dma_start(b2_sb[:], A["b2"].rearrange("(o e) n -> o (e n)", o=1).to_broadcast([RT, E * D])
                             .rearrange("p (e n) -> p e n", e=E)).then_inc(b2_loaded, 16)
                with sp.Fori(1, E // 2) as i:
                    for b in range(2):
                        sp_weights(sp, 2 * i + b, i, b)

            @block.gpsimd
            def _(pool):
                pool.memset(step[:, 0:1], 1 << (SEARCH_BITS - 2)).then_inc(consts, 1)
                pool.memset(step[:, 1:2], 2 << (SEARCH_BITS - 2)).then_inc(consts, 1)
                pool.memset(step[:, 2:3], 3 << (SEARCH_BITS - 2)).then_inc(consts, 1)
                pool.memset(cand[0][:], 0).then_inc(consts, 1)
                pool.memset(ones_b[:], 1.0).then_inc(consts, 1)
                pool.memset(before[:], 1.0).then_inc(masks_set, 1)
                pool.wait_ge(masks_set, 1)
                pool.affine_select(out=before[:], in_=before[:], compare_op=ALU.is_gt, fill=0.0, base=0,
                                   pattern=[[1, P]], channel_multiplier=-1).then_inc(masks_set, 1)
                pool.iota(iota_i[:], pattern=[[1, P]], base=0, channel_multiplier=0).then_inc(masks_set, 1)
                pool.wait_ge(masks_set, 3)
                pool.tensor_copy(iota_r[:], iota_i[:, 0:RT]).then_inc(masks_set, 1)
                pool.wait_ge(masks_set, 4)
                pool.iota(iota_i[:, 0:1], pattern=[[0, 1]], base=0, channel_multiplier=1).then_inc(masks_set, 1)
                pool.wait_ge(masks_set, 5)
                pool.tensor_copy(iota_p[:], iota_i[:, 0:1]).then_inc(masks_set, 1)
                pool.memset(raw(xt_hi[:, :, CAP:NS]), 0.0).then_inc(padded, 1)
                pool.memset(raw(xt_lo[:, :, CAP:NS]), 0.0).then_inc(padded, 1)
                pool_lo(pool, 0, 0)
                pool_gather(pool, 0, 0, 0)
                for e in range(E):
                    pool_expert(pool, e, e // 2, e % 2, e == E - 1)
                pool_scatter(pool, E - 1, E // 2 - 1, 1)
                for b in range(2):
                    pool.wait_ge(scattered[b], 16 * ST * (E // 2))

            @block.scalar
            def _(act):
                act_w2_hi(act, 0, 0, 0)
                for n in range(TJ):
                    act_xgt(act, 0, n)
                all_experts(act, act_expert)

            @block.tensor
            def _(pe):
                pe.wait_ge(consts, 5)
                with pe.Fori(0, ROUNDS) as r:
                    pe.wait_ge(cand_done, r + 1)
                    pe.matmul(ps_c[:, 0, 0:3 * E], ones_b[:], part[:].rearrange("p e j -> p (e j)"), start=True, stop=True).then_inc(counts_ready, 1)
                pe.wait_ge(masks_set, 2)
                pe.wait_ge(ranks, 3)
                pe.matmul(ps_c[:, 1, 0:E], ones_b[:], cnt[:], start=True, stop=True).then_inc(counts_ready, 1)
                flat = mask[:].rearrange("p a e t -> p (a e) t")
                pre = ps_pre.rearrange("p (a t) -> p a t", t=TT)
                pe.matmul(pre, before[:], flat, start=True, stop=False)
                for t in range(TT - 1):
                    last = pe.matmul(pre[:, :, t + 1:TT], ones_b[:], flat[:, :, t:t + 1].to_broadcast([P, 2 * E, TT - 1 - t]),
                                     start=False, stop=(t == TT - 2))
                last.then_inc(counts_ready, 1)
                pe.wait_ge(ranks, RANKS)
                pe_list(pe, 0, 0)
                pe.wait_ge(padded, 2)
                for n in range(TJ):
                    pe_xgt(pe, 0, 0, 0, n)
                all_experts(pe, pe_expert)

            @block.vector
            def _(dve):
                dve_w1_hi(dve, 0, 0, 0)
                dve.wait_ge(consts, 5)
                with dve.Fori(0, ROUNDS) as r:
                    a, c = cand
                    base = r * STEPS
                    dve.tensor_tensor(a[:, :, 1:4], a[:, :, 0:1].to_broadcast([P, E, 3]),
                                      step[:, None, :].to_broadcast([P, E, 3]), ALU.bitwise_or).then_inc(srch, 1)
                    dve.wait_ge(srch, base + 1)
                    dve.tensor_scalar(step[:], step[:], 2, None, ALU.logical_shift_right).then_inc(srch, 1)
                    dve.tensor_tensor(above[:], G.scores[:, :, None, :].to_broadcast([P, E, 3, TT]),
                                      a[:, :, 1:4, None].bitcast(F32).to_broadcast([P, E, 3, TT]), ALU.is_ge).then_inc(srch, 1)
                    dve.wait_ge(srch, base + 3)
                    with nc.allow_low_precision("counts of at most 16"):
                        dve.tensor_reduce(part[:], above[:], AX.X, ALU.add).then_inc(cand_done, 1)
                    dve.wait_ge(counts_ready, r + 1)
                    dve.scalar_tensor_tensor(out=a[:, :, 1:4].bitcast(F32), in0=ps_c[:, 0, 0:3 * E].rearrange("p (e j) -> p e j", j=3),
                                             scalar=float(CAP), in1=a[:, :, 1:4].bitcast(F32), op0=ALU.is_ge,
                                             op1=ALU.mult).then_inc(srch, 1)
                    dve.wait_ge(srch, base + 4)
                    dve.tensor_reduce(c[:, :, 0].bitcast(F32), a[:].bitcast(F32), AX.X, ALU.max).then_inc(srch, 1)
                    dve.wait_ge(srch, base + 5)
                    dve.tensor_copy(a[:, :, 0], c[:, :, 0]).then_inc(counted, 1)
                    dve.wait_ge(counted, r + 1)
                n = 0

                def step_done(ins):
                    nonlocal n
                    n += 1
                    ins.then_inc(ranks, 1)

                thr = cand[0][:, :, 0:1].bitcast(F32).to_broadcast([P, E, TT])
                step_done(dve.tensor_tensor(mask[:, 0], G.scores[:], thr, ALU.is_gt))
                step_done(dve.tensor_tensor(mask[:, 1], G.scores[:], thr, ALU.is_equal))
                dve.wait_ge(ranks, 2)
                with nc.allow_low_precision("counts of at most 16"):
                    step_done(dve.tensor_reduce(cnt[:], mask[:, 0], AX.X, ALU.add))
                dve.wait_ge(counts_ready, ROUNDS + 1)
                step_done(dve.tensor_scalar(need[:], ps_c[:, 1, 0:E], -1.0, float(CAP), ALU.mult, ALU.add))
                dve.wait_ge(ranks, n)
                dve.wait_ge(counts_ready, ROUNDS + 2)
                above_before, equal_before = (ps_pre[:, k * P:(k + 1) * P].rearrange("p (e t) -> p e t", e=E) for k in range(2))
                need_b = need[:, :, None].to_broadcast([P, E, TT])
                step_done(dve.tensor_tensor(tie[:], equal_before, need_b, ALU.is_lt))
                step_done(dve.tensor_tensor(pos[:], equal_before, need_b, ALU.min))
                dve.wait_ge(ranks, n)
                step_done(dve.tensor_tensor(sel[:], tie[:], mask[:, 1], ALU.mult))
                step_done(dve.tensor_tensor(pos[:], pos[:], above_before, ALU.add))
                dve.wait_ge(ranks, n)
                step_done(dve.tensor_tensor(sel[:], sel[:], mask[:, 0], ALU.add))
                dve.wait_ge(ranks, n)
                step_done(dve.scalar_tensor_tensor(out=pos[:], in0=pos[:], scalar=-float(FAR), in1=sel[:], op0=ALU.add, op1=ALU.mult))
                dve.wait_ge(ranks, n)
                step_done(dve.tensor_scalar(pos[:], pos[:], float(FAR), None, ALU.add))
                dve.wait_ge(ranks, n)
                step_done(dve.tensor_scalar(tile_no[:], pos[:], float(RT), None, ALU.is_ge))
                for j in range(2, ST):
                    dve.wait_ge(ranks, n)
                    step_done(dve.scalar_tensor_tensor(out=tile_no[:], in0=pos[:], scalar=float(j * RT), in1=tile_no[:],
                                                       op0=ALU.is_ge, op1=ALU.add))
                dve.wait_ge(ranks, n)
                dve.wait_ge(masks_set, 6)
                step_done(dve.scalar_tensor_tensor(out=slot[:], in0=tile_no[:], scalar=-float(RT), in1=pos[:], op0=ALU.mult, op1=ALU.add))
                step_done(dve.tensor_tensor(tile_hot[:], tile_no[:, :, :, None].to_broadcast([P, E, TT, ST]),
                                            iota_r[:, None, None, 0:ST].to_broadcast([P, E, TT, ST]), ALU.is_equal))
                dve.wait_ge(ranks, n)
                step_done(dve.tensor_tensor(ids[:, :, :, 0, :], tile_hot[:],
                                            iota_r[:, None, 0:TT, None].to_broadcast([P, E, TT, ST]), ALU.mult))
                step_done(dve.tensor_scalar(ids[:, :, :, 1, :], tile_hot[:], iota_p[:, 0:1], None, ALU.mult))
                assert n == RANKS
                dve_hot(dve, 0, 0)
                dve_index(dve, 0, 0, 0)
                dve.wait_ge(b2_loaded, 16)
                for k in range(TJ):
                    dve_xgt(dve, 0, k)
                all_experts(dve, dve_expert)


FAR = 4096
RANKS = 19


class Shared:
    pass


def build(nc, A, out, debug=None):
    S = Shapes(A["x"], A["ctx"], A["wq"], A["router_w"], A["w1"])
    G = Shared()
    with ExitStack() as top:
        def sem(name):
            return top.enter_context(nc.semaphore(name))

        G.wq_scr = nc.dram_tensor("wq_scr", [S.NP, P, 2, 2, P], F32).ap()
        G.wk_scr = nc.dram_tensor("wk_scr", [S.NP, P, 2, 2, P], F32).ap()
        G.q_scr = nc.dram_tensor("q_scr", [S.NP, 2, P, S.NT], F32).ap()
        G.k_scr = nc.dram_tensor("k_scr", [S.NP, 2, P, S.NKP], F32).ap()
        G.v_scr = nc.dram_tensor("v_scr", [S.H, P, S.KT, S.DH], F32).ap()
        G.rec_scr = nc.dram_tensor("rec_scr", [2, S.QC], F32).ap()
        G.o_scr = nc.dram_tensor("o_scr", [S.NP, P, S.NT], F32).ap()
        G.table = nc.dram_tensor("table", [S.NT, S.D + S.E], F32).ap()
        G.ident = top.enter_context(nc.sbuf_tensor("ident", [P, P], F32))
        G.ones = top.enter_context(nc.sbuf_tensor("ones", [P, P], F32))
        G.pad_bias = top.enter_context(nc.sbuf_tensor("pad_bias", [P, 1], F32))
        with ExitStack() as att:
            def sb(name, shape, dt=F32R):
                return att.enter_context(nc.sbuf_tensor(name, shape, dt))
            G.xt_hi, G.xt_lo = sb("xt_hi", [P, S.KD, S.NT]), sb("xt_lo", [P, S.KD, S.NT])
            G.wo_hi, G.wo_lo = sb("wo_hi", [P, S.NP, S.D]), sb("wo_lo", [P, S.NP, S.D])
            G.c1_hi, G.c1_lo, G.c2 = sb("c1_hi", [P, S.NKP]), sb("c1_lo", [P, S.NKP]), sb("c2", [P, S.NKP])
            G.k2 = [sb(f"k2_{b}", [P, S.NKP]) for b in range(2)]
            G.q2 = [sb(f"q2_{b}", [P, S.NT]) for b in range(2)]
            G.k1, G.q1 = [sb("k1_0", [P, S.NKP])], [sb("q1_0", [P, S.NT])]
            G.mx_part = sb("mx_part", [P, S.UQ // P, 4], F32)
            G.rough_ready, G.rough_used = sem("rough_ready"), sem("rough_used")
            phase_prologue(nc, S, A, G, sem)
            if debug != "prologue":
                phase_attention(nc, S, A, G, sem)
        if debug is None:
            G.scores = top.enter_context(nc.sbuf_tensor("scores", [P, S.E, S.TT], F32))
            G.b1_t = top.enter_context(nc.sbuf_tensor("b1_t", [P, S.E * S.HT], F32))
            phase_output(nc, S, A, G, sem, out)
            phase_experts(nc, S, A, G, sem, out)


_INS = {"x": "x", "ctx_768": "ctx", "L0_xattn_Wq": "wq", "L0_xattn_Wk": "wk", "L0_xattn_Wv": "wv", "L0_xattn_Wo": "wo",
        "L0_xattn_bo": "bo", "L0_ffn_router_w": "router_w", "L0_ffn_w1": "w1", "L0_ffn_b1": "b1", "L0_ffn_w2": "w2",
        "L0_ffn_b2": "b2"}


def kernel(**inputs):
    import numpy as _np
    import concourse.bacc as _bacc
    from concourse.bass_utils import run_bass_kernel_spmd as _run

    nc = _bacc.Bacc("TRN2", target_bir_lowering=False, num_devices=1)
    arrays, A = {}, {}
    for name, short in _INS.items():
        a = _np.ascontiguousarray(inputs[name])
        arrays[f"in_{short}"] = a
        A[short] = nc.dram_tensor(f"in_{short}", a.shape, mybir.dt.from_np(a.dtype), kind="ExternalInput").ap()
    out = nc.dram_tensor("out_0", inputs["x"].shape, F32, kind="ExternalOutput").ap()
    build(nc, A, out)
    r = _run(nc, [arrays], core_ids=[0])
    return r.results[0]["out_0"]
```

```python
from contextlib import ExitStack

import concourse.bass as bass
from concourse import mybir

ALU = mybir.AluOpType
ACT = mybir.ActivationFunctionType
AX = mybir.AxisListType
F32 = mybir.dt.float32
F32R = mybir.dt.float32r
BF16 = mybir.dt.bfloat16
I32 = mybir.dt.int32
U32 = mybir.dt.uint32

P = 128
EPS = 1e-5


def raw(ap):
    return ap.bitcast(F32)


class Shapes:

    def __init__(self, x, ctx, wq, router_w, w1):
        self.NT, self.D = x.shape[1], x.shape[2]
        self.NK, self.DC = ctx.shape[1], ctx.shape[2]
        self.DI = wq.shape[1]
        self.DH = 64
        self.H = self.DI // self.DH
        self.TT = self.NT // P
        self.KT = -(-self.NK // P)
        self.NKP = self.KT * P
        self.LAST = self.NK - (self.KT - 1) * P
        self.KD = self.D // P
        self.NP = self.H // 2
        self.QC = 512
        self.QB = self.NT // self.QC
        self.UQ = 2 * self.QC
        self.KC = self.NKP // 4
        self.MC = 402
        self.MS = [0, self.MC - 2, self.NK - 2 * self.MC + 2, self.NK - self.MC]
        assert self.MS[2] <= self.MS[1] + self.MC and self.DC == P + P // 2
        self.E, self.HID = router_w.shape[0], w1.shape[2]
        self.HT = self.HID // P
        self.CAP = int(self.NT * 2.0 / self.E) + 1


def refine_rstd(dve, var, rstd, tmp, done, count):
    dve.tensor_tensor(tmp, rstd, rstd, ALU.mult).then_inc(done, 1)
    dve.wait_ge(done, count + 1)
    dve.scalar_tensor_tensor(out=tmp, in0=var, scalar=EPS, in1=tmp, op0=ALU.add, op1=ALU.mult).then_inc(done, 1)
    dve.wait_ge(done, count + 2)
    dve.tensor_scalar(tmp, tmp, -0.5, 1.5, ALU.mult, ALU.add).then_inc(done, 1)
    dve.wait_ge(done, count + 3)
    dve.tensor_tensor(rstd, rstd, tmp, ALU.mult).then_inc(done, 1)
    dve.wait_ge(done, count + 4)


def head_parts(S, G, hd):
    HP = P // 2
    q1, q2, k1, k2 = G.q1[hd], G.q2[hd], G.k1[hd], G.k2[hd]
    return ((q1[0:HP, :], G.q_scr, 0), (q1[HP:P, :], G.q_scr, 0), (q2[0:HP, :], G.q_scr, 1),
            (k1[0:HP, :], G.k_scr, 0), (k1[HP:P, :], G.k_scr, 1), (k2[0:HP, :], G.k_scr, 0))


MJOBS = 32
ROUGH_LEAD = 2


def rough_scores(S, G, pe, bank, hd, half, j):
    q0, k0 = half * S.UQ + (j // 4) * P, S.MS[j % 4]
    pe.matmul(bank[:, 0:S.MC], G.q1[hd][:, q0:q0 + P], G.k1[hd][:, k0:k0 + S.MC], start=True, stop=True).then_inc(G.rough_ready, 1)


def rough_max(S, G, dve, bank, j):
    dve.tensor_reduce(G.mx_part[:, j // 4, j % 4:j % 4 + 1], bank[:, 0:S.MC], AX.X, ALU.max).then_inc(G.rough_used, 1)


def phase_prologue(nc, S, A, G, sem):
    with ExitStack() as ctx:
        def sb(name, shape, dt=F32):
            return ctx.enter_context(nc.sbuf_tensor(name, shape, dt))

        TT, KT, KD, LAST = S.TT, S.KT, S.KD, S.LAST
        HP = P // 2
        x_in = G.x_in
        stats = sb("ln1_stats", [P, TT, 6])
        mv = sb("ln1_mv", [P, TT, 2])
        std = sb("ln1_std", [P, TT])
        rstd = sb("ln1_rstd", [P, TT])
        nt = sb("ln1_nt", [P, TT])
        eps = sb("ln1_eps", [P, 1])
        c_in = sb("c_in", [P, KT, 2 * P])
        w_in = [sb(f"w_in{n}", [P, 2, S.DI]) for n in range(2)]
        w_in.append(w_in[0])
        w_hi = [sb(f"w_hi{n}", [P, 2, S.DI], F32R)[:] for n in range(2)] + [G.wo_hi[:].rearrange("p (k a) n -> p k (a n)", k=2)]
        w_lo = [sb(f"w_lo{n}", [P, 2, S.DI], F32R)[:] for n in range(2)] + [G.wo_lo[:].rearrange("p (k a) n -> p k (a n)", k=2)]
        v_st = G.v_st
        ps = [ctx.enter_context(nc.psum_tensor(f"pro_ps{i}", [P, 512], F32)) for i in range(8)]

        VS = KT * 2 * P // S.DI
        v_slot = [c_in[:].rearrange("p t c -> p (t c)")[:, i * S.DI:(i + 1) * S.DI] for i in range(VS)]

        s_c, s_cz = sem("p_c_loaded"), sem("p_c_padded")
        s_x = [sem(f"p_x_loaded{i}") for i in range(4)]
        s_w = [sem(f"p_w_loaded{i}") for i in range(3)]
        s_eps, s_stats, s_mv, s_std, s_rstd, s_xn = (sem(f"p_{n}") for n in ("eps", "stats", "mv", "std", "rstd", "xn"))
        s_whi, s_wlo, s_wst = sem("p_whi"), sem("p_wlo"), sem("p_wstored")
        s_ps, s_hi, s_lo = sem("p_ps_ready"), sem("p_hi_done"), sem("p_lo_done")
        s_v = sem("p_v_ready")
        s_vev = [sem(f"p_v_copied{i}") for i in range(2)]
        s_vst = [sem(f"p_v_stored{i}") for i in range(VS)]
        s_id, s_ones = sem("p_ident"), sem("p_ones")
        s_rows = sem("p_rows")
        s_proj, s_sthi, s_stlo, s_head = sem("p_proj_ready"), sem("p_stage_hi"), sem("p_stage_lo"), sem("p_head_loaded")
        s_sst = [sem(f"p_stage_stored{i}") for i in range(2)]
        ident = G.ident

        xt = [("x", range(4 * g, 4 * g + 4), k) for g in range(TT // 4) for k in range(KD)]
        ct = [("c", range(4 * g, min(4 * g + 4, KT)), k) for g in range(-(-KT // 4)) for k in range(2)]
        tjobs = ct + xt
        NTJ = len(tjobs)

        def targets(job):
            src, tiles, k = job
            a, b = tiles[0] * P, (tiles[-1] + 1) * P
            if src == "x":
                return G.xt_hi[:, k, a:b], G.xt_lo[:, k, a:b], 0, b - a
            if k == 0:
                return G.c1_hi[:, a:b], G.c1_lo[:, a:b], 0, b - a
            return G.c2[:, a:b], G.c2[HP:P, a:b], HP, b - a

        vjobs = [(kt, half) for kt in range(KT) for half in range(2)]
        LOADS = (48, 16, 48)
        NPJ = 4

        def width(n):
            return S.KC if n < NPJ else S.QC

        def proj_before(j):
            return {len(ct): (0, 1), len(ct) + 4: (2, 3)}.get(j, ())

        def rough_after(j):
            first = len(vjobs) - MJOBS // 2 - ROUGH_LEAD
            return [2 * (j - first) + i for i in range(2)] if first <= j < first + MJOBS // 2 else []

        def stage(n, part):
            return v_st[:, part, (n % 2) * S.QC:(n % 2) * S.QC + width(n)].bitcast(F32R)

        with nc.Block() as block:

            @block.sync
            def _(sp):
                sp.dma_start(c_in[:, 0:KT - 1, 0:S.DC],
                             A["ctx"][0, 0:(KT - 1) * P, :].rearrange("(t p) d -> p t d", p=P)).then_inc(s_c, 16)
                sp.dma_start(c_in[:, 0:KT - 1, S.DC:2 * P],
                             A["ctx"][0, 0:(KT - 1) * P, P:S.DC].rearrange("(t p) d -> p t d", p=P)).then_inc(s_c, 16)
                sp.wait_ge(s_cz, 1)
                sp.dma_start(c_in[0:LAST, KT - 1, 0:S.DC], A["ctx"][0, (KT - 1) * P:S.NK, :]).then_inc(s_c, 16)
                sp.dma_start(c_in[0:LAST, KT - 1, S.DC:2 * P],
                             A["ctx"][0, (KT - 1) * P:S.NK, P:S.DC]).then_inc(s_c, 16)

                def load_split(n, w):
                    sp.dma_start(w_in[n][:, 0, :], A[w][0:P, :]).then_inc(s_w[n], 16)
                    sp.dma_start(w_in[n][0:HP, 1, :], A[w][P:S.DC, :]).then_inc(s_w[n], 16)
                    sp.dma_start(w_in[n][HP:P, 1, :], A[w][P:S.DC, :]).then_inc(s_w[n], 16)

                load_split(0, "wk")
                for g in range(4):
                    t = slice(g * TT // 4, (g + 1) * TT // 4)
                    sp.dma_start(x_in[:, t, :], A["x"][0].rearrange("(t p) d -> p t d", p=P)[:, t, :]).then_inc(s_x[g], 16)
                sp.dma_start(w_in[1][:], A["wq"].rearrange("(k p) n -> p k n", p=P)).then_inc(s_w[1], 16)
                sp.wait_ge(s_wlo, 1)
                load_split(2, "wv")

                def store_weight(n, scr):
                    sp.wait_ge(s_whi, n + 1)
                    sp.wait_ge(s_wlo, n + 1)
                    for k in range(2):
                        for part, w in ((0, w_hi[n]), (1, w_lo[n])):
                            sp.dma_start(scr[:, :, part, k, :].rearrange("h p c -> p h c"),
                                         raw(w[:, k, :]).rearrange("p (h c) -> p h c", c=P)).then_inc(s_wst, 16)

                def store_blocks(blocks, scr, w):
                    for c, n in enumerate(blocks):
                        sp.wait_ge(s_stlo, n + 1)
                        for part in range(2):
                            sp.dma_start(scr[0, part, :, c * w:(c + 1) * w], raw(stage(n, part))).then_inc(s_sst[n % 2], 16)

                def store_v(kt):
                    sp.wait_ge(s_vev[0], kt + 1)
                    sp.wait_ge(s_vev[1], kt + 1)
                    sp.dma_start(G.v_scr[:, kt, :], v_slot[kt % VS]).then_inc(s_vst[kt % VS], 16)

                store_weight(0, G.wk_scr)
                store_blocks(range(NPJ), G.k_scr, S.KC)
                store_blocks(range(NPJ, 2 * NPJ), G.q_scr, S.QC)
                for b in range(2):
                    sp.wait_ge(s_sst[b], 32 * NPJ)
                for dst, scr, part in head_parts(S, G, 0):
                    sp.dma_start(raw(dst), scr[0, part, 0:HP, :]).then_inc(s_head, 16)
                for kt in range(KT):
                    store_v(kt)
                    if kt == KT // 2:
                        store_weight(1, G.wq_scr)
                sp.wait_ge(s_head, 96)
                sp.wait_ge(s_wst, 128)
                for i in range(VS):
                    sp.wait_ge(s_vst[i], 16 * len(range(i, KT, VS)))

            @block.gpsimd
            def _(pool):
                pool.memset(ident[:], 0.0).then_inc(s_id, 1)
                pool.wait_ge(s_id, 1)
                pool.affine_select(out=ident[:], in_=ident[:], compare_op=ALU.not_equal, fill=1.0, base=0,
                                   pattern=[[-1, P]], channel_multiplier=1).then_inc(s_id, 1)
                pool.memset(G.ones[:], 1.0).then_inc(s_ones, 1)
                pool.memset(G.pad_bias[:], 0.0).then_inc(s_ones, 1)
                pool.wait_ge(s_ones, 2)
                pool.affine_select(out=G.pad_bias[:], in_=G.pad_bias[:], compare_op=ALU.is_gt, fill=-10000.0,
                                   base=LAST, pattern=[[0, 1]], channel_multiplier=-1).then_inc(s_ones, 1)
                pool.wait_ge(s_id, 2)
                pool.wait_ge(s_ones, 3)
                n = 0
                for b in range(2):
                    for rows, value in ((G.k2[b][HP:P, :], 0.0), (G.q2[b][HP:P, :], 0.0), (G.k2[b][HP:HP + 1, 0:S.NK], 1.0)):
                        pool.memset(raw(rows), value).then_inc(s_rows, 1)
                        n += 1
                        pool.wait_ge(s_rows, n)
                for n in range(3):
                    pool.wait_ge(s_w[n], LOADS[n])
                    pool.wait_ge(s_whi, n + 1)
                    pool.tensor_tensor(w_lo[n], w_in[n][:], raw(w_hi[n]), ALU.subtract).then_inc(s_wlo, 1)

            @block.vector
            def _(dve):
                dve.memset(c_in[HP:P, KT - 1, :], 0.0).then_inc(s_cz, 1)
                dve.memset(eps[:], EPS).then_inc(s_eps, 1)

                def weight_hi(n):
                    dve.wait_ge(s_w[n], LOADS[n])
                    dve.tensor_copy(w_hi[n], w_in[n][:]).then_inc(s_whi, 1)

                def lo(j):
                    hi_t, lo_t, r0, n = targets(tjobs[j])
                    dve.wait_ge(s_ps, j + 1)
                    dve.wait_ge(s_hi, j + 1)
                    src = hi_t if r0 == 0 else G.c2[HP:P, tjobs[j][1][0] * P:(tjobs[j][1][-1] + 1) * P]
                    dve.tensor_tensor(lo_t, ps[j % 4][r0:P, 0:n], raw(src), ALU.subtract).then_inc(s_lo, 1)

                def proj_lo(n):
                    dve.wait_ge(s_sthi, n + 1)
                    dve.tensor_tensor(stage(n, 1), ps[4 + n % 4][:, 0:width(n)], raw(stage(n, 0)), ALU.subtract).then_inc(s_stlo, 1)

                for j in range(len(ct)):
                    lo(j)
                    if j == 2:
                        weight_hi(0)
                for t in range(TT):
                    if t % (TT // 4) == 0:
                        dve.wait_ge(s_x[t // (TT // 4)], 16)
                    dve.bn_stats(stats[:, t, :], x_in[:, t, :]).then_inc(s_stats, 1)
                for t in range(TT):
                    dve.wait_ge(s_stats, t + 1)
                    dve.bn_aggr(mv[:, t, :], stats[:, t, :]).then_inc(s_mv, 1)
                weight_hi(1)
                dve.wait_ge(s_std, 1)
                dve.reciprocal(rstd[:], std[:]).then_inc(s_rstd, 1)
                dve.wait_ge(s_rstd, 1)
                refine_rstd(dve, mv[:, :, 1], rstd[:], nt[:], s_rstd, 1)
                for t in range(TT):
                    dve.tensor_scalar(x_in[:, t, :], x_in[:, t, :], mv[:, t, 0:1], rstd[:, t:t + 1],
                                      ALU.subtract, ALU.mult).then_inc(s_xn, 1)
                for j in range(len(ct), NTJ):
                    for n in proj_before(j):
                        proj_lo(n)
                    lo(j)
                weight_hi(2)
                for n in range(NPJ, 2 * NPJ):
                    proj_lo(n)

                def rough(job):
                    for j in rough_after(job):
                        dve.wait_ge(G.rough_ready, j + 1)
                        rough_max(S, G, dve, ps[j % 2], j)

                for kt in range(KT):
                    rough(2 * kt)
                    dve.wait_ge(s_v, 2 * kt + 2)
                    if kt >= VS:
                        dve.wait_ge(s_vst[kt % VS], 16 * (kt // VS))
                    dve.tensor_copy(v_slot[kt % VS][:, 512:1024], ps[4 + (2 * kt + 1) % 4][:]).then_inc(s_vev[1], 1)
                    rough(2 * kt + 1)

            @block.scalar
            def _(act):
                def hi(j):
                    hi_t, lo_t, r0, n = targets(tjobs[j])
                    act.wait_ge(s_ps, j + 1)
                    act.activation(hi_t, ps[j % 4][:, 0:n], ACT.Copy).then_inc(s_hi, 1)

                def proj_hi(n):
                    act.wait_ge(s_proj, n + 1)
                    if n >= 2:
                        act.wait_ge(s_sst[n % 2], 32 * (n // 2))
                    act.activation(stage(n, 0), ps[4 + n % 4][:, 0:width(n)], ACT.Copy).then_inc(s_sthi, 1)

                for j in range(len(ct)):
                    hi(j)
                act.wait_ge(s_mv, TT)
                act.wait_ge(s_eps, 1)
                act.activation(std[:], mv[:, :, 1], ACT.Sqrt, bias=eps[:, 0:1]).then_inc(s_std, 1)
                for j in range(len(ct), NTJ):
                    for n in proj_before(j):
                        proj_hi(n)
                    hi(j)
                for n in range(NPJ, 2 * NPJ):
                    proj_hi(n)
                for kt in range(KT):
                    act.wait_ge(s_v, 2 * kt + 1)
                    if kt >= VS:
                        act.wait_ge(s_vst[kt % VS], 16 * (kt // VS))
                    act.activation(v_slot[kt % VS][:, 0:512], ps[4 + (2 * kt) % 4][:], ACT.Copy).then_inc(s_vev[0], 1)

            @block.tensor
            def _(pe):
                def product(bank, terms):
                    for i, (a, b) in enumerate(terms):
                        last = pe.matmul(bank, a, b, start=(i == 0), stop=(i == len(terms) - 1))
                    return last

                def proj(n):
                    if n >= NPJ:
                        pe.wait_ge(s_stlo, n - NPJ + 1)
                    if n < NPJ:
                        hi, lo, cols = w_hi[0], w_lo[0], slice(n * S.KC, (n + 1) * S.KC)
                        terms = [(hi[:, 0, 0:P], G.c1_hi[:, cols]), (hi[:, 0, 0:P], G.c1_lo[:, cols]), (lo[:, 0, 0:P], G.c1_hi[:, cols]),
                                 (hi[:, 1, 0:P], G.c2[:, cols]), (lo[:, 1, 0:P], G.c2[:, cols])]
                    else:
                        hi, lo, cols = w_hi[1], w_lo[1], slice((n - NPJ) * S.QC, (n - NPJ + 1) * S.QC)
                        terms = [(w[:, k, 0:P], xt[:, k, cols]) for w, xt in ((hi, G.xt_hi), (hi, G.xt_lo), (lo, G.xt_hi))
                                 for k in range(KD)]
                    product(ps[4 + n % 4][:, 0:width(n)], terms).then_inc(s_proj, 1)

                pe.wait_ge(s_id, 2)
                pe.wait_ge(s_c, 64)
                for j, (src, tiles, k) in enumerate(tjobs):
                    if j == len(ct):
                        pe.wait_ge(s_lo, len(ct))
                        pe.wait_ge(s_whi, 1)
                        pe.wait_ge(s_wlo, 1)
                        for n in range(NPJ):
                            proj(n)
                    if j >= 4:
                        pe.wait_ge(s_lo, j - 3)
                    if src == "x":
                        pe.wait_ge(s_xn, tiles[-1] + 1)
                    buf = x_in if src == "x" else c_in
                    for i, t in enumerate(tiles):
                        last = pe.transpose(ps[j % 4][:, i * P:(i + 1) * P], buf[:, t, k * P:(k + 1) * P], ident[:])
                    last.then_inc(s_ps, 1)
                pe.wait_ge(s_lo, NTJ)
                pe.wait_ge(s_whi, 2)
                pe.wait_ge(s_wlo, 2)
                for n in range(NPJ, 2 * NPJ):
                    proj(n)
                pe.wait_ge(s_whi, 3)
                pe.wait_ge(s_wlo, 3)
                for j, (kt, half) in enumerate(vjobs):
                    if j < 4:
                        pe.wait_ge(s_stlo, NPJ + j + 1)
                    else:
                        pe.wait_ge(s_vev[half], kt - 1)
                    keys = slice(kt * P, (kt + 1) * P)
                    cols = slice(half * 512, half * 512 + 512)
                    product(ps[4 + j % 4][:], [(c[:, keys], w[:, k, cols]) for c, w, k in (
                        (G.c1_hi, w_hi[2], 0), (G.c1_lo, w_hi[2], 0), (G.c1_hi, w_lo[2], 0), (G.c2, w_hi[2], 1),
                        (G.c2, w_lo[2], 1))]).then_inc(s_v, 1)
                    for r in rough_after(j):
                        if r == 0:
                            pe.wait_ge(s_head, 96)
                        if r >= 2:
                            pe.wait_ge(G.rough_used, r - 1)
                        rough_scores(S, G, pe, ps[r % 2], 0, 0, r)


UNITS = 4
LAG = 2
RING = 4
DVE_TILES = (2, 5, 9, 12)
POOL_TILES = (0, 1, 3, 4, 6, 7, 8, 10, 11)
PROJ_SLOTS = (4, 6, 8, 10)
DEN_SLOT, MROW_SLOT = 3, 11
REC_SLOT, NORM_SLOT = 7, 12
MAHEAD = 3
PLACES = 3
PROJ_JOBS = 2 * len(PROJ_SLOTS)


def wait_for(eng, s, count):
    if not (isinstance(count, int) and count <= 0):
        eng.wait_ge(s, count)


def tile_summed(t):
    tiles = DVE_TILES if t in DVE_TILES else POOL_TILES
    return t in DVE_TILES, max(tiles.index(t), 1)


def phase_attention(nc, S, A, G, sem):
    KT, DH, NP, UQ, QC, KC, MC = S.KT, S.DH, S.NP, S.UQ, S.QC, S.KC, S.MC
    HP = P // 2
    SLOTS = UNITS * KT
    SCALE = float(DH) ** -0.5
    NMU = UQ // P
    ND, NPL = len(DVE_TILES) - 1, len(POOL_TILES) - 1
    assert SLOTS % RING == 0
    with ExitStack() as ctx:
        def sb(name, shape, dt=F32):
            return ctx.enter_context(nc.sbuf_tensor(name, shape, dt))

        wq_s = sb("wq_s", [P, 4, P], F32R)
        wk_s = sb("wk_s", [P, 4, P], F32R)
        st_hi = sb("st_hi", [P, 2, QC], F32R)
        st_lo = sb("st_lo", [P, 2, QC], F32R)
        probs = sb("probs", [P, RING, UQ])
        acc_d = sb("acc_d", [P, UQ])
        acc_p = sb("acc_p", [P, 2, UQ])
        den_sb = G.den_sb
        den_c, rec_c = G.den_c, G.rec_c
        mx = sb("mx", [P, NMU])
        m_row = sb("m_row", [NMU, P], F32R)
        o_n = G.v_st[:, 0, :].rearrange("p (a q) -> p a q", a=2)
        o_sb, rec = G.v_st[:, 1, 0:QC], G.v_st[:, 1, QC:2 * QC]
        vh = [sb(f"vh{b}", [P, KT, DH]) for b in range(2)]
        G.k1.append(sb("k1_1", [P, S.NKP], F32R))
        G.q1.append(sb("q1_1", [P, S.NT], F32R))
        k1, q1 = G.k1, G.q1
        k2, q2 = G.k2, G.q2
        ps_s = ctx.enter_context(nc.psum_tensor("ps_s", [P, 2, 2 * QC], F32))
        ps_m = ctx.enter_context(nc.psum_tensor("ps_m", [P, 2, QC], F32))
        ps_o = ctx.enter_context(nc.psum_tensor("ps_o", [P, QC], F32))
        ps_x = ctx.enter_context(nc.psum_tensor("ps_x", [P, QC], F32))

        w_loaded = sem("w_loaded")
        qk_loaded = [sem(f"qk_loaded{b}") for b in range(2)]
        v_loaded = [sem(f"v_loaded{b}") for b in range(2)]
        stage_stored = [sem(f"stage_stored{b}") for b in range(2)]
        mrow_placed = sem("mrow_placed")
        o_stored = [sem(f"o_stored{b}") for b in range(2)]
        den_moved, rec_stored, rec_placed = sem("den_moved"), sem("rec_stored"), sem("rec_placed")
        scores_ready, exp_done, pv_done = sem("scores_ready"), sem("exp_done"), sem("pv_done")
        rough_ready, rough_used = G.rough_ready, G.rough_used
        max_ready, maxt_ready, mrow_ready = (sem(n) for n in ("max_ready", "maxt_ready", "mrow_ready"))
        proj_ready, stage_hi, stage_lo = sem("proj_ready"), sem("stage_hi"), sem("stage_lo")
        summed_dve, summed_pool = sem("summed_dve"), sem("summed_pool")
        joined = sem("joined")
        wo_loaded, wo_hi_done, wo_split = sem("wo_loaded"), sem("wo_hi_done"), sem("wo_split")
        den_ready, den_copied, rec_ready, o_copied, o_ready = sem("den_ready"), sem("den_copied"), sem("rec_ready"), sem("o_copied"), sem("o_ready")

        def rough_places():
            return [(j, j * KT * PLACES // MJOBS) for j in range(MJOBS)]

        def rough_jobs(u, s, last):
            ahead = 1 if s < KT - MAHEAD else 2
            place = (s + MAHEAD) % KT
            if last and u + ahead >= UNITS:
                return []
            return [(j, ahead, at % PLACES) for j, at in rough_places() if at // PLACES == place]

        def x_wait(pe, p, u, s, last):
            unit = UNITS * p + u
            if s == DEN_SLOT:
                pe.wait_ge(mrow_ready, unit + 1)
            elif s in PROJ_SLOTS and s != PROJ_SLOTS[0]:
                pe.wait_ge(stage_lo, PROJ_JOBS * p + u * len(PROJ_SLOTS) + PROJ_SLOTS.index(s))
            elif s == MROW_SLOT and u < 2 and not last:
                pe.wait_ge(stage_lo, PROJ_JOBS * p + (u + 1) * len(PROJ_SLOTS))
            else:
                wait_for(pe, den_copied, unit)

        def pe_rough(pe, hd, half, j, count):
            wait_for(pe, rough_used, count - 1)
            rough_scores(S, G, pe, ps_m[:, j % 2, :], hd, half, j)

        def dve_rough(dve, j, unit, count):
            if j == 0:
                wait_for(dve, max_ready, unit)
            dve.wait_ge(rough_ready, count + 1)
            rough_max(S, G, dve, ps_m[:, j % 2, :], j)

        def dve_max(dve, unit):
            dve.wait_ge(rough_used, (unit + 1) * MJOBS)
            wait_for(dve, maxt_ready, unit)
            dve.tensor_reduce(mx[:], G.mx_part[:], AX.X, ALU.max).then_inc(max_ready, 1)

        def pe_maxt(pe, unit):
            pe.wait_ge(max_ready, unit + 1)
            pe.transpose(ps_x[0:NMU, 0:P], mx[:], G.ident[:]).then_inc(maxt_ready, 1)

        def act_mrow(act, unit):
            act.wait_ge(maxt_ready, unit + 1)
            wait_for(act, mrow_placed, 16 * unit)
            act.activation(m_row[:], ps_x[0:NMU, 0:P], ACT.Copy, scale=-1.0).then_inc(mrow_ready, 1)

        def sp_mrow(sp, unit, hd, half):
            sp.wait_ge(mrow_ready, unit + 1)
            sp.dma_start(raw(q2[hd][HP:HP + 1, half * UQ:(half + 1) * UQ]), raw(m_row[:])).then_inc(mrow_placed, 16)

        def block_of(n):
            return n % 2 == 0, n // 2

        def pe_proj(pe, n, pair):
            is_q, c = block_of(n)
            if n == 0:
                pe.wait_ge(w_loaded, 32 * pair)
            if is_q:
                cols = slice(c * QC, (c + 1) * QC)
                terms = [(wq_s[:, 2 * part + k, :], xt[:, k, cols])
                         for part, xt in ((0, G.xt_hi), (0, G.xt_lo), (1, G.xt_hi)) for k in range(S.KD)]
            else:
                cols = slice(c * KC, (c + 1) * KC)
                terms = [(wk_s[:, 0, :], G.c1_hi[:, cols]), (wk_s[:, 0, :], G.c1_lo[:, cols]),
                         (wk_s[:, 2, :], G.c1_hi[:, cols]), (wk_s[:, 1, :], G.c2[:, cols]), (wk_s[:, 3, :], G.c2[:, cols])]
            for i, (w, m) in enumerate(terms):
                last = pe.matmul(ps_x[:, 0:QC if is_q else KC], w, m, start=(i == 0), stop=(i == len(terms) - 1))
            last.then_inc(proj_ready, 1)

        def act_proj(act, n, count):
            w = QC if block_of(n)[0] else KC
            act.wait_ge(proj_ready, count + 1)
            wait_for(act, stage_stored[n % 2], 16 * (count - n % 2))
            act.activation(st_hi[:, n % 2, 0:w], ps_x[:, 0:w], ACT.Copy).then_inc(stage_hi, 1)

        def dve_proj(dve, n, count):
            w = QC if block_of(n)[0] else KC
            dve.wait_ge(stage_hi, count + 1)
            dve.tensor_tensor(st_lo[:, n % 2, 0:w], ps_x[:, 0:w], raw(st_hi[:, n % 2, 0:w]), ALU.subtract).then_inc(stage_lo, 1)

        def sp_proj(sp, n, pair, count):
            is_q, c = block_of(n)
            sp.wait_ge(stage_lo, count + 1)
            scr, w = (G.q_scr, QC) if is_q else (G.k_scr, KC)
            for part, st in ((0, st_hi), (1, st_lo)):
                sp.dma_start(scr[pair, part, :, c * w:(c + 1) * w], raw(st[:, n % 2, 0:w])).then_inc(stage_stored[n % 2], 16)

        def sp_load_w(sp, pair):
            sp.dma_start(raw(wq_s[:]), G.wq_scr[pair].rearrange("p a k c -> p (a k) c")).then_inc(w_loaded, 16)
            sp.dma_start(raw(wk_s[:]), G.wk_scr[pair].rearrange("p a k c -> p (a k) c")).then_inc(w_loaded, 16)

        def sp_load_head(sp, pair, hd):
            sp.dma_start(vh[hd][:], G.v_scr.rearrange("p t (h d) -> h p t d", d=DH)[2 * pair + hd]).then_inc(v_loaded[hd], 16)
            rows = slice(hd * HP, (hd + 1) * HP)
            if not (isinstance(pair, int) and pair == 0 and hd == 0):
                for n, (dst, scr, part) in enumerate(head_parts(S, G, hd)):
                    if hd == 0 and n % 3 == 0:
                        sp.wait_ge(stage_stored[n // 3], 16 * PROJ_JOBS * pair)
                    sp.dma_start(raw(dst), scr[pair, part, rows, :]).then_inc(qk_loaded[hd], 16)

        def pe_pv(pe, g, slot, unit, pair):
            hd, s = g // (2 * KT), g % KT
            pe.wait_ge(exp_done, slot + 1)
            if s == 0:
                if g % (2 * KT) == 0:
                    pe.wait_ge(v_loaded[hd], 16 * (pair + 1))
                wait_for(pe, o_copied, unit)
            for b in range(2):
                last = pe.matmul(ps_o[b * HP:b * HP + DH, :], vh[hd][:, s, :], probs[:, g % RING, b * QC:(b + 1) * QC],
                                 start=(s == 0), stop=(s == KT - 1))
            last.then_inc(pv_done, 1)

        def pool_join(pool, u, unit):
            pool.wait_ge(summed_dve, (unit + 1) * ND)
            pool.wait_ge(summed_pool, (unit + 1) * NPL)
            pool.tensor_tensor(acc_p[:, u % 2, :], acc_p[:, u % 2, :], acc_d[:], ALU.add).then_inc(joined, 1)

        def pe_den(pe, u, unit):
            pe.wait_ge(joined, unit + 1)
            for b in range(2):
                last = pe.matmul(ps_x[b * HP:(b + 1) * HP, :], G.ones[:, 0:HP], acc_p[:, u % 2, b * QC:(b + 1) * QC],
                                 start=True, stop=True)
            last.then_inc(den_ready, 1)

        def act_o(act, unit):
            act.wait_ge(pv_done, (unit + 1) * KT)
            wait_for(act, o_ready, unit)
            act.activation(o_sb, ps_o[:], ACT.Copy).then_inc(o_copied, 1)

        def act_den(act, unit):
            act.wait_ge(den_ready, unit + 1)
            wait_for(act, den_moved, 32 * unit)
            act.activation(den_sb[:], ps_x[:], ACT.Copy).then_inc(den_copied, 1)

        def sp_den(sp, unit):
            sp.wait_ge(den_copied, unit + 1)
            for b in range(2):
                sp.dma_start(den_c[8 * b:8 * b + 8, :], den_sb[b * HP:b * HP + 1, :]).then_inc(den_moved, 16)

        def dve_rec(dve, unit):
            dve.wait_ge(den_moved, 32 * (unit + 1))
            dve.reciprocal(rec_c[:], den_c[:]).then_inc(rec_ready, 1)

        def sp_rec(sp, unit):
            sp.wait_ge(rec_ready, unit + 1)
            sp.dma_start(G.rec_scr.rearrange("b (r c) -> (b r) c", r=8), rec_c[:]).then_inc(rec_stored, 16)
            sp.wait_ge(rec_stored, 16 * (unit + 1))
            for b in range(2):
                sp.dma_start(rec[b * HP:(b + 1) * HP, :], G.rec_scr[b:b + 1, :].to_broadcast([HP, QC])).then_inc(rec_placed, 16)

        def dve_norm(dve, unit, u):
            dve.wait_ge(rec_placed, 32 * (unit + 1))
            dve.wait_ge(o_copied, unit + 1)
            wait_for(dve, o_stored[u % 2], 16 * (unit - u % 2))
            dve.tensor_tensor(o_n[:, u % 2, :], o_sb, rec, ALU.mult).then_inc(o_ready, 1)

        def sp_store_o(sp, unit, pair, u):
            hd, q0 = u // 2, (u % 2) * UQ
            sp.wait_ge(o_ready, unit + 1)
            for b in range(2):
                sp.dma_start(G.o_scr[pair, hd * HP:(hd + 1) * HP, q0 + b * QC:q0 + (b + 1) * QC],
                             o_n[b * HP:(b + 1) * HP, u % 2, :]).then_inc(o_stored[u % 2], 16)

        def add_tile(eng, k, u, unit, slot, dve=False):
            tiles, done = (DVE_TILES, summed_dve) if dve else (POOL_TILES, summed_pool)
            acc = acc_d[:] if dve else acc_p[:, u % 2, :]
            t = tiles[k + 1]
            eng.wait_ge(exp_done, slot + t + 1)
            if k == 0:
                if dve:
                    wait_for(eng, joined, unit)
                else:
                    wait_for(eng, den_ready, unit - 1)
                other = probs[:, (u * KT + tiles[0]) % RING, :]
            else:
                eng.wait_ge(done, unit * (len(tiles) - 1) + k)
                other = acc
            eng.tensor_tensor(acc, other, probs[:, (u * KT + t) % RING, :], ALU.add).then_inc(done, 1)

        def pe_pair(pe, p, first=False, last=False):
            for g in range(SLOTS):
                u, s = divmod(g, KT)
                hd, half = divmod(u, 2)
                unit, slot = p * UNITS + u, p * SLOTS + g
                jobs = rough_jobs(u, s, last)

                def rough(place):
                    for j, ahead, at in jobs:
                        if at != place:
                            continue
                        nu = (u + ahead) % UNITS
                        if j == 0 and nu % 2 == 0:
                            pe.wait_ge(qk_loaded[nu // 2], 96 * (p + (u + ahead) // UNITS + (nu // 2)))
                        pe_rough(pe, *divmod(nu, 2), j, (unit + ahead) * MJOBS + j)

                rough(0)
                if s == 0:
                    pe.wait_ge(mrow_placed, 16 * (unit + 1))
                if not (first and g < 2):
                    pe.wait_ge(exp_done, slot - 1)
                keys = slice(s * P, (s + 1) * P)
                for b in range(2):
                    qs = slice(half * UQ + b * QC, half * UQ + (b + 1) * QC)
                    out = ps_s[:, g % 2, b * QC:(b + 1) * QC]
                    pe.matmul(out, k1[hd][:, keys], q1[hd][:, qs], start=True, stop=False)
                    mm = pe.matmul(out, k2[hd][:, keys], q2[hd][:, qs], start=False, stop=True)
                    if b:
                        mm.then_inc(scores_ready, 1)
                    rough(b + 1)
                if not (first and g < LAG):
                    pe_pv(pe, (g - LAG) % SLOTS, slot - LAG, p * UNITS + (g - LAG) // KT, p if g >= LAG else p - 1)
                if s == DEN_SLOT and not (first and u == 0):
                    x_wait(pe, p, u, s, last)
                    pe_den(pe, (u - 1) % UNITS, unit - 1)
                if s in PROJ_SLOTS and u < 2 and not last:
                    x_wait(pe, p, u, s, last)
                    pe_proj(pe, u * len(PROJ_SLOTS) + PROJ_SLOTS.index(s), p + 1)
                if s == MROW_SLOT and not (last and u == UNITS - 1):
                    x_wait(pe, p, u, s, last)
                    pe_maxt(pe, unit + 1)

        def act_pair(act, p, first=False, last=False):
            for g in range(SLOTS):
                u, s = divmod(g, KT)
                if last and u == 1 and s == 1:
                    act.wait_ge(wo_loaded, 16)
                    act.activation(G.wo_hi[:], G.wo_in, ACT.Copy).then_inc(wo_hi_done, 1)
                unit, slot = p * UNITS + u, p * SLOTS + g
                if not (first and g < RING):
                    act.wait_ge(pv_done, slot - RING + 1)
                    by_dve, n = tile_summed((g - RING) % KT)
                    then = p * UNITS + (g - RING) // KT
                    if by_dve:
                        act.wait_ge(summed_dve, then * ND + n)
                    else:
                        act.wait_ge(summed_pool, then * NPL + n)
                act.wait_ge(scores_ready, slot + 1)
                act.activation(probs[:, g % RING, :], ps_s[:, g % 2, :], ACT.Exp,
                               bias=G.pad_bias[:, 0:1] if s == KT - 1 else 0.0, scale=SCALE).then_inc(exp_done, 1)
                if s == LAG - 1 and not (first and u == 0):
                    act_o(act, unit - 1)
                if s == DEN_SLOT and not (first and u == 0):
                    act_den(act, unit - 1)
                if s in PROJ_SLOTS and u < 2 and not last:
                    n = u * len(PROJ_SLOTS) + PROJ_SLOTS.index(s)
                    act_proj(act, n, PROJ_JOBS * p + n)
                if s == MROW_SLOT and not (last and u == UNITS - 1):
                    act_mrow(act, unit + 1)

        def dve_pair(dve, p, first=False, last=False):
            for g in range(SLOTS):
                u, s = divmod(g, KT)
                unit, slot = p * UNITS + u, p * SLOTS + g
                jobs = rough_jobs(u, s, last)
                if s == KT - MAHEAD and not (last and u == UNITS - 1):
                    dve_max(dve, unit + 1)

                def rough(*places):
                    for j, ahead, at in jobs:
                        if at in places:
                            dve_rough(dve, j, unit + ahead, (unit + ahead) * MJOBS + j)

                rough(0)
                if s == 0 and not (first and u == 0):
                    add_tile(dve, ND - 1, (u - 1) % UNITS, unit - 1, slot - KT, dve=True)
                if s - 1 in DVE_TILES[1:]:
                    add_tile(dve, DVE_TILES.index(s - 1) - 1, u, unit, slot - s, dve=True)
                if s - 1 in PROJ_SLOTS and u < 2 and not last:
                    n = u * len(PROJ_SLOTS) + PROJ_SLOTS.index(s - 1)
                    dve_proj(dve, n, PROJ_JOBS * p + n)
                rough(1, 2)
                if s == REC_SLOT and not (first and u == 0):
                    dve_rec(dve, unit - 1)
                if last and u == 1 and s == 2:
                    dve.wait_ge(wo_hi_done, 1)
                    dve.tensor_tensor(G.wo_lo[:], G.wo_in, raw(G.wo_hi[:]), ALU.subtract).then_inc(wo_split, 1)
                if s == NORM_SLOT and not (first and u == 0):
                    dve_norm(dve, unit - 1, (u - 1) % UNITS)

        def pool_pair(pool, p, first=False):
            for u in range(UNITS):
                if not (first and u == 0):
                    pool_join(pool, (u - 1) % UNITS, p * UNITS + u - 1)
                for k in range(NPL):
                    add_tile(pool, k, u, p * UNITS + u, p * SLOTS + u * KT)

        def sp_ahead(sp, u):
            if u == 0:
                sp.dma_start(G.wo_in, A["wo"].rearrange("(h p) n -> p h n", p=P)).then_inc(wo_loaded, 16)
            if u == 2:
                sp.wait_ge(wo_split, 1)
                for b in range(2):
                    sp.wait_ge(o_stored[b], 64 * (NP - 1) + 32 * (1 - b))
                sp.dma_start(G.ot0[:, 0:NP - 1, :], G.o_scr[0:NP - 1, :, 0:QC].rearrange("h p q -> p h q")).then_inc(G.ot_ahead, 16)

        def sp_pair(sp, p, first=False, last=False):
            if not last:
                wait_for(sp, proj_ready, PROJ_JOBS * p)
                sp_load_w(sp, p + 1)
            if not first:
                sp.wait_ge(pv_done, p * SLOTS)
                sp_load_head(sp, p, 1)
            for u in range(UNITS):
                unit = p * UNITS + u
                if last:
                    sp_ahead(sp, u)
                if u == 2 and not last:
                    sp.wait_ge(pv_done, p * SLOTS + 2 * KT)
                    sp_load_head(sp, p + 1, 0)
                blocks = range(u * len(PROJ_SLOTS), (u + 1) * len(PROJ_SLOTS)) if u < 2 and not last else []
                if not (first and u == 0):
                    sp_den(sp, unit - 1)
                for n in blocks[:1]:
                    sp_proj(sp, n, p + 1, PROJ_JOBS * p + n)
                if not (first and u == 0):
                    sp_rec(sp, unit - 1)
                for n in blocks[1:]:
                    sp_proj(sp, n, p + 1, PROJ_JOBS * p + n)
                if not (last and u == UNITS - 1):
                    sp_mrow(sp, unit + 1, *divmod((u + 1) % UNITS, 2))
                if not (first and u == 0):
                    sp_store_o(sp, unit - 1, p if u else p - 1, (u - 1) % UNITS)

        G.last_den = lambda sp: sp_den(sp, NP * UNITS - 1)
        G.last_dve_rec = lambda dve: dve_rec(dve, NP * UNITS - 1)
        G.last_sp_rec = lambda sp: sp_rec(sp, NP * UNITS - 1)
        G.last_norm = lambda dve: dve_norm(dve, NP * UNITS - 1, UNITS - 1)

        def last_store(sp):
            sp_store_o(sp, NP * UNITS - 1, NP - 1, UNITS - 1)
            sp.wait_ge(o_stored[1], 64 * NP)
        G.last_store = last_store

        with nc.Block() as block:

            @block.sync
            def _(sp):
                sp_load_head(sp, 0, 0)
                sp_mrow(sp, 0, 0, 0)
                sp_load_head(sp, 0, 1)
                sp_pair(sp, 0, first=True)
                with sp.Fori(1, NP - 1) as p:
                    sp_pair(sp, p)
                sp_pair(sp, NP - 1, last=True)
                for b in range(2):
                    sp.wait_ge(o_stored[b], 64 * NP - 32 * b)
                sp.wait_ge(G.ot_ahead, 16)

            @block.tensor
            def _(pe):
                pe_maxt(pe, 0)
                for j, ahead in [(j, 1) for j, at in rough_places() if at // PLACES < MAHEAD]:
                    pe_rough(pe, 0, 1, j, MJOBS + j)
                pe_pair(pe, 0, first=True)
                with pe.Fori(1, NP - 1) as p:
                    pe_pair(pe, p)
                pe_pair(pe, NP - 1, last=True)
                for g in range(SLOTS - LAG, SLOTS):
                    pe_pv(pe, g, (NP - 1) * SLOTS + g, NP * UNITS - 1, NP - 1)
                pe.wait_ge(den_copied, NP * UNITS - 1)
                pe_den(pe, UNITS - 1, NP * UNITS - 1)

            @block.scalar
            def _(act):
                act_mrow(act, 0)
                act_pair(act, 0, first=True)
                with act.Fori(1, NP - 1) as p:
                    act_pair(act, p)
                act_pair(act, NP - 1, last=True)
                act_o(act, NP * UNITS - 1)
                act_den(act, NP * UNITS - 1)

            @block.vector
            def _(dve):
                dve_max(dve, 0)
                for j, ahead in [(j, 1) for j, at in rough_places() if at // PLACES < MAHEAD]:
                    dve_rough(dve, j, 1, MJOBS + j)
                dve_pair(dve, 0, first=True)
                with dve.Fori(1, NP - 1) as p:
                    dve_pair(dve, p)
                dve_pair(dve, NP - 1, last=True)
                add_tile(dve, ND - 1, UNITS - 1, NP * UNITS - 1, NP * SLOTS - KT, dve=True)

            @block.gpsimd
            def _(pool):
                pool_pair(pool, 0, first=True)
                with pool.Fori(1, NP) as p:
                    pool_pair(pool, p)
                pool_join(pool, UNITS - 1, NP * UNITS - 1)


def phase_output(nc, S, A, G, sem, out):
    TT, D, E, NP, QC = S.TT, S.D, S.E, S.NP, S.QC
    BT = QC // P
    NB = TT // BT
    HN = 5 * NP // 8
    with ExitStack() as ctx:
        def sb(name, shape, dt=F32):
            return ctx.enter_context(nc.sbuf_tensor(name, shape, dt))

        wo_hi, wo_lo = G.wo_hi, G.wo_lo
        ot = [G.ot0, sb("ot1", [P, NP, QC])[:]]
        bo_sb = sb("bo_sb", [P, D])
        ot_hi = [sb(f"ot_hi{b}", [P, NP, QC], F32R) for b in range(2)]
        ot_lo = [sb(f"ot_lo{b}", [P, NP, QC], F32R) for b in range(2)]
        x1 = sb("x1", [P, TT, D])
        xn = sb("xn2", [P, TT, D + E])
        xn_t = sb("xn_t", [P, S.KD, QC])
        rw_in = sb("rw_in", [E, D])
        rw_t = sb("rw_t", [P, S.KD, E])
        b1_in = sb("b1_in", [E * S.HT, P])
        stats, mv = sb("ln2_stats", [P, TT, 6]), sb("ln2_mv", [P, TT, 2])
        std, rstd, nt, eps = sb("ln2_std", [P, TT]), sb("ln2_rstd", [P, TT]), sb("ln2_nt", [P, TT]), sb("ln2_eps", [P, 1])
        lg = sb("lg", [P, TT, E])
        lmax, lsum, lrec = sb("lmax", [P, TT]), sb("lsum", [P, TT]), sb("lrec", [P, TT])
        ps_y = ctx.enter_context(nc.psum_tensor("ps_out", [P, 2, QC], F32))
        ps_t = ctx.enter_context(nc.psum_tensor("ps_out_t", [P, 2, QC], F32))
        ps_l = ctx.enter_context(nc.psum_tensor("ps_logits", [P, TT, E], F32))
        ps_r = ctx.enter_context(nc.psum_tensor("ps_small", [P, QC], F32))

        bo_loaded, small_loaded = sem("bo_loaded"), sem("small_loaded")
        x_loaded = [sem(f"x_loaded{b}") for b in range(NB)]
        ot_loaded = [sem(f"ot_loaded{b}") for b in range(2)]
        ot_hi_done, ot_lo_dve, ot_lo_pool = sem("ot_hi_done"), sem("ot_lo_dve"), sem("ot_lo_pool")
        biased, eps_set = sem("biased"), sem("eps_set")
        y_ready, x1_done = sem("y_ready"), sem("x1_done")
        stats_done, mv_done, std_done, rstd_done, xn_done = (sem(f"ln2_{n}_done") for n in ("stats", "mv", "std", "rstd", "xn"))
        small_t, small_copied = sem("small_t"), sem("small_copied")
        t_ready, t_copied, logits_ready = sem("xn_t_ready"), sem("xn_t_copied"), sem("logits_ready")
        softmax, exp_l = sem("softmax_steps"), sem("logits_exp")
        x1_stored, table_stored = sem("x1_stored"), sem("table_stored")

        xv = A["x"][0].rearrange("(t p) d -> p t d", p=P)
        ov = out[0].rearrange("(t p) d -> p t d", p=P)
        tv = G.table.rearrange("(t p) d -> p t d", p=P)

        with nc.Block() as block:

            @block.sync
            def _(sp):
                def load_ot(b, pairs):
                    sp.dma_start(ot[b % 2][:, pairs, :], G.o_scr[pairs, :, b * QC:(b + 1) * QC].rearrange("h p q -> p h q")).then_inc(ot_loaded[b % 2], 16)

                G.last_den(sp)
                load_ot(0, slice(NP - 1, NP))
                load_ot(1, slice(0, NP))
                sp.dma_start(bo_sb[:], A["bo"].rearrange("(o n) -> o n", o=1).to_broadcast([P, D])).then_inc(bo_loaded, 16)
                for b in range(NB):
                    sp.dma_start(x1[:, b * BT:(b + 1) * BT, :], xv[:, b * BT:(b + 1) * BT, :]).then_inc(x_loaded[b], 16)
                    if b == 0:
                        sp.dma_start(rw_in[:], A["router_w"]).then_inc(small_loaded, 16)
                        sp.dma_start(b1_in[:], A["b1"].rearrange("e (h p) -> (e h) p", p=P)).then_inc(small_loaded, 16)
                G.last_sp_rec(sp)
                G.last_store(sp)
                for b in range(2, NB):
                    sp.wait_ge(ot_hi_done, 2 * (b - 1))
                    sp.wait_ge(ot_lo_dve, b - 1)
                    sp.wait_ge(ot_lo_pool, b - 1)
                    load_ot(b, slice(0, NP))
                for b in range(NB):
                    sp.wait_ge(x1_done, (b + 1) * BT)
                    sp.dma_start(ov[:, b * BT:(b + 1) * BT, :], x1[:, b * BT:(b + 1) * BT, :]).then_inc(x1_stored, 16)
                    sp.wait_ge(xn_done, (b + 1) * BT)
                    sp.dma_start(tv[:, b * BT:(b + 1) * BT, 0:D], xn[:, b * BT:(b + 1) * BT, 0:D]).then_inc(table_stored, 16)
                sp.wait_ge(softmax, 5)
                sp.dma_start(tv[:, :, D:D + E], xn[:, :, D:D + E]).then_inc(table_stored, 16)
                sp.wait_ge(x1_stored, 16 * NB)
                sp.wait_ge(table_stored, 16 * NB + 16)

            @block.gpsimd
            def _(pool):
                def bias(b):
                    pool.wait_ge(x_loaded[b], 16)
                    pool.tensor_tensor(x1[:, b * BT:(b + 1) * BT, :], x1[:, b * BT:(b + 1) * BT, :],
                                       bo_sb[:, None, :].to_broadcast([P, BT, D]), ALU.add).then_inc(biased, 1)

                def lo(b):
                    pool.wait_ge(ot_hi_done, 2 * b + 2)
                    if b >= 2:
                        pool.wait_ge(y_ready, (b - 1) * BT)
                    pool.tensor_tensor(ot_lo[b % 2][:, HN:NP, :], ot[b % 2][:, HN:NP, :], raw(ot_hi[b % 2][:, HN:NP, :]),
                                       ALU.subtract).then_inc(ot_lo_pool, 1)

                lo(0)
                pool.wait_ge(bo_loaded, 16)
                bias(0)
                for b in range(1, NB):
                    lo(b)
                    bias(b)

            @block.scalar
            def _(act):
                def hi(b):
                    if b >= 2:
                        act.wait_ge(y_ready, (b - 1) * BT)
                    if b >= 1:
                        act.wait_ge(ot_loaded[b % 2], 16 * (b // 2 + 1))
                    act.activation(ot_hi[b % 2][:, 0:HN, :], ot[b % 2][:, 0:HN, :], ACT.Copy).then_inc(ot_hi_done, 1)
                    if b == 0:
                        act.wait_ge(ot_loaded[b], 16)
                    act.activation(ot_hi[b % 2][:, HN:NP, :], ot[b % 2][:, HN:NP, :], ACT.Copy).then_inc(ot_hi_done, 1)

                hi(0)
                hi(1)
                act.wait_ge(small_t, 1)
                act.activation(rw_t[:].rearrange("p k e -> p (k e)"), ps_r[:, 0:S.KD * E], ACT.Copy).then_inc(small_copied, 1)
                act.activation(G.b1_t[:], ps_r[:, S.KD * E:S.KD * E + E * S.HT], ACT.Copy).then_inc(small_copied, 1)
                act.wait_ge(eps_set, 1)
                for b in range(NB):
                    act.wait_ge(mv_done, (b + 1) * BT)
                    act.activation(std[:, b * BT:(b + 1) * BT], mv[:, b * BT:(b + 1) * BT, 1], ACT.Sqrt,
                                   bias=eps[:, 0:1]).then_inc(std_done, 1)
                    if b + 2 < NB:
                        hi(b + 2)
                    act.wait_ge(t_ready, b + 1)
                    if b >= 1:
                        act.wait_ge(logits_ready, b)
                    act.activation(xn_t[:], ps_t[:], ACT.Copy).then_inc(t_copied, 1)
                act.wait_ge(softmax, 2)
                act.activation(lg[:], lg[:], ACT.Exp).then_inc(exp_l, 1)

            @block.vector
            def _(dve):
                def lo(b):
                    dve.wait_ge(ot_hi_done, 2 * b + 1)
                    if b >= 2:
                        dve.wait_ge(y_ready, (b - 1) * BT)
                    dve.tensor_tensor(ot_lo[b % 2][:, 0:HN, :], ot[b % 2][:, 0:HN, :], raw(ot_hi[b % 2][:, 0:HN, :]),
                                      ALU.subtract).then_inc(ot_lo_dve, 1)

                dve.memset(eps[:], EPS).then_inc(eps_set, 1)
                lo(0)
                G.last_dve_rec(dve)
                lo(1)
                for b in range(NB):
                    dve.wait_ge(biased, b + 1)
                    for t in range(b * BT, (b + 1) * BT):
                        dve.wait_ge(y_ready, t + 1)
                        dve.tensor_tensor(x1[:, t, :], ps_y[:, t % 2, 0:D], x1[:, t, :], ALU.add).then_inc(x1_done, 1)
                        if t == 1:
                            G.last_norm(dve)
                        if t % BT == 1 and 2 <= b + 1 < NB:
                            lo(b + 1)
                        dve.wait_ge(x1_done, t + 1)
                        dve.bn_stats(stats[:, t, :], x1[:, t, :]).then_inc(stats_done, 1)
                        dve.wait_ge(stats_done, t + 1)
                        dve.bn_aggr(mv[:, t, :], stats[:, t, :]).then_inc(mv_done, 1)
                    g = slice(b * BT, (b + 1) * BT)
                    dve.wait_ge(std_done, b + 1)
                    dve.reciprocal(rstd[:, g], std[:, g]).then_inc(rstd_done, 1)
                    dve.wait_ge(rstd_done, 5 * b + 1)
                    refine_rstd(dve, mv[:, g, 1], rstd[:, g], nt[:, g], rstd_done, 5 * b + 1)
                    for t in range(b * BT, (b + 1) * BT):
                        dve.tensor_scalar(xn[:, t, 0:D], x1[:, t, :], mv[:, t, 0:1], rstd[:, t:t + 1],
                                          ALU.subtract, ALU.mult).then_inc(xn_done, 1)
                dve.wait_ge(logits_ready, NB)
                dve.tensor_reduce(lmax[:], ps_l[:], AX.X, ALU.max).then_inc(softmax, 1)
                dve.wait_ge(softmax, 1)
                dve.tensor_tensor(lg[:], ps_l[:], lmax[:, :, None].to_broadcast([P, TT, E]), ALU.subtract).then_inc(softmax, 1)
                dve.wait_ge(exp_l, 1)
                dve.tensor_reduce(lsum[:], lg[:], AX.X, ALU.add).then_inc(softmax, 1)
                dve.wait_ge(softmax, 3)
                dve.reciprocal(lrec[:], lsum[:]).then_inc(softmax, 1)
                dve.wait_ge(softmax, 4)
                dve.tensor_tensor(xn[:, :, D:D + E], lg[:], lrec[:, :, None].to_broadcast([P, TT, E]), ALU.mult).then_inc(softmax, 1)
                dve.tensor_tensor(G.scores[:], lg[:].rearrange("p t e -> p e t"), lrec[:, None, :].to_broadcast([P, E, TT]),
                                  ALU.mult).then_inc(softmax, 1)

            @block.tensor
            def _(pe):
                def transposes(b):
                    pe.wait_ge(xn_done, (b + 1) * BT)
                    if b >= 1:
                        pe.wait_ge(t_copied, b)
                    for k in range(S.KD):
                        for i in range(BT):
                            last = pe.transpose(ps_t[:, k, i * P:(i + 1) * P], xn[:, b * BT + i, k * P:(k + 1) * P], G.ident[:])
                    last.then_inc(t_ready, 1)

                def logits(b):
                    pe.wait_ge(t_copied, b + 1)
                    for i in range(BT):
                        for k in range(S.KD):
                            last = pe.matmul(ps_l[:, b * BT + i, :], xn_t[:, k, i * P:(i + 1) * P], rw_t[:, k, :],
                                             start=(k == 0), stop=(k == S.KD - 1))
                    last.then_inc(logits_ready, 1)

                def small():
                    pe.wait_ge(small_loaded, 32)
                    for k in range(S.KD):
                        pe.transpose(ps_r[:, k * E:(k + 1) * E], rw_in[:, k * P:(k + 1) * P], G.ident[0:E, 0:E])
                    pe.transpose(ps_r[:, S.KD * E:S.KD * E + E * S.HT], b1_in[:], G.ident[0:E * S.HT, 0:E * S.HT]).then_inc(small_t, 1)

                for b in range(NB):
                    pe.wait_ge(ot_hi_done, 2 * b + 1)
                    pe.wait_ge(ot_lo_dve, b + 1)
                    for i in range(BT):
                        t = b * BT + i
                        if t >= 2:
                            pe.wait_ge(x1_done, t - 1)
                        cols = slice(i * P, (i + 1) * P)
                        n = 0
                        for h in range(NP):
                            if i == 0 and h == HN:
                                pe.wait_ge(ot_hi_done, 2 * b + 2)
                                pe.wait_ge(ot_lo_pool, b + 1)
                            for o, w in ((ot_hi[b % 2], wo_hi), (ot_hi[b % 2], wo_lo), (ot_lo[b % 2], wo_hi)):
                                last = pe.matmul(ps_y[:, t % 2, 0:D], o[:, h, cols], w[:, h, :], start=(n == 0), stop=(n == 3 * NP - 1))
                                n += 1
                        last.then_inc(y_ready, 1)
                        if i == 1 and b == 0:
                            small()
                        if i == 2 and b >= 1:
                            transposes(b - 1)
                        if i == 3 and b >= 1:
                            if b == 1:
                                pe.wait_ge(small_copied, 2)
                            logits(b - 1)
                transposes(NB - 1)
                logits(NB - 1)


RT = 104
SEARCH_BITS = 30


def phase_experts(nc, S, A, G, sem, out):
    TT, D, E, HT, KD, CAP = S.TT, S.D, S.E, S.HT, S.KD, S.CAP
    ST = -(-CAP // RT)
    TAIL = CAP - (ST - 1) * RT
    NS = CAP + 3 - (CAP + 3) % 4
    HS = NS // 2
    ROUNDS = SEARCH_BITS // 2
    TJ = 3
    assert E * TT == P and TAIL % 2 == 1 and NS <= ST * RT and HS % 2 == 0
    rows = [RT] * (ST - 1) + [TAIL]
    with ExitStack() as ctx:
        def sb(name, shape, dt=F32):
            return ctx.enter_context(nc.sbuf_tensor(name, shape, dt))

        def ps(name, shape):
            return ctx.enter_context(nc.psum_tensor(name, shape, F32))

        scores_t = sb("scores_t", [P, P])
        cand = sb("cand", [P, 4], I32)
        step = sb("step", [P, 3], I32)
        reached = sb("reached", [P, 3, P], BF16)
        part = sb("part", [P, 3], BF16)
        thr_all = sb("thr_all", [P, P])
        ones_b = sb("ones_b", [P, P], BF16)
        same = sb("same", [P, E, TT], BF16)
        before = sb("before", [P, P], BF16)
        mask = sb("mask", [P, 2, E, TT], BF16)
        cnt = sb("cnt", [P, E], BF16)
        need = sb("need", [P, E])
        tie, sel, pos = sb("tie", [P, E, TT]), sb("sel", [P, E, TT]), sb("pos", [P, E, TT])
        tile_no, slot = sb("tile_no", [P, E, TT]), sb("slot", [P, E, TT], BF16)
        iota_i = sb("iota_i", [P, P], I32)
        iota_r = sb("iota_r", [P, RT], BF16)
        iota_p = sb("iota_p", [P, 1])
        tile_hot = sb("tile_hot", [P, TT, ST])
        ids = [sb(f"ids{b}", [P, TT, 2, ST], BF16) for b in range(2)]
        row_hot = [sb(f"row_hot{b}", [P, TT, RT], BF16) for b in range(2)]
        idx_g = [sb(f"idx_g{b}", [RT, ST], I32) for b in range(2)]
        idx_s = [sb(f"idx_s{b}", [RT, ST], I32) for b in range(2)]
        w1_in = [sb(f"w1_in{b}", [P, KD, S.HID]) for b in range(2)]
        w2_in = [sb(f"w2_in{b}", [P, HT, D]) for b in range(2)]
        w1_hi = [sb(f"w1_hi{b}", [P, KD, S.HID], F32R) for b in range(2)]
        w1_lo = [sb(f"w1_lo{b}", [P, KD, S.HID], F32R) for b in range(2)]
        w2_hi = [sb(f"w2_hi{b}", [P, HT, D], F32R) for b in range(2)]
        w2_lo = [sb(f"w2_lo{b}", [P, HT, D], F32R) for b in range(2)]
        b2_sb = sb("b2_sb", [RT, E, D])
        xg = [sb(f"xg{b}", [RT, ST, D + E]) for b in range(2)]
        xt_hi, xt_lo = sb("xgt_hi", [P, KD, ST * RT], F32R), sb("xgt_lo", [P, KD, ST * RT], F32R)
        h_f = sb("h_f", [P, 2, NS])
        h_hi, h_lo = sb("h_hi", [P, HT, NS], F32R), sb("h_lo", [P, HT, NS], F32R)
        y_sb = [sb(f"y_sb{b}", [RT, ST, D]) for b in range(2)]
        ps_h = ps("ps_h", [P, 2, 2, 512])
        ps_y = ps("ps_y2", [P, 2, 512])
        ps_t = ps("ps_xgt", [P, 2, 512])
        ps_c, ps_pre, ps_i = ps_y, ps_t[:, 0, 0:2 * P], ps_t[:, 1, 0:2 * ST]

        consts, masks_set = sem("consts"), sem("masks_set")
        srch, counted, parts_ready, turned, thr_spread = (sem(n) for n in ("srch", "counted", "parts_ready", "turned", "thr_spread"))
        counts_ready, ranks = sem("counts_ready"), sem("ranks_ready")
        hot_ready, list_ready, idx_ready, idx_kept = sem("hot_ready"), sem("list_ready"), sem("idx_ready"), sem("idx_kept")
        w1_loaded = [sem(f"w1_loaded{b}") for b in range(2)]
        w2_loaded = [sem(f"w2_loaded{b}") for b in range(2)]
        b2_loaded = sem("b2_loaded")
        w1_hi_done, w1_lo_done, w2_hi_done, w2_lo_done = (sem(n) for n in ("w1_hi_done", "w1_lo_done", "w2_hi_done", "w2_lo_done"))
        gathered = [sem(f"gathered{b}") for b in range(2)]
        scattered = [sem(f"scattered{b}") for b in range(2)]
        xgt_ready, xgt_hi_done, xgt_lo_done, padded = sem("xgt_ready"), sem("xgt_hi_done"), sem("xgt_lo_done"), sem("xgt_padded")
        h_ready, gelu_done, h_hi_done, h_lo_done = sem("h_ready"), sem("gelu_done"), sem("h_hi_done"), sem("h_lo_done")
        y_ready, y_read, y_done = sem("y2_ready"), sem("y2_read"), sem("y2_done")

        def sp_weights(sp, e, i, b):
            wait_for(sp, w1_lo_done, e - 1)
            sp.dma_start(w1_in[b][:], w1v(e)).then_inc(w1_loaded[b], 16)
            wait_for(sp, w2_lo_done, e - 1)
            sp.dma_start(w2_in[b][:], w2v(e)).then_inc(w2_loaded[b], 16)

        def w1v(e):
            return (A["w1"][e:e + 1] if isinstance(e, int) else A["w1"][bass.ds(e, 1)]).rearrange("o (k p) n -> p (o k) n", p=P)

        def w2v(e):
            return (A["w2"][e:e + 1] if isinstance(e, int) else A["w2"][bass.ds(e, 1)]).rearrange("o (h p) n -> p (o h) n", p=P)

        def at(e):
            return slice(e, e + 1) if isinstance(e, int) else bass.ds(e, 1)

        def act_w1_hi(act, e, i, b):
            act.wait_ge(w1_loaded[b], 16 * (i + 1))
            wait_for(act, h_ready, HT * (e - 1))
            act.activation(w1_hi[b][:], w1_in[b][:], ACT.Copy).then_inc(w1_hi_done, 1)

        def act_w2_hi(act, e, i, b):
            act.wait_ge(w2_loaded[b], 16 * (i + 1))
            wait_for(act, y_ready, ST * (e - 1))
            act.activation(w2_hi[b][:], w2_in[b][:], ACT.Copy).then_inc(w2_hi_done, 1)

        def pool_lo(pool, e, b):
            pool.wait_ge(w1_hi_done, e + 1)
            pool.tensor_tensor(w1_lo[b][:], w1_in[b][:], raw(w1_hi[b][:]), ALU.subtract).then_inc(w1_lo_done, 1)
            pool.wait_ge(w2_hi_done, e + 1)
            pool.tensor_tensor(w2_lo[b][:], w2_in[b][:], raw(w2_hi[b][:]), ALU.subtract).then_inc(w2_lo_done, 1)

        def dve_hot(dve, e, b):
            wait_for(dve, list_ready, e - 1)
            wait_for(dve, ids_made, 2 * e)
            dve.tensor_tensor(tile_hot[:], tile_no[:, at(e), :].rearrange("p o t -> p (o t)")[:, :, None].to_broadcast([P, TT, ST]),
                              iota_r[:, None, 0:ST].to_broadcast([P, TT, ST]), ALU.is_equal).then_inc(tile_hot_made, 1)
            dve.wait_ge(tile_hot_made, e + 1)
            dve.tensor_tensor(ids[b][:, :, 0, :], tile_hot[:], iota_r[:, 0:TT, None].to_broadcast([P, TT, ST]), ALU.mult).then_inc(ids_made, 1)
            dve.tensor_scalar(ids[b][:, :, 1, :], tile_hot[:], iota_p[:, 0:1], None, ALU.mult).then_inc(ids_made, 1)
            dve.tensor_tensor(row_hot[b][:], slot[:, at(e), :].rearrange("p o t -> p (o t)")[:, :, None].to_broadcast([P, TT, RT]),
                              iota_r[:, None, :].to_broadcast([P, TT, RT]), ALU.is_equal).then_inc(hot_ready, 1)

        def pe_list(pe, e, b):
            pe.wait_ge(ids_made, 2 * e + 2)
            pe.wait_ge(hot_ready, e + 1)
            wait_for(pe, xgt_lo_done, TJ * e - 1)
            for t in range(TT):
                last = pe.matmul(ps_i[0:RT, :], row_hot[b][:, t, :], ids[b][:, t, :, :].rearrange("p a j -> p (a j)"),
                                 start=(t == 0), stop=(t == TT - 1))
            last.then_inc(list_ready, 1)

        def dve_index(dve, e, i, b):
            dve.wait_ge(list_ready, e + 1)
            wait_for(dve, gathered[b], 16 * ST * i)
            wait_for(dve, idx_kept, e - 1)
            dve.tensor_scalar(idx_f[:], ps_i[0:RT, 0:ST], float(P), None, ALU.mult).then_inc(idx_mul, 1)
            dve.wait_ge(idx_mul, e + 1)
            dve.tensor_tensor(idx_g[b][:], ps_i[0:RT, ST:2 * ST], idx_f[:], ALU.add).then_inc(idx_ready, 1)

        tile_hot_made, ids_made = sem("tile_hot_made"), sem("ids_made")
        idx_f, idx_mul = sb("idx_f", [RT, ST]), sem("idx_mul")

        def pool_gather(pool, e, i, b):
            pool.wait_ge(idx_ready, e + 1)
            wait_for(pool, xgt_ready, TJ * (e - 1))
            wait_for(pool, y_done, ST * (e - 1))
            for j, n in enumerate(rows):
                pool.indirect_dma_start(xg[b][0:n, j, :], None, G.table,
                                        bass.IndirectOffsetOnAxis(ap=idx_g[b][0:n, j:j + 1], axis=0)).then_inc(gathered[b], 16)

        groups = [(0, [(j, 0) for j in range(ST - 1)]), (1, [(j, 1) for j in range(ST - 1)]), (0, [(ST - 1, 0), (ST - 1, 1)])]
        FULL = (ST - 1) * RT

        def xgt_views(n):
            if n < 2:
                return ps_t[:, n, 0:FULL], xt_hi[:, n, 0:FULL], xt_lo[:, n, 0:FULL]
            return (ps_t[:, 0, 0:2 * RT].rearrange("p (k c) -> p k c", k=2)[:, :, 0:TAIL],
                    xt_hi[:, :, FULL:FULL + TAIL], xt_lo[:, :, FULL:FULL + TAIL])

        def pe_xgt(pe, e, i, b, n):
            if n == 0:
                pe.wait_ge(gathered[b], 16 * ST * (i + 1))
                wait_for(pe, xgt_lo_done, TJ * e)
            elif n == 1:
                pe.wait_ge(idx_ready, e + 1)
            else:
                pe.wait_ge(xgt_lo_done, TJ * e + 1)
            bank, tiles = groups[n]
            for c, (j, k) in enumerate(tiles):
                r = rows[j]
                last = pe.transpose(ps_t[:, bank, c * RT:c * RT + r], xg[b][0:r, j, k * P:(k + 1) * P], G.ident[0:r, 0:r])
            last.then_inc(xgt_ready, 1)

        def act_xgt(act, e, n):
            act.wait_ge(xgt_ready, TJ * e + n + 1)
            src, hi, _ = xgt_views(n)
            act.activation(hi, src, ACT.Copy).then_inc(xgt_hi_done, 1)

        def dve_xgt(dve, e, n):
            dve.wait_ge(xgt_hi_done, TJ * e + n + 1)
            src, hi, lo = xgt_views(n)
            dve.tensor_tensor(lo, src, raw(hi), ALU.subtract).then_inc(xgt_lo_done, 1)

        def pe_h(pe, e, b, h):
            if h == 0:
                pe.wait_ge(w1_lo_done, e + 1)
                pe.wait_ge(xgt_lo_done, TJ * (e + 1))
            wait_for(pe, gelu_done, HT * e + h - 1)
            cols = slice(h * P, (h + 1) * P)
            terms = [(w, x, k) for k in range(KD) for w, x in ((w1_hi[b], xt_hi), (w1_hi[b], xt_lo), (w1_lo[b], xt_hi))]
            for c in range(2):
                for n, (w, x, k) in enumerate(terms):
                    last = pe.matmul(ps_h[:, h % 2, c, 0:HS], w[:, k, cols], x[:, k, c * HS:(c + 1) * HS],
                                     start=(n == 0), stop=(n == len(terms) - 1))
            last.then_inc(h_ready, 1)

        def act_h(act, e, h):
            act.wait_ge(h_ready, HT * e + h + 1)
            wait_for(act, h_lo_done, HT * e + h - 1)
            act.activation(h_f[:, h % 2, :].rearrange("p (c n) -> p c n", c=2), ps_h[:, h % 2, :, 0:HS], ACT.Gelu,
                           bias=G.b1_t[:, b1_col(e, h)]).then_inc(gelu_done, 1)
            act.wait_ge(gelu_done, HT * e + h + 1)
            act.activation(h_hi[:, h, :], h_f[:, h % 2, :], ACT.Copy).then_inc(h_hi_done, 1)

        def b1_col(e, h):
            return at(e * HT + h)

        def dve_h(dve, e, h):
            dve.wait_ge(h_hi_done, HT * e + h + 1)
            dve.tensor_tensor(h_lo[:, h, :], h_f[:, h % 2, :], raw(h_hi[:, h, :]), ALU.subtract).then_inc(h_lo_done, 1)

        def pe_y(pe, e, b, j):
            if j == 0:
                pe.wait_ge(w2_lo_done, e + 1)
            wait_for(pe, y_read, ST * e + j - 1)
            m = rows[j] + rows[j] % 2
            bank = (ST * b + j) % 2
            for h in range(HT):
                if j == 0:
                    pe.wait_ge(h_lo_done, HT * e + h + 1)
                for n, (x, w) in enumerate(((h_hi, w2_hi[b]), (h_hi, w2_lo[b]), (h_lo, w2_hi[b]))):
                    last = pe.matmul(ps_y[0:m, bank, 0:D], x[:, h, j * RT:j * RT + m], w[:, h, :],
                                     start=(h == 0 and n == 0), stop=(h == HT - 1 and n == 2))
            last.then_inc(y_ready, 1)

        def dve_y(dve, e, i, b, j):
            n = rows[j]
            dve.wait_ge(y_ready, ST * e + j + 1)
            if j == 0:
                wait_for(dve, scattered[b], 16 * ST * i)
                dve.tensor_copy(idx_s[b][:], idx_g[b][:]).then_inc(idx_kept, 1)
            dve.tensor_tensor(y_sb[b][0:n, j, :], ps_y[0:n, (ST * b + j) % 2, 0:D],
                              b2_sb[0:n, at(e), :].rearrange("p o d -> p (o d)"), ALU.add).then_inc(y_read, 1)
            dve.wait_ge(y_read, ST * e + j + 1)
            dve.tensor_scalar(y_sb[b][0:n, j, :], y_sb[b][0:n, j, :], xg[b][0:n, j, at(D + e)], None, ALU.mult).then_inc(y_done, 1)

        def pool_scatter(pool, e, i, b):
            pool.wait_ge(idx_kept, e + 1)
            wait_for(pool, scattered[1 - b], 16 * ST * (i + b))
            for j, n in enumerate(rows):
                pool.wait_ge(y_done, ST * e + j + 1)
                pool.indirect_dma_start(out[0], bass.IndirectOffsetOnAxis(ap=idx_s[b][0:n, j:j + 1], axis=0),
                                        y_sb[b][0:n, j, :], None, compute_op=ALU.add).then_inc(scattered[b], 16)

        def nxt(i, b):
            return i + b, 1 - b

        def pe_expert(pe, e, i, b, last):
            for h in range(HT):
                pe_h(pe, e, b, h)
                if h == 0 and not last:
                    pe_list(pe, e + 1, 1 - b)
            for j in range(ST):
                pe_y(pe, e, b, j)
                if not last:
                    for n in {0: (0, 1), 1: (2,)}.get(j, ()):
                        pe_xgt(pe, e + 1, *nxt(i, b), n)

        def act_expert(act, e, i, b, last):
            for h in range(HT):
                act_h(act, e, h)
            if not last:
                act_w1_hi(act, e + 1, *nxt(i, b))
                for n in range(TJ):
                    act_xgt(act, e + 1, n)
                act_w2_hi(act, e + 1, *nxt(i, b))

        def dve_expert(dve, e, i, b, last):
            hot = not (isinstance(e, int) and e + 2 >= E)
            for h in range(HT):
                dve_h(dve, e, h)
                if h == 1 and not last:
                    dve_index(dve, e + 1, *nxt(i, b))
            for j in range(ST):
                dve_y(dve, e, i, b, j)
                if not last:
                    for n in {0: (0, 1), 1: (2,)}.get(j, ()):
                        dve_xgt(dve, e + 1, n)
                if j == 2 and hot:
                    dve_hot(dve, e + 2, b)

        def pool_expert(pool, e, i, b, last):
            if not (isinstance(e, int) and e == 0):
                pool_scatter(pool, e - 1, i - 1 + b, 1 - b)
            if not last:
                pool_gather(pool, e + 1, *nxt(i, b))
                pool_lo(pool, e + 1, 1 - b)

        def all_experts(eng, expert):
            for b in range(2):
                expert(eng, b, 0, b, False)
            with eng.Fori(1, E // 2 - 1) as i:
                for b in range(2):
                    expert(eng, 2 * i + b, i, b, False)
            for b in range(2):
                expert(eng, E - 2 + b, E // 2 - 1, b, b == 1)

        UNROLL = 3
        assert ROUNDS % UNROLL == 0
        STEPS = 4

        with nc.Block() as block:

            @block.sync
            def _(sp):
                sp_weights(sp, 0, 0, 0)
                sp_weights(sp, 1, 0, 1)
                sp.dma_start(b2_sb[:], A["b2"].rearrange("(o e) n -> o (e n)", o=1).to_broadcast([RT, E * D])
                             .rearrange("p (e n) -> p e n", e=E)).then_inc(b2_loaded, 16)
                with sp.Fori(1, E // 2) as i:
                    for b in range(2):
                        sp_weights(sp, 2 * i + b, i, b)

            @block.gpsimd
            def _(pool):
                pool.memset(step[:, 0:1], 1 << (SEARCH_BITS - 2)).then_inc(consts, 1)
                pool.memset(step[:, 1:2], 2 << (SEARCH_BITS - 2)).then_inc(consts, 1)
                pool.memset(step[:, 2:3], 3 << (SEARCH_BITS - 2)).then_inc(consts, 1)
                pool.memset(cand[:], 0).then_inc(consts, 1)
                pool.memset(ones_b[:], 1.0).then_inc(consts, 1)
                pool.memset(same[:], 1.0).then_inc(consts, 1)
                pool.wait_ge(consts, 6)
                pool.affine_select(out=same[:], in_=same[:], compare_op=ALU.is_ge, fill=0.0, base=0,
                                   pattern=[[-TT, E], [0, TT]], channel_multiplier=1).then_inc(consts, 1)
                pool.wait_ge(consts, 7)
                pool.affine_select(out=same[:], in_=same[:], compare_op=ALU.is_ge, fill=0.0, base=TT - 1,
                                   pattern=[[TT, E], [0, TT]], channel_multiplier=-1).then_inc(consts, 1)
                pool.memset(before[:], 1.0).then_inc(masks_set, 1)
                pool.wait_ge(masks_set, 1)
                pool.affine_select(out=before[:], in_=before[:], compare_op=ALU.is_gt, fill=0.0, base=0,
                                   pattern=[[1, P]], channel_multiplier=-1).then_inc(masks_set, 1)
                pool.iota(iota_i[:], pattern=[[1, P]], base=0, channel_multiplier=0).then_inc(masks_set, 1)
                pool.wait_ge(masks_set, 3)
                pool.tensor_copy(iota_r[:], iota_i[:, 0:RT]).then_inc(masks_set, 1)
                pool.wait_ge(masks_set, 4)
                pool.iota(iota_i[:, 0:1], pattern=[[0, 1]], base=0, channel_multiplier=1).then_inc(masks_set, 1)
                pool.wait_ge(masks_set, 5)
                pool.tensor_copy(iota_p[:], iota_i[:, 0:1]).then_inc(masks_set, 1)
                pool.memset(raw(xt_hi[:, :, CAP:NS]), 0.0).then_inc(padded, 1)
                pool.memset(raw(xt_lo[:, :, CAP:NS]), 0.0).then_inc(padded, 1)
                pool_lo(pool, 0, 0)
                pool_gather(pool, 0, 0, 0)
                for e in range(E):
                    pool_expert(pool, e, e // 2, e % 2, e == E - 1)
                pool_scatter(pool, E - 1, E // 2 - 1, 1)
                for b in range(2):
                    pool.wait_ge(scattered[b], 16 * ST * (E // 2))

            @block.scalar
            def _(act):
                act_w1_hi(act, 0, 0, 0)
                act_w2_hi(act, 0, 0, 0)
                for n in range(TJ):
                    act_xgt(act, 0, n)
                all_experts(act, act_expert)

            @block.tensor
            def _(pe):
                pe.transpose(ps_c[:, 1, 0:P], G.scores[:].rearrange("p e t -> p (e t)"), G.ident[:]).then_inc(turned, 1)
                pe.wait_ge(consts, 8)
                with pe.Fori(0, ROUNDS // UNROLL) as group:
                    for k in range(UNROLL):
                        pe.wait_ge(parts_ready, 3 * (group * UNROLL + k + 1))
                        pe.matmul(ps_c[:, 0, 0:3], same[:].rearrange("p e t -> p (e t)"), part[:], start=True,
                                  stop=True).then_inc(counts_ready, 1)
                pe.wait_ge(thr_spread, 1)
                pe.transpose(ps_c[:, 1, 0:P], thr_all[:], G.ident[:]).then_inc(turned, 1)
                pe.wait_ge(masks_set, 2)
                pe.wait_ge(ranks, 3)
                pe.matmul(ps_c[:, 0, 0:E], ones_b[:], cnt[:], start=True, stop=True).then_inc(counts_ready, 1)
                flat = mask[:].rearrange("p a e t -> p (a e) t")
                pre = ps_pre.rearrange("p (a t) -> p a t", t=TT)
                pe.matmul(pre, before[:], flat, start=True, stop=False)
                for t in range(TT - 1):
                    last = pe.matmul(pre[:, :, t + 1:TT], ones_b[:], flat[:, :, t:t + 1].to_broadcast([P, 2 * E, TT - 1 - t]),
                                     start=False, stop=(t == TT - 2))
                last.then_inc(counts_ready, 1)
                pe_list(pe, 0, 0)
                pe.wait_ge(padded, 2)
                for n in range(TJ):
                    pe_xgt(pe, 0, 0, 0, n)
                all_experts(pe, pe_expert)

            @block.vector
            def _(dve):
                dve.wait_ge(turned, 1)
                dve.tensor_copy(scores_t[:], ps_c[:, 1, 0:P]).then_inc(counted, 1)
                dve.wait_ge(counted, 1)
                dve.wait_ge(consts, 8)
                thr = cand[:].bitcast(F32)
                with dve.Fori(0, ROUNDS // UNROLL) as group:
                    for k in range(UNROLL):
                        r = group * UNROLL + k
                        base = r * STEPS
                        dve.tensor_tensor(cand[:, 1:4], cand[:, 0:1].to_broadcast([P, 3]), step[:], ALU.bitwise_or).then_inc(srch, 1)
                        dve.wait_ge(srch, base + 1)
                        for j in range(3):
                            with nc.allow_low_precision("counts of at most 128"):
                                dve.tensor_scalar(reached[:, j, :], scores_t[:], thr[:, j + 1:j + 2], None, ALU.is_ge, ALU.add,
                                                  accum_out=part[:, j:j + 1]).then_inc(parts_ready, 1)
                        dve.tensor_scalar(step[:], step[:], 2, None, ALU.logical_shift_right).then_inc(srch, 1)
                        dve.wait_ge(counts_ready, r + 1)
                        dve.scalar_tensor_tensor(out=thr[:, 1:4], in0=ps_c[:, 0, 0:3], scalar=float(CAP), in1=thr[:, 1:4],
                                                 op0=ALU.is_ge, op1=ALU.mult).then_inc(srch, 1)
                        dve.wait_ge(srch, base + 3)
                        dve.tensor_reduce(thr[:, 0:1], thr, AX.X, ALU.max).then_inc(srch, 1)
                        dve.wait_ge(srch, base + 4)
                dve.tensor_copy(thr_all[:], thr[:, 0:1].to_broadcast([P, P])).then_inc(thr_spread, 1)
                dve.wait_ge(turned, 2)
                n = 0

                def step_done(ins):
                    nonlocal n
                    n += 1
                    ins.then_inc(ranks, 1)

                limit = ps_c[:, 1, 0:P].rearrange("p (e t) -> p e t", t=TT)
                step_done(dve.tensor_tensor(mask[:, 0], G.scores[:], limit, ALU.is_gt))
                step_done(dve.tensor_tensor(mask[:, 1], G.scores[:], limit, ALU.is_equal))
                dve.wait_ge(ranks, 2)
                with nc.allow_low_precision("counts of at most 16"):
                    step_done(dve.tensor_reduce(cnt[:], mask[:, 0], AX.X, ALU.add))
                dve.wait_ge(counts_ready, ROUNDS + 1)
                step_done(dve.tensor_scalar(need[:], ps_c[:, 0, 0:E], -1.0, float(CAP), ALU.mult, ALU.add))
                dve.wait_ge(ranks, n)
                dve.wait_ge(counts_ready, ROUNDS + 2)
                above_before, equal_before = (ps_pre[:, k * P:(k + 1) * P].rearrange("p (e t) -> p e t", e=E) for k in range(2))
                need_b = need[:, :, None].to_broadcast([P, E, TT])
                step_done(dve.tensor_tensor(tie[:], equal_before, need_b, ALU.is_lt))
                step_done(dve.tensor_tensor(pos[:], equal_before, need_b, ALU.min))
                dve.wait_ge(ranks, n)
                step_done(dve.tensor_tensor(sel[:], tie[:], mask[:, 1], ALU.mult))
                step_done(dve.tensor_tensor(pos[:], pos[:], above_before, ALU.add))
                dve.wait_ge(ranks, n)
                step_done(dve.tensor_tensor(sel[:], sel[:], mask[:, 0], ALU.add))
                dve.wait_ge(ranks, n)
                step_done(dve.scalar_tensor_tensor(out=pos[:], in0=pos[:], scalar=-float(FAR), in1=sel[:], op0=ALU.add, op1=ALU.mult))
                dve.wait_ge(ranks, n)
                step_done(dve.tensor_scalar(pos[:], pos[:], float(FAR), None, ALU.add))
                dve.wait_ge(ranks, n)
                step_done(dve.tensor_scalar(tile_no[:], pos[:], float(RT), None, ALU.is_ge))
                for j in range(2, ST):
                    dve.wait_ge(ranks, n)
                    step_done(dve.scalar_tensor_tensor(out=tile_no[:], in0=pos[:], scalar=float(j * RT), in1=tile_no[:],
                                                       op0=ALU.is_ge, op1=ALU.add))
                dve.wait_ge(ranks, n)
                dve.wait_ge(masks_set, 6)
                step_done(dve.scalar_tensor_tensor(out=slot[:], in0=tile_no[:], scalar=-float(RT), in1=pos[:], op0=ALU.mult, op1=ALU.add))
                dve.wait_ge(ranks, n)
                dve_hot(dve, 0, 0)
                dve_index(dve, 0, 0, 0)
                dve_hot(dve, 1, 1)
                dve.wait_ge(b2_loaded, 16)
                for k in range(TJ):
                    dve_xgt(dve, 0, k)
                all_experts(dve, dve_expert)


FAR = 4096


class Shared:
    pass


def build(nc, A, out, debug=None):
    S = Shapes(A["x"], A["ctx"], A["wq"], A["router_w"], A["w1"])
    G = Shared()
    with ExitStack() as top:
        def sem(name):
            return top.enter_context(nc.semaphore(name))

        G.wq_scr = nc.dram_tensor("wq_scr", [S.NP, P, 2, 2, P], F32).ap()
        G.wk_scr = nc.dram_tensor("wk_scr", [S.NP, P, 2, 2, P], F32).ap()
        G.q_scr = nc.dram_tensor("q_scr", [S.NP, 2, P, S.NT], F32).ap()
        G.k_scr = nc.dram_tensor("k_scr", [S.NP, 2, P, S.NKP], F32).ap()
        G.v_scr = nc.dram_tensor("v_scr", [P, S.KT, S.DI], F32).ap()
        G.rec_scr = nc.dram_tensor("rec_scr", [2, S.QC], F32).ap()
        G.o_scr = nc.dram_tensor("o_scr", [S.NP, P, S.NT], F32).ap()
        G.table = nc.dram_tensor("table", [S.NT, S.D + S.E], F32).ap()
        G.ident = top.enter_context(nc.sbuf_tensor("ident", [P, P], F32))
        G.ones = top.enter_context(nc.sbuf_tensor("ones", [P, P], F32))
        G.pad_bias = top.enter_context(nc.sbuf_tensor("pad_bias", [P, 1], F32))
        G.scores = top.enter_context(nc.sbuf_tensor("scores", [P, S.E, S.TT], F32))
        G.b1_t = top.enter_context(nc.sbuf_tensor("b1_t", [P, S.E * S.HT], F32))
        with ExitStack() as first:
            def lasting(name, shape, dt=F32R):
                return first.enter_context(nc.sbuf_tensor(name, shape, dt))
            G.x_in = lasting("x_in", [P, S.TT, S.D], F32)
            G.wo_in = G.x_in[:, 0:S.NP, :]
            G.v_st = lasting("v_st", [P, 2, S.DI], F32)
            G.den_sb = lasting("den_sb", [P, S.QC], F32)
            G.den_c, G.rec_c = (lasting(n, [16, 2 * S.QC // 16], F32) for n in ("den_c", "rec_c"))
            G.ot0 = G.x_in[:].rearrange("p t d -> p (t d)").rearrange("p (h q) -> p h q", q=S.QC)
            G.wo_hi, G.wo_lo = lasting("wo_hi", [P, S.NP, S.D]), lasting("wo_lo", [P, S.NP, S.D])
            G.ot_ahead = sem("ot_ahead")
            with ExitStack() as att:
                def sb(name, shape, dt=F32R):
                    return att.enter_context(nc.sbuf_tensor(name, shape, dt))
                G.xt_hi, G.xt_lo = sb("xt_hi", [P, S.KD, S.NT]), sb("xt_lo", [P, S.KD, S.NT])
                G.c1_hi, G.c1_lo, G.c2 = sb("c1_hi", [P, S.NKP]), sb("c1_lo", [P, S.NKP]), sb("c2", [P, S.NKP])
                G.k2 = [sb(f"k2_{b}", [P, S.NKP]) for b in range(2)]
                G.q2 = [sb(f"q2_{b}", [P, S.NT]) for b in range(2)]
                G.k1, G.q1 = [sb("k1_0", [P, S.NKP])], [sb("q1_0", [P, S.NT])]
                G.mx_part = sb("mx_part", [P, S.UQ // P, 4], F32)
                G.rough_ready, G.rough_used = sem("rough_ready"), sem("rough_used")
                phase_prologue(nc, S, A, G, sem)
                if debug != "prologue":
                    phase_attention(nc, S, A, G, sem)
            if debug is None:
                phase_output(nc, S, A, G, sem, out)
        if debug is None:
            phase_experts(nc, S, A, G, sem, out)


_INS = {"x": "x", "ctx_768": "ctx", "L0_xattn_Wq": "wq", "L0_xattn_Wk": "wk", "L0_xattn_Wv": "wv", "L0_xattn_Wo": "wo",
        "L0_xattn_bo": "bo", "L0_ffn_router_w": "router_w", "L0_ffn_w1": "w1", "L0_ffn_b1": "b1", "L0_ffn_w2": "w2",
        "L0_ffn_b2": "b2"}


def kernel(**inputs):
    import numpy as _np
    import concourse.bacc as _bacc
    from concourse.bass_utils import run_bass_kernel_spmd as _run

    nc = _bacc.Bacc("TRN2", target_bir_lowering=False, num_devices=1)
    arrays, A = {}, {}
    for name, short in _INS.items():
        a = _np.ascontiguousarray(inputs[name])
        arrays[f"in_{short}"] = a
        A[short] = nc.dram_tensor(f"in_{short}", a.shape, mybir.dt.from_np(a.dtype), kind="ExternalInput").ap()
    out = nc.dram_tensor("out_0", inputs["x"].shape, F32, kind="ExternalOutput").ap()
    build(nc, A, out)
    r = _run(nc, [arrays], core_ids=[0])
    return r.results[0]["out_0"]
```
